# Optimizing a Trainium2 kernel written in Bass

```python
import numpy as np
import jax
import jax.numpy as jnp

def _softmax(x, axis=-1):
    return jax.nn.softmax(x, axis=axis)

def _gelu(x):
    return jax.nn.gelu(x, approximate=True)

def _silu(x):
    return jax.nn.silu(x)

def _sigmoid(x):
    return jax.nn.sigmoid(x)

def _layernorm(x, axis=-1, eps=1e-05):
    m = jnp.mean(x, axis=axis, keepdims=True)
    v = jnp.var(x, axis=axis, keepdims=True)
    return (x - m) / jnp.sqrt(v + eps)

def _scatter_add(tgt, idx, src, axis=0):
    return tgt.at[idx].add(src)

def _segment_sum(src, seg, n):
    return jax.ops.segment_sum(src, seg, n)
kernel_name = 'mk_seq_postln_d2_jaxref_r8_f533c4'

def setup_inputs(seed: int=0):
    np.random.seed(seed)
    _w = jnp.asarray

    def _L0_attn_setup():
        import jax, jax.numpy as jnp
        import numpy as np
        D_MODEL = 128
        D_STATE = 128
        D_CONV = 4
        EXPAND = 2
        HEADDIM = 64
        D_INNER = EXPAND * D_MODEL
        NHEADS = D_INNER // HEADDIM
        NGROUPS = 1
        CONV_DIM = D_INNER + 2 * NGROUPS * D_STATE
        D_IN_PROJ = 2 * D_INNER + 2 * NGROUPS * D_STATE + NHEADS
        CHUNK = 64
        BATCH, SEQLEN = (4, 256)
        EPS = 1e-05

        def _segsum_exp(x):
            T = x.shape[-1]
            cs = jnp.cumsum(x, axis=-1)
            seg = cs[..., :, None] - cs[..., None, :]
            mask = jnp.tril(jnp.ones((T, T), dtype=bool))
            return jnp.where(mask, jnp.exp(jnp.where(mask, seg, 0.0)), 0.0)

        def _causal_conv(x, w, b):
            xt = jnp.transpose(x, (0, 2, 1))
            out = jax.lax.conv_general_dilated(xt, w[:, None, :], (1,), [(w.shape[-1] - 1, 0)], dimension_numbers=('NCH', 'OIH', 'NCH'), feature_group_count=w.shape[0])
            return jnp.transpose(out, (0, 2, 1)) + b

        def _ssd(X, A, B, C):
            b, l, h, p = X.shape
            c, Q = (l // CHUNK, CHUNK)
            X = X.reshape(b, c, Q, h, p)
            A = jnp.transpose(A.reshape(b, c, Q, h), (0, 3, 1, 2))
            B = B.reshape(b, c, Q, -1)
            C = C.reshape(b, c, Q, -1)
            A_cum = jnp.cumsum(A, axis=-1)
            L = _segsum_exp(A)
            Y_diag = jnp.einsum('bcln,bcsn,bhcls,bcshp->bclhp', C, B, L, X)
            decay_states = jnp.exp(A_cum[..., -1:] - A_cum)
            states = jnp.einsum('bcln,bhcl,bclhp->bchpn', B, decay_states, X)
            A_sum = jnp.pad(A_cum[..., -1], ((0, 0), (0, 0), (1, 0)))
            decay_chunk = _segsum_exp(A_sum)
            states = jnp.concatenate([jnp.zeros_like(states[:, :1]), states], axis=1)
            prev = jnp.einsum('bhzc,bchpn->bzhpn', decay_chunk, states)[:, :-1]
            Y_off = jnp.einsum('bcln,bchpn,bhcl->bclhp', C, prev, jnp.exp(A_cum))
            return (Y_diag + Y_off).reshape(b, l, h, p)
        key = jax.random.key(seed)
        ks = jax.random.split(key, 8)
        return {'hidden_states': jax.random.normal(ks[0], (BATCH, SEQLEN, D_MODEL), jnp.float32), 'W_in': jax.random.normal(ks[1], (D_MODEL, D_IN_PROJ), jnp.float32) * D_MODEL ** (-0.5), 'conv_w': jax.random.normal(ks[2], (CONV_DIM, D_CONV), jnp.float32) * 0.2, 'conv_b': jnp.zeros((CONV_DIM,), jnp.float32), 'dt_bias': jax.random.normal(ks[3], (NHEADS,), jnp.float32) * 0.1, 'A_log': jnp.log(jnp.arange(1, NHEADS + 1, dtype=jnp.float32)), 'D': jnp.ones((NHEADS,), jnp.float32), 'rms_w': jnp.ones((D_INNER,), jnp.float32), 'W_out': jax.random.normal(ks[4], (D_INNER, D_MODEL), jnp.float32) * D_INNER ** (-0.5), 'ln_g': jnp.ones((D_MODEL,), jnp.float32), 'ln_b': jnp.zeros((D_MODEL,), jnp.float32)}
    _L0_attn_in = _L0_attn_setup()

    def _L0_ffn_setup():
        import jax, jax.numpy as jnp
        import numpy as np
        D_MODEL = 128
        N_HEADS = 16
        HEAD_DIM = D_MODEL // N_HEADS
        KV_LATENT = 64
        N_EXPERTS = 4
        D_HIDDEN = 4 * D_MODEL
        B, T = (2, 128)

        def rmsnorm(x, w, eps=1e-06):
            return w * (x * jax.lax.rsqrt(jnp.mean(x * x, axis=-1, keepdims=True) + eps))

        def layernorm(x, g, b, eps=1e-05):
            mu = jnp.mean(x, axis=-1, keepdims=True)
            var = jnp.mean((x - mu) ** 2, axis=-1, keepdims=True)
            return (x - mu) * jax.lax.rsqrt(var + eps) * g + b

        def apply_rope(x):
            t, d = (x.shape[2], x.shape[3])
            half = d // 2
            pos = jnp.arange(t, dtype=x.dtype)[:, None]
            inv_freq = 1.0 / 10000.0 ** (jnp.arange(half, dtype=x.dtype) / half)
            ang = pos * inv_freq[None, :]
            sin, cos = (jnp.sin(ang), jnp.cos(ang))
            x1, x2 = (x[..., :half], x[..., half:])
            return jnp.concatenate([x1 * cos - x2 * sin, x1 * sin + x2 * cos], axis=-1)

        def mla_attention(x, Wq, Wdkv, Wuk, Wuv, Wo, ln_g, ln_b):
            b, t, _ = x.shape
            q = (x @ Wq.T).reshape(b, t, N_HEADS, HEAD_DIM).transpose(0, 2, 1, 3)
            latent = layernorm(x @ Wdkv.T, ln_g, ln_b)
            k = (latent @ Wuk.T).reshape(b, t, N_HEADS, HEAD_DIM).transpose(0, 2, 1, 3)
            v = (latent @ Wuv.T).reshape(b, t, N_HEADS, HEAD_DIM).transpose(0, 2, 1, 3)
            q = apply_rope(q)
            k = apply_rope(k)
            scores = jnp.einsum('bhqd,bhkd->bhqk', q, k) / np.sqrt(HEAD_DIM)
            causal = jnp.tril(jnp.ones((t, t), dtype=bool))
            scores = jnp.where(causal, scores, -jnp.inf)
            attn = jax.nn.softmax(scores, axis=-1)
            out = jnp.einsum('bhqk,bhkd->bhqd', attn, v).transpose(0, 2, 1, 3).reshape(b, t, D_MODEL)
            return out @ Wo.T

        def moe(x, gate_w, gate_b, W1, b1, W2, b2):
            logits = x @ gate_w.T + gate_b
            top = jnp.argmax(logits, axis=-1)
            onehot = jax.nn.one_hot(top, N_EXPERTS, dtype=x.dtype)
            h = jax.nn.relu(jnp.einsum('btd,ehd->bteh', x, W1) + b1)
            y = jnp.einsum('bteh,edh->bted', h, W2) + b2
            return jnp.einsum('bted,bte->btd', y, onehot)
        key = jax.random.key(seed)
        ks = jax.random.split(key, 16)
        s = lambda fan_in: 1.0 / np.sqrt(fan_in)
        return {'x': jax.random.normal(ks[0], (B, T, D_MODEL), jnp.float32), 'norm1_w': jnp.ones((D_MODEL,), jnp.float32), 'norm2_w': jnp.ones((D_MODEL,), jnp.float32), 'Wq': jax.random.normal(ks[1], (D_MODEL, D_MODEL), jnp.float32) * s(D_MODEL), 'Wdkv': jax.random.normal(ks[2], (KV_LATENT, D_MODEL), jnp.float32) * s(D_MODEL), 'Wuk': jax.random.normal(ks[3], (D_MODEL, KV_LATENT), jnp.float32) * s(KV_LATENT), 'Wuv': jax.random.normal(ks[4], (D_MODEL, KV_LATENT), jnp.float32) * s(KV_LATENT), 'Wo': jax.random.normal(ks[5], (D_MODEL, D_MODEL), jnp.float32) * s(D_MODEL), 'ln_g': jnp.ones((KV_LATENT,), jnp.float32), 'ln_b': jnp.zeros((KV_LATENT,), jnp.float32), 'gate_w': jax.random.normal(ks[6], (N_EXPERTS, D_MODEL), jnp.float32) * s(D_MODEL), 'gate_b': jnp.zeros((N_EXPERTS,), jnp.float32), 'W1': jax.random.normal(ks[7], (N_EXPERTS, D_HIDDEN, D_MODEL), jnp.float32) * s(D_MODEL), 'b1': jnp.zeros((N_EXPERTS, D_HIDDEN), jnp.float32), 'W2': jax.random.normal(ks[8], (N_EXPERTS, D_MODEL, D_HIDDEN), jnp.float32) * s(D_HIDDEN), 'b2': jnp.zeros((N_EXPERTS, D_MODEL), jnp.float32)}
    _L0_ffn_in = _L0_ffn_setup()

    def _L1_attn_setup():
        import jax, jax.numpy as jnp
        import numpy as np
        B, L, D_MODEL, H = (4, 512, 128, 16)
        HD = D_MODEL // H
        EPS = 1e-06

        def _heads(y):
            b, l, _ = y.shape
            return jnp.transpose(y.reshape(b, l, H, HD), (0, 2, 1, 3))
        key = jax.random.key(seed)
        ks = jax.random.split(key, 5)
        s = 1.0 / np.sqrt(D_MODEL)
        return {'x': jax.random.normal(ks[0], (B, L, D_MODEL), dtype=jnp.float32), 'Wq': jax.random.normal(ks[1], (D_MODEL, D_MODEL), dtype=jnp.float32) * s, 'bq': jnp.zeros((D_MODEL,), jnp.float32), 'Wk': jax.random.normal(ks[2], (D_MODEL, D_MODEL), dtype=jnp.float32) * s, 'bk': jnp.zeros((D_MODEL,), jnp.float32), 'Wv': jax.random.normal(ks[3], (D_MODEL, D_MODEL), dtype=jnp.float32) * s, 'bv': jnp.zeros((D_MODEL,), jnp.float32), 'Wo': jax.random.normal(ks[4], (D_MODEL, D_MODEL), dtype=jnp.float32) * s, 'bo': jnp.zeros((D_MODEL,), jnp.float32)}
    _L1_attn_in = _L1_attn_setup()

    def _L1_ffn_setup():
        import jax, jax.numpy as jnp
        import numpy as np
        EPS = 1e-06
        LN_EPS = 1e-05

        def _absmean_core(W):
            gamma = jnp.mean(jnp.abs(W)) + EPS
            Ws = W / gamma
            Wq = jnp.sign(Ws) * jnp.minimum(jnp.round(jnp.abs(Ws)), 1.0)
            return (Wq, gamma)

        @jax.custom_vjp
        def absmean(W):
            return _absmean_core(W)[0]

        def _absmean_fwd(W):
            Wq, gamma = _absmean_core(W)
            return (Wq, gamma)

        def _absmean_bwd(gamma, g):
            return (g / gamma,)
        absmean.defvjp(_absmean_fwd, _absmean_bwd)

        def layernorm(x, w, b, eps=LN_EPS):
            mu = jnp.mean(x, axis=-1, keepdims=True)
            var = jnp.mean((x - mu) ** 2, axis=-1, keepdims=True)
            return (x - mu) * jax.lax.rsqrt(var + eps) * w + b
        key = jax.random.key(seed)
        k1, k2, k3 = jax.random.split(key, 3)
        d, h = (128, 512)
        B, T = (8, 256)
        return {'x': jax.random.normal(k1, (B, T, d), jnp.float32), 'W_fc': jax.random.normal(k2, (h, d), jnp.float32), 'ln_w': jnp.ones((h,), jnp.float32), 'ln_b': jnp.zeros((h,), jnp.float32), 'W_proj': jax.random.normal(k3, (d, h), jnp.float32)}
    _L1_ffn_in = _L1_ffn_setup()
    _d = {'L0_attn_hidden_states': _L0_attn_in['hidden_states'], 'L0_attn_W_in': _L0_attn_in['W_in'], 'L0_attn_conv_w': _L0_attn_in['conv_w'], 'L0_attn_conv_b': _L0_attn_in['conv_b'], 'L0_attn_dt_bias': _L0_attn_in['dt_bias'], 'L0_attn_A_log': _L0_attn_in['A_log'], 'L0_attn_D': _L0_attn_in['D'], 'L0_attn_rms_w': _L0_attn_in['rms_w'], 'L0_attn_W_out': _L0_attn_in['W_out'], 'L0_attn_ln_g': _L0_attn_in['ln_g'], 'L0_attn_ln_b': _L0_attn_in['ln_b'], 'L0_ffn_norm1_w': _L0_ffn_in['norm1_w'], 'L0_ffn_norm2_w': _L0_ffn_in['norm2_w'], 'L0_ffn_Wq': _L0_ffn_in['Wq'], 'L0_ffn_Wdkv': _L0_ffn_in['Wdkv'], 'L0_ffn_Wuk': _L0_ffn_in['Wuk'], 'L0_ffn_Wuv': _L0_ffn_in['Wuv'], 'L0_ffn_Wo': _L0_ffn_in['Wo'], 'L0_ffn_ln_g': _L0_ffn_in['ln_g'], 'L0_ffn_ln_b': _L0_ffn_in['ln_b'], 'L0_ffn_gate_w': _L0_ffn_in['gate_w'], 'L0_ffn_gate_b': _L0_ffn_in['gate_b'], 'L0_ffn_W1': _L0_ffn_in['W1'], 'L0_ffn_b1': _L0_ffn_in['b1'], 'L0_ffn_W2': _L0_ffn_in['W2'], 'L0_ffn_b2': _L0_ffn_in['b2'], 'L1_attn_Wq': _L1_attn_in['Wq'], 'L1_attn_bq': _L1_attn_in['bq'], 'L1_attn_Wk': _L1_attn_in['Wk'], 'L1_attn_bk': _L1_attn_in['bk'], 'L1_attn_Wv': _L1_attn_in['Wv'], 'L1_attn_bv': _L1_attn_in['bv'], 'L1_attn_Wo': _L1_attn_in['Wo'], 'L1_attn_bo': _L1_attn_in['bo'], 'L1_ffn_W_fc': _L1_ffn_in['W_fc'], 'L1_ffn_ln_w': _L1_ffn_in['ln_w'], 'L1_ffn_ln_b': _L1_ffn_in['ln_b'], 'L1_ffn_W_proj': _L1_ffn_in['W_proj']}
    _x0 = _d['L0_attn_hidden_states']
    _d['L0_attn_hidden_states'] = jax.random.normal(jax.random.fold_in(jax.random.key(seed), 1), (4, 1024, 128), dtype=_x0.dtype)
    del _x0
    return _d

def reference(L0_attn_hidden_states, L0_attn_W_in, L0_attn_conv_w, L0_attn_conv_b, L0_attn_dt_bias, L0_attn_A_log, L0_attn_D, L0_attn_rms_w, L0_attn_W_out, L0_attn_ln_g, L0_attn_ln_b, L0_ffn_norm1_w, L0_ffn_norm2_w, L0_ffn_Wq, L0_ffn_Wdkv, L0_ffn_Wuk, L0_ffn_Wuv, L0_ffn_Wo, L0_ffn_ln_g, L0_ffn_ln_b, L0_ffn_gate_w, L0_ffn_gate_b, L0_ffn_W1, L0_ffn_b1, L0_ffn_W2, L0_ffn_b2, L1_attn_Wq, L1_attn_bq, L1_attn_Wk, L1_attn_bk, L1_attn_Wv, L1_attn_bv, L1_attn_Wo, L1_attn_bo, L1_ffn_W_fc, L1_ffn_ln_w, L1_ffn_ln_b, L1_ffn_W_proj):

    def _L0_attn_ref(hidden_states, W_in, conv_w, conv_b, dt_bias, A_log, D, rms_w, W_out, ln_g, ln_b):
        import jax, jax.numpy as jnp
        import numpy as np
        D_MODEL = 128
        D_STATE = 128
        D_CONV = 4
        EXPAND = 2
        HEADDIM = 64
        D_INNER = EXPAND * D_MODEL
        NHEADS = D_INNER // HEADDIM
        NGROUPS = 1
        CONV_DIM = D_INNER + 2 * NGROUPS * D_STATE
        D_IN_PROJ = 2 * D_INNER + 2 * NGROUPS * D_STATE + NHEADS
        CHUNK = 64
        BATCH, SEQLEN = (4, 256)
        EPS = 1e-05

        def _segsum_exp(x):
            T = x.shape[-1]
            cs = jnp.cumsum(x, axis=-1)
            seg = cs[..., :, None] - cs[..., None, :]
            mask = jnp.tril(jnp.ones((T, T), dtype=bool))
            return jnp.where(mask, jnp.exp(jnp.where(mask, seg, 0.0)), 0.0)

        def _causal_conv(x, w, b):
            xt = jnp.transpose(x, (0, 2, 1))
            out = jax.lax.conv_general_dilated(xt, w[:, None, :], (1,), [(w.shape[-1] - 1, 0)], dimension_numbers=('NCH', 'OIH', 'NCH'), feature_group_count=w.shape[0])
            return jnp.transpose(out, (0, 2, 1)) + b

        def _ssd(X, A, B, C):
            b, l, h, p = X.shape
            c, Q = (l // CHUNK, CHUNK)
            X = X.reshape(b, c, Q, h, p)
            A = jnp.transpose(A.reshape(b, c, Q, h), (0, 3, 1, 2))
            B = B.reshape(b, c, Q, -1)
            C = C.reshape(b, c, Q, -1)
            A_cum = jnp.cumsum(A, axis=-1)
            L = _segsum_exp(A)
            Y_diag = jnp.einsum('bcln,bcsn,bhcls,bcshp->bclhp', C, B, L, X)
            decay_states = jnp.exp(A_cum[..., -1:] - A_cum)
            states = jnp.einsum('bcln,bhcl,bclhp->bchpn', B, decay_states, X)
            A_sum = jnp.pad(A_cum[..., -1], ((0, 0), (0, 0), (1, 0)))
            decay_chunk = _segsum_exp(A_sum)
            states = jnp.concatenate([jnp.zeros_like(states[:, :1]), states], axis=1)
            prev = jnp.einsum('bhzc,bchpn->bzhpn', decay_chunk, states)[:, :-1]
            Y_off = jnp.einsum('bcln,bchpn,bhcl->bclhp', C, prev, jnp.exp(A_cum))
            return (Y_diag + Y_off).reshape(b, l, h, p)
        residual = hidden_states
        zxbcdt = hidden_states @ W_in
        z, xBC, dt = jnp.split(zxbcdt, [D_INNER, D_INNER + CONV_DIM], axis=-1)
        dt = jax.nn.softplus(dt + dt_bias)
        xBC = jax.nn.silu(_causal_conv(xBC, conv_w, conv_b))
        x, B, C = jnp.split(xBC, [D_INNER, D_INNER + NGROUPS * D_STATE], axis=-1)
        b, l, _ = x.shape
        x = x.reshape(b, l, NHEADS, HEADDIM)
        a = -jnp.exp(A_log)
        y = _ssd(x * dt[..., None], dt * a, B, C)
        y = y + x * D[None, None, :, None]
        y = y.reshape(b, l, D_INNER)
        y = y * jax.nn.silu(z)
        y = y * jax.lax.rsqrt(jnp.mean(y * y, axis=-1, keepdims=True) + EPS) * rms_w
        out = y @ W_out
        h = residual + out
        mu = jnp.mean(h, axis=-1, keepdims=True)
        var = jnp.mean((h - mu) ** 2, axis=-1, keepdims=True)
        return (h - mu) * jax.lax.rsqrt(var + EPS) * ln_g + ln_b

    def _L0_ffn_ref(x, norm1_w, norm2_w, Wq, Wdkv, Wuk, Wuv, Wo, ln_g, ln_b, gate_w, gate_b, W1, b1, W2, b2):
        import jax, jax.numpy as jnp
        import numpy as np
        D_MODEL = 128
        N_HEADS = 16
        HEAD_DIM = D_MODEL // N_HEADS
        KV_LATENT = 64
        N_EXPERTS = 4
        D_HIDDEN = 4 * D_MODEL
        B, T = (2, 128)

        def rmsnorm(x, w, eps=1e-06):
            return w * (x * jax.lax.rsqrt(jnp.mean(x * x, axis=-1, keepdims=True) + eps))

        def layernorm(x, g, b, eps=1e-05):
            mu = jnp.mean(x, axis=-1, keepdims=True)
            var = jnp.mean((x - mu) ** 2, axis=-1, keepdims=True)
            return (x - mu) * jax.lax.rsqrt(var + eps) * g + b

        def apply_rope(x):
            t, d = (x.shape[2], x.shape[3])
            half = d // 2
            pos = jnp.arange(t, dtype=x.dtype)[:, None]
            inv_freq = 1.0 / 10000.0 ** (jnp.arange(half, dtype=x.dtype) / half)
            ang = pos * inv_freq[None, :]
            sin, cos = (jnp.sin(ang), jnp.cos(ang))
            x1, x2 = (x[..., :half], x[..., half:])
            return jnp.concatenate([x1 * cos - x2 * sin, x1 * sin + x2 * cos], axis=-1)

        def mla_attention(x, Wq, Wdkv, Wuk, Wuv, Wo, ln_g, ln_b):
            b, t, _ = x.shape
            q = (x @ Wq.T).reshape(b, t, N_HEADS, HEAD_DIM).transpose(0, 2, 1, 3)
            latent = layernorm(x @ Wdkv.T, ln_g, ln_b)
            k = (latent @ Wuk.T).reshape(b, t, N_HEADS, HEAD_DIM).transpose(0, 2, 1, 3)
            v = (latent @ Wuv.T).reshape(b, t, N_HEADS, HEAD_DIM).transpose(0, 2, 1, 3)
            q = apply_rope(q)
            k = apply_rope(k)
            scores = jnp.einsum('bhqd,bhkd->bhqk', q, k) / np.sqrt(HEAD_DIM)
            causal = jnp.tril(jnp.ones((t, t), dtype=bool))
            scores = jnp.where(causal, scores, -jnp.inf)
            attn = jax.nn.softmax(scores, axis=-1)
            out = jnp.einsum('bhqk,bhkd->bhqd', attn, v).transpose(0, 2, 1, 3).reshape(b, t, D_MODEL)
            return out @ Wo.T

        def moe(x, gate_w, gate_b, W1, b1, W2, b2):
            logits = x @ gate_w.T + gate_b
            top = jnp.argmax(logits, axis=-1)
            onehot = jax.nn.one_hot(top, N_EXPERTS, dtype=x.dtype)
            h = jax.nn.relu(jnp.einsum('btd,ehd->bteh', x, W1) + b1)
            y = jnp.einsum('bteh,edh->bted', h, W2) + b2
            return jnp.einsum('bted,bte->btd', y, onehot)
        x = x + mla_attention(rmsnorm(x, norm1_w), Wq, Wdkv, Wuk, Wuv, Wo, ln_g, ln_b)
        x = x + moe(rmsnorm(x, norm2_w), gate_w, gate_b, W1, b1, W2, b2)
        return x

    def _L1_attn_ref(x, Wq, bq, Wk, bk, Wv, bv, Wo, bo):
        import jax, jax.numpy as jnp
        import numpy as np
        B, L, D_MODEL, H = (4, 512, 128, 16)
        HD = D_MODEL // H
        EPS = 1e-06

        def _heads(y):
            b, l, _ = y.shape
            return jnp.transpose(y.reshape(b, l, H, HD), (0, 2, 1, 3))
        b, l, _ = x.shape
        q = jax.nn.sigmoid(_heads(x @ Wq + bq))
        k = jax.nn.sigmoid(_heads(x @ Wk + bk))
        v = _heads(x @ Wv + bv)
        sink_incoming = 1.0 / jnp.einsum('bhld,bhd->bhl', q + EPS, k.sum(axis=2) + EPS)
        source_outgoing = 1.0 / jnp.einsum('bhld,bhd->bhl', k + EPS, q.sum(axis=2) + EPS)
        conserved_sink = jnp.einsum('bhld,bhd->bhl', q + EPS, (k * source_outgoing[..., None]).sum(axis=2) + EPS)
        conserved_source = jnp.einsum('bhld,bhd->bhl', k + EPS, (q * sink_incoming[..., None]).sum(axis=2) + EPS)
        conserved_source = jnp.clip(conserved_source, -1.0, 1.0)
        sink_allocation = jax.nn.sigmoid(conserved_sink * (float(l) / float(l)))
        source_competition = jax.nn.softmax(conserved_source, axis=-1) * float(l)
        kv = jnp.einsum('bhld,bhlm->bhdm', k, v * source_competition[..., None])
        out = jnp.einsum('bhld,bhdm->bhlm', q * sink_incoming[..., None], kv)
        out = out * sink_allocation[..., None]
        out = jnp.transpose(out, (0, 2, 1, 3)).reshape(b, l, D_MODEL)
        return out @ Wo + bo

    def _L1_ffn_ref(x, W_fc, ln_w, ln_b, W_proj):
        import jax, jax.numpy as jnp
        import numpy as np
        EPS = 1e-06
        LN_EPS = 1e-05

        def _absmean_core(W):
            gamma = jnp.mean(jnp.abs(W)) + EPS
            Ws = W / gamma
            Wq = jnp.sign(Ws) * jnp.minimum(jnp.round(jnp.abs(Ws)), 1.0)
            return (Wq, gamma)

        @jax.custom_vjp
        def absmean(W):
            return _absmean_core(W)[0]

        def _absmean_fwd(W):
            Wq, gamma = _absmean_core(W)
            return (Wq, gamma)

        def _absmean_bwd(gamma, g):
            return (g / gamma,)
        absmean.defvjp(_absmean_fwd, _absmean_bwd)

        def layernorm(x, w, b, eps=LN_EPS):
            mu = jnp.mean(x, axis=-1, keepdims=True)
            var = jnp.mean((x - mu) ** 2, axis=-1, keepdims=True)
            return (x - mu) * jax.lax.rsqrt(var + eps) * w + b
        h = jnp.einsum('btd,hd->bth', x, absmean(W_fc))
        h = jax.nn.gelu(h, approximate=False)
        h = layernorm(h, ln_w, ln_b)
        return jnp.einsum('bth,dh->btd', h, absmean(W_proj))
    x = L0_attn_hidden_states
    x = _layernorm(x + _L0_attn_ref(x, L0_attn_W_in, L0_attn_conv_w, L0_attn_conv_b, L0_attn_dt_bias, L0_attn_A_log, L0_attn_D, L0_attn_rms_w, L0_attn_W_out, L0_attn_ln_g, L0_attn_ln_b), axis=-1)
    x = _layernorm(x + _L0_ffn_ref(x, L0_ffn_norm1_w, L0_ffn_norm2_w, L0_ffn_Wq, L0_ffn_Wdkv, L0_ffn_Wuk, L0_ffn_Wuv, L0_ffn_Wo, L0_ffn_ln_g, L0_ffn_ln_b, L0_ffn_gate_w, L0_ffn_gate_b, L0_ffn_W1, L0_ffn_b1, L0_ffn_W2, L0_ffn_b2), axis=-1)
    x = _layernorm(x + _L1_attn_ref(x, L1_attn_Wq, L1_attn_bq, L1_attn_Wk, L1_attn_bk, L1_attn_Wv, L1_attn_bv, L1_attn_Wo, L1_attn_bo), axis=-1)
    x = _layernorm(x + _L1_ffn_ref(x, L1_ffn_W_fc, L1_ffn_ln_w, L1_ffn_ln_b, L1_ffn_W_proj), axis=-1)
    return x

_drawn_inputs = setup_inputs


def setup_inputs(seed=0):
    import zlib

    import numpy as np

    out = dict(_drawn_inputs(seed))
    spreads = {'L0_attn_conv_b': (0.0, 0.1),
     'L0_attn_D': (1.0, 0.2),
     'L0_attn_rms_w': (1.0, 0.2),
     'L0_attn_ln_g': (1.0, 0.2),
     'L0_attn_ln_b': (0.0, 0.1),
     'L0_ffn_norm1_w': (1.0, 0.2),
     'L0_ffn_norm2_w': (1.0, 0.2),
     'L0_ffn_ln_g': (1.0, 0.2),
     'L0_ffn_ln_b': (0.0, 0.1),
     'L0_ffn_gate_b': (0.0, 0.1),
     'L0_ffn_b1': (0.0, 0.1),
     'L0_ffn_b2': (0.0, 0.1),
     'L1_attn_bq': (0.0, 0.8),
     'L1_attn_bk': (0.0, 0.8),
     'L1_attn_bv': (0.0, 0.1),
     'L1_attn_bo': (0.0, 0.1),
     'L1_ffn_ln_w': (1.0, 0.2),
     'L1_ffn_ln_b': (0.0, 0.1)}
    factors = {'L1_attn_Wq': 7.426, 'L1_attn_Wk': 2.98}
    for name, (base, spread) in spreads.items():
        noise = np.random.default_rng([zlib.crc32(name.encode()), seed]).standard_normal(out[name].shape)
        drawn = base * np.exp(spread * noise) if base else spread * noise
        out[name] = jnp.asarray(drawn.astype(out[name].dtype))
    for name, factor in factors.items():
        out[name] = (out[name] * factor).astype(out[name].dtype)
    return out
```

```python
from contextlib import ExitStack

import numpy as np
import concourse.bass as bass
from concourse import mybir

F32 = mybir.dt.float32
BF16 = mybir.dt.bfloat16
I32 = mybir.dt.int32
ACT = mybir.ActivationFunctionType
ALU = mybir.AluOpType
AX = mybir.AxisListType

P = 128
BATCH, SEQ, DM = 4, 1024, 128
TOK = BATCH * SEQ
TILES = TOK // P
TPB = SEQ // P
G = 4
W = G * P

DIN, NST, NH, HD, TAPS = 256, 128, 4, 64, 4
NBLK = (DIN + 2 * NST) // P
ZB = DIN // P
EPS_RMS, EPS_LN = 1e-5, 1e-5

AH, AD, LAT, NE, HID = 16, 8, 64, 4, 512
EPS_RMS2 = 1e-6
SPLITS = 3
SROWS = SPLITS * SPLITS * AD
SHIFT_ROW = 96
MASKED = -1e30

FLOW_EPS = 1e-6
FH = 512
GAMMA_EPS = 1e-6

MAGIC = 1597463007.0


class Chain:

    def __init__(self, eng, sem, start=0, step=0, per=0):
        self.eng, self.sem, self.start, self.before, self.per = eng, sem, start, start + step * per, per
        self.count = 0

    def __call__(self, instruction):
        self.count += 1
        instruction.then_inc(self.sem, 1)
        self.eng.wait_ge(self.sem, self.before + self.count)

    def end(self):
        assert self.count == self.per, (self.count, self.per)


class Signals:

    def __init__(self, nc, ctx):
        self.nc, self.ctx = nc, ctx
        self.loaded, self.chain = self.new("loaded"), self.new("chain")
        self.loads = self.links = 0
        self.set_up = self.new("set_up")

    def new(self, name):
        return self.ctx.enter_context(self.nc.semaphore(name))


def inverse_root(eng, link, v, y, t, h):
    eng.tensor_scalar(h, v, -0.5, None, ALU.mult)
    link(eng.tensor_scalar(y.bitcast(I32), v.bitcast(I32), -0.5, MAGIC, ALU.mult, ALU.add))
    for _ in range(3):
        link(eng.tensor_tensor(t, y, y, ALU.mult))
        link(eng.tensor_tensor(t, t, h, ALU.mult))
        link(eng.scalar_tensor_tensor(out=y, in0=t, scalar=1.5, in1=y, op0=ALU.add, op1=ALU.mult))


ROOT_LINKS = 10


class NormScratch:

    def __init__(self, sb, name, n=G):
        self.st = sb(name + "_stats", [P, n, 6], F32)
        self.sum = sb(name + "_sum", [P, n], F32)
        self.dif = sb(name + "_dif", [P, n], F32)
        self.m2 = sb(name + "_m2", [P, n], F32)
        self.v = sb(name + "_var", [P, n], F32)
        self.y = sb(name + "_rstd", [P, n], F32)
        self.t = sb(name + "_t", [P, n], F32)
        self.h = sb(name + "_h", [P, n], F32)
        self.b = sb(name + "_shift", [P, n], F32)


NORM_LINKS = 4 + ROOT_LINKS + 2


def layer_norm(eng, link, s, src, dst, eps, width, n=G, done=None):
    for k in range(n):
        last = eng.bn_stats(s.st[:, k, :], src(k))
    link(last)
    eng.tensor_tensor(s.sum[:, :], s.st[:, :, 1], s.st[:, :, 4], ALU.add)
    eng.tensor_tensor(s.dif[:, :], s.st[:, :, 1], s.st[:, :, 4], ALU.subtract)
    link(eng.scalar_tensor_tensor(out=s.m2[:, :], in0=s.st[:, :, 2], scalar=eps * width, in1=s.st[:, :, 5],
                                  op0=ALU.add, op1=ALU.add))
    link(eng.scalar_tensor_tensor(out=s.dif[:, :], in0=s.dif[:, :], scalar=0.25, in1=s.dif[:, :],
                                  op0=ALU.mult, op1=ALU.mult))
    link(eng.scalar_tensor_tensor(out=s.v[:, :], in0=s.m2[:, :], scalar=1.0 / width, in1=s.dif[:, :],
                                  op0=ALU.mult, op1=ALU.add))
    inverse_root(eng, link, s.v[:, :], s.y[:, :], s.t[:, :], s.h[:, :])
    link(eng.scalar_tensor_tensor(out=s.b[:, :], in0=s.sum[:, :], scalar=-0.5, in1=s.y[:, :],
                                  op0=ALU.mult, op1=ALU.mult))
    for k in range(n):
        last = eng.tensor_scalar(dst(k), src(k), s.y[:, k:k + 1], s.b[:, k:k + 1], ALU.mult, ALU.add)
    if done is None:
        link(last)
    else:
        last.then_inc(done, 1)


def mamba(nc, signals, x_all, tri, past, ones, ident, d):
    with ExitStack() as ctx:
        def sb(name, shape, dt=F32):
            return ctx.enter_context(nc.sbuf_tensor(name, shape, dt))

        def sem(name):
            return signals.new(name)

        ps = ctx.enter_context(nc.psum_tensor("mamba_psum", [P, 8, 512], F32))
        proj = [ps[:, 0, :], ps[:, 1, :]]
        outp = ps[:, 0, :].rearrange("p (b n) -> p b n", b=G)
        ssp = ps[:, 1, 0:G]
        decp = ps[:, 2:4, :]
        xtokp = ps[:, 4:6, :].rearrange("p k (b n) -> p (k b) n", n=DIN)
        yp = ps[:, 4:6, :].rearrange("p k (b l) -> p k b l", b=G)
        btokp = ps[:, 6, :]
        scorep = ps[:, 7, :]
        newp = ps[:, 6:8, :].rearrange("p k (b n) -> p (k b) n", n=DIN)

        xT = sb("xT", [P, TOK])
        xTb = xT[:, :].rearrange("p (b l) -> p b l", b=BATCH)
        w_in = sb("w_in", [P, 2 * DIN + 2 * NST + NH])
        conv_w = sb("conv_w", [P, NBLK, TAPS])
        conv_b = sb("conv_b", [P, NBLK])
        dcol = sb("dcol", [P, ZB])
        rms_w = sb("rms_w", [P, ZB])
        w_out = sb("w_out", [P, ZB, DM])
        dt_bias = sb("dt_bias", [P, NH])
        a_log = sb("a_log", [P, NH])
        ln_g = sb("ln_g", [P, DM])
        ln_b = sb("ln_b", [P, DM])

        u = sb("u", [P, TILES, NH])
        au = sb("au", [P, TILES, NH])
        dt = sb("dt", [P, TILES, NH])
        ada = sb("ada", [P, TILES, NH])
        carry = sb("carry", [P, 2, TILES, NH])

        pre = sb("pre", [P, NBLK, BATCH, TAPS - 1 + P])
        cv = sb("cv", [P, NBLK, W])
        xbc = sb("xbc", [P, NBLK, W])
        zs = sb("zs", [P, ZB, W])
        ta = sb("ta", [P, 2, NH, P])
        le = sb("le", [P, 2, 2, NH, P])
        mm = sb("mm", [P, 2, NH, P])
        ce = sb("ce", [P, 2, NH, P])
        xdt = sb("xdt", [P, BATCH, DIN])
        xdd = sb("xdd", [P, BATCH, DIN])
        btok = sb("btok", [P, BATCH, NST])
        sm = sb("sm", [P, BATCH, P])
        state = sb("state", [P, BATCH, DIN])
        yg = sb("yg", [P, ZB, W])
        sq = sb("sq", [P, ZB, W])
        h = sb("h", [P, G, DM])
        r = sb("r", [P, G])
        rv = sb("rv", [P, G])
        rt = sb("rt", [P, G])
        rh = sb("rh", [P, G])
        ns = NormScratch(sb, "mnorm")

        loaded, chain = signals.loaded, signals.chain
        dt_raw = sem("dt_raw")
        e_abs = sem("e_abs")
        dt_act = sem("dt_act")
        dt_ready = sem("dt_ready")
        carry_sum = sem("carry_sum")
        carry_ready = sem("carry_ready")
        proj_done = sem("proj_done")
        proj_read = sem("proj_read")
        tail_kept = sem("tail_kept")
        conv_done = sem("conv_done")
        xbc_ready = sem("xbc_ready")
        z_ready = sem("z_ready")
        ta_ready = sem("ta_ready")
        dec_done = sem("dec_done")
        dec_exp = sem("dec_exp")
        mix_ready = sem("mix_ready")
        xtok_done = sem("xtok_done")
        btok_done = sem("btok_done")
        score_done = sem("score_done")
        xdt_ready = sem("xdt_ready")
        xdd_ready = sem("xdd_ready")
        btok_ready = sem("btok_ready")
        sm_ready = sem("sm_ready")
        y_done = sem("y_done")
        new_done = sem("new_done")
        state_ready = sem("state_ready")
        yg_ready = sem("yg_ready")
        sq_ready = sem("sq_ready")
        ss_done = sem("ss_done")
        out_done = sem("out_done")
        out_read = sem("out_read")
        act_chain = sem("mamba_act_chain")


        with nc.Block() as block:
            @block.sync
            def _(sp):
                for dst, src in ((xT[:, :], d["xT"]), (w_in[:, :], d["w_in"]), (x_all[:, :, :], d["x"]),
                                 (tri[:, :], d["tri"]), (past[:, :], d["past"]), (ident[:, :], d["ident"]),
                                 (conv_w[:, :, :], d["conv_w"]), (conv_b[:, :], d["conv_b"]),
                                 (dcol[:, :], d["dcol"]), (rms_w[:, :], d["rms_w"]),
                                 (w_out[:, :, :], d["w_out"])):
                    sp.dma_start(dst, src).then_inc(loaded, 16)
                for dst, src in ((dt_bias, d["dt_bias"]), (a_log, d["a_log"]), (ln_g, d["m_ln_g"]),
                                 (ln_b, d["m_ln_b"])):
                    sp.dma_start(dst[:, :], src.partition_broadcast(P)).then_inc(loaded, 16)

            ALL = signals.loads = 16 * 15

            @block.tensor
            def _(pe):
                pe.wait_ge(loaded, ALL)
                for t in range(TILES):
                    last = nc.tensor.matmul(ps[:, 4, NH * t:NH * t + NH], xT[:, t * P:(t + 1) * P],
                                            w_in[:, 2 * DIN + 2 * NST:], start=True, stop=True)
                last.then_inc(dt_raw, 1)
                pe.wait_ge(dt_ready, 1)
                flat = ada[:, :, :].rearrange("p t h -> p (t h)")
                nc.tensor.matmul(ps[:, 5, 0:P], past[:, :], flat, start=True, stop=True)
                nc.tensor.matmul(ps[:, 5, P:2 * P], ones[:, :], flat, start=True, stop=True).then_inc(carry_sum, 1)

                def project(i, n, col):
                    if n < 2:
                        pe.wait_ge(out_read, i)
                    else:
                        pe.wait_ge(proj_read, 6 * i + n - 1)
                    nc.tensor.matmul(proj[n % 2], w_in[:, col:col + P], xTb[:, :, bass.ds(i * P, P)],
                                     start=True, stop=True).then_inc(proj_done, 1)

                def decays(i, b):
                    pe.wait_ge(ta_ready, 4 * i + b + 1)
                    pe.wait_ge(dec_exp, 4 * i + b)
                    rhs = ta[:, b % 2, :, :]
                    nc.tensor.matmul(decp[:, 0, :], past[:, :], rhs, start=True, stop=True)
                    nc.tensor.matmul(decp[:, 1, :], ones[:, :], rhs, start=True, stop=True).then_inc(dec_done, 1)

                with pe.Fori(0, TPB) as i:
                    for n in range(NBLK):
                        project(i, n, DIN + n * P)
                    decays(i, 0)
                    for n in range(ZB):
                        project(i, NBLK + n, n * P)
                    pe.wait_ge(yg_ready, i)
                    for k in range(ZB):
                        pe.wait_ge(xbc_ready, 4 * i + k + 1)
                        for b in range(BATCH):
                            last = nc.tensor.transpose(xtokp[:, b, k * P:(k + 1) * P], xbc[:, k, b * P:(b + 1) * P],
                                                       ident[:, :])
                    last.then_inc(xtok_done, 1)
                    pe.wait_ge(state_ready, i + 1)
                    pe.wait_ge(xbc_ready, 4 * i + 3)
                    for b in range(BATCH):
                        last = nc.tensor.transpose(btokp[:, b * P:(b + 1) * P], xbc[:, 2, b * P:(b + 1) * P], ident[:, :])
                    last.then_inc(btok_done, 1)
                    pe.wait_ge(xbc_ready, 4 * i + 4)
                    for b in range(BATCH):
                        last = nc.tensor.matmul(scorep[:, b * P:(b + 1) * P], xbc[:, 2, b * P:(b + 1) * P],
                                                xbc[:, 3, b * P:(b + 1) * P], start=True, stop=True)
                    last.then_inc(score_done, 1)
                    pe.wait_ge(xdt_ready, i + 1)
                    for b in range(BATCH):
                        if b + 1 < BATCH:
                            decays(i, b + 1)
                        pe.wait_ge(mix_ready, 4 * i + b + 1)
                        for hh in range(NH):
                            out = yp[HD * (hh % 2):HD * (hh % 2) + HD, hh // 2, b, :]
                            nc.tensor.matmul(out, xdt[:, b, hh * HD:(hh + 1) * HD], mm[:, b % 2, hh, :],
                                             start=True, stop=False)
                            last = nc.tensor.matmul(out, state[:, b, hh * HD:(hh + 1) * HD], ce[:, b % 2, hh, :],
                                                    start=False, stop=True)
                        last.then_inc(y_done, 1)
                    pe.wait_ge(btok_ready, i + 1)
                    pe.wait_ge(sm_ready, i + 1)
                    pe.wait_ge(xdd_ready, i + 1)
                    for b in range(BATCH):
                        last = nc.tensor.matmul(newp[:, b, :], btok[:, b, :], xdd[:, b, :], start=True, stop=True)
                    last.then_inc(new_done, 1)
                    pe.wait_ge(sq_ready, 2 * i + 2)
                    pe.wait_ge(proj_read, 6 * i + 6)
                    for b in range(BATCH):
                        for k in range(ZB):
                            last = nc.tensor.matmul(ssp[:, b:b + 1], sq[:, k, b * P:(b + 1) * P], ones[:, 0:1],
                                                    start=(k == 0), stop=(k == ZB - 1))
                    last.then_inc(ss_done, 1)
                    for b in range(BATCH):
                        for k in range(ZB):
                            last = nc.tensor.matmul(outp[:, b, :], yg[:, k, b * P:(b + 1) * P], w_out[:, k, :],
                                                    start=(k == 0), stop=(k == ZB - 1))
                    last.then_inc(out_done, 1)

            @block.scalar
            def _(act):
                act.wait_ge(loaded, ALL)
                nc.scalar.activation(a_log[:, :], a_log[:, :], ACT.Exp).then_inc(dt_act, 1)
                act.wait_ge(e_abs, 1)
                nc.scalar.activation(au[:, :, :], au[:, :, :], ACT.Exp, scale=-1.0).then_inc(act_chain, 1)
                act.wait_ge(act_chain, 1)
                nc.scalar.activation(au[:, :, :], au[:, :, :], ACT.Ln, bias=ones[:, 0:1]).then_inc(dt_act, 1)
                act.wait_ge(carry_sum, 1)
                nc.scalar.activation(carry[:, :, :, :].rearrange("p a t h -> p (a t h)"), ps[:, 5, 0:2 * P],
                                     ACT.Exp).then_inc(carry_ready, 1)
                with act.Fori(0, TPB) as i:
                    act.wait_ge(tail_kept, i + 1)
                    for n in range(NBLK):
                        act.wait_ge(proj_done, 6 * i + n + 1)
                        nc.scalar.copy(pre[:, n, :, TAPS - 1:], proj[n % 2].rearrange("p (b l) -> p b l", b=BATCH))\
                            .then_inc(proj_read, 1)
                    act.wait_ge(yg_ready, i)
                    for n in range(ZB):
                        act.wait_ge(proj_done, 6 * i + NBLK + n + 1)
                        last = nc.scalar.activation(zs[:, n, :], proj[(NBLK + n) % 2], ACT.Silu)
                        last.then_inc(proj_read, 1)
                    for n in range(NBLK):
                        act.wait_ge(conv_done, 4 * i + n + 1)
                        nc.scalar.activation(xbc[:, n, :], cv[:, n, :], ACT.Silu, bias=conv_b[:, n:n + 1])\
                            .then_inc(xbc_ready, 1)
                    nc.scalar.copy(pre[:, :, :, 0:TAPS - 1], pre[:, :, :, P:P + TAPS - 1]).then_inc(tail_kept, 1)
                    for b in range(BATCH):
                        act.wait_ge(dec_done, 4 * i + b + 1)
                        if b < 2:
                            act.wait_ge(mix_ready, 4 * i)
                        else:
                            act.wait_ge(mix_ready, 4 * i + b - 1)
                        nc.scalar.activation(le[:, b % 2, :, :, :].rearrange("p k h l -> p k (h l)"), decp, ACT.Exp)\
                            .then_inc(dec_exp, 1)
                        if b == 0:
                            act.wait_ge(btok_done, i + 1)
                            act.wait_ge(new_done, i)
                            nc.scalar.copy(btok[:, :, :].rearrange("p b n -> p (b n)"), btokp).then_inc(btok_ready, 1)
                    act.wait_ge(yg_ready, i + 1)
                    act.wait_ge(ss_done, i)
                    for k in range(ZB):
                        nc.scalar.activation(sq[:, k, :], yg[:, k, :], ACT.Square).then_inc(sq_ready, 1)

            @block.gpsimd
            def _(pool):
                nc.gpsimd.memset(pre[:, :, :, 0:TAPS - 1], 0.0).then_inc(tail_kept, 1)
                pool.wait_ge(loaded, ALL)
                pool.wait_ge(dt_ready, 1)
                pool.wait_ge(carry_ready, 1)
                with pool.Fori(0, TPB) as i:
                    def spread(b):
                        pool.wait_ge(dec_done, 4 * i + b - 1 if b >= 2 else 4 * i)
                        nc.gpsimd.tensor_tensor(
                            ta[:, b % 2, :, :], tri[:, :].unsqueeze(1).to_broadcast([P, NH, P]),
                            ada[:, bass.ds(i + b * TPB, 1), :].rearrange("p t h -> p (t h)").unsqueeze(2)
                            .to_broadcast([P, NH, P]), ALU.mult).then_inc(ta_ready, 1)

                    spread(0)
                    spread(1)
                    pool.wait_ge(xdt_ready, i + 1)
                    pool.wait_ge(new_done, i)
                    for b in range(BATCH):
                        last = nc.gpsimd.tensor_tensor(
                            xdd[:, b, :].rearrange("p (h n) -> p h n", h=NH), xdt[:, b, :].rearrange("p (h n) -> p h n", h=NH),
                            carry[:, 0, bass.ds(i + b * TPB, 1), :].rearrange("p t h -> p (t h)").unsqueeze(2)
                            .to_broadcast([P, NH, HD]), ALU.mult)
                    last.then_inc(xdd_ready, 1)
                    spread(2)
                    spread(3)

            @block.vector
            def _(dve):
                dve.wait_ge(loaded, ALL)
                nc.vector.memset(state[:, :, :], 0.0).then_inc(state_ready, 1)
                link = Chain(dve, chain)
                dve.wait_ge(dt_raw, 1)
                link(nc.vector.tensor_tensor(u[:, :, :], ps[:, 4, 0:TILES * NH].rearrange("p (t h) -> p t h", h=NH),
                                             dt_bias[:, :].unsqueeze(1).to_broadcast([P, TILES, NH]), ALU.add))
                nc.vector.scalar_tensor_tensor(out=au[:, :, :], in0=u[:, :, :], scalar=-1.0, in1=u[:, :, :],
                                               op0=ALU.mult, op1=ALU.max).then_inc(e_abs, 1)
                link(nc.vector.tensor_tensor(w_out[:, :, :], w_out[:, :, :],
                                             rms_w[:, :].unsqueeze(2).to_broadcast([P, ZB, DM]), ALU.mult))
                dve.wait_ge(dt_act, 2)
                link(nc.vector.scalar_tensor_tensor(out=dt[:, :, :], in0=u[:, :, :], scalar=0.0, in1=au[:, :, :],
                                                    op0=ALU.max, op1=ALU.add))
                nc.vector.scalar_tensor_tensor(out=ada[:, :, :], in0=dt[:, :, :], scalar=-1.0,
                                               in1=a_log[:, :].unsqueeze(1).to_broadcast([P, TILES, NH]),
                                               op0=ALU.mult, op1=ALU.mult).then_inc(dt_ready, 1)
                dve.wait_ge(carry_ready, 1)
                with dve.Fori(0, TPB) as i:
                    step = Chain(dve, chain, link.count, i, MAMBA_LINKS)
                    dve.wait_ge(tail_kept, i + 1)
                    dve.wait_ge(xbc_ready, 4 * i)
                    for pair in (0, 2):
                        for tap in range(TAPS):
                            for n in (pair, pair + 1):
                                o = cv[:, n, :].rearrange("p (b l) -> p b l", b=BATCH)
                                src = pre[:, n, :, tap:tap + P]
                                w = conv_w[:, n, tap:tap + 1]
                                if tap == 0:
                                    dve.wait_ge(proj_read, 6 * i + n + 1)
                                    op = nc.vector.tensor_scalar(o, src, w, None, ALU.mult)
                                else:
                                    op = nc.vector.scalar_tensor_tensor(out=o, in0=src, scalar=w, in1=o,
                                                                        op0=ALU.mult, op1=ALU.add)
                                if tap == TAPS - 1:
                                    op.then_inc(conv_done, 1)
                                elif n == pair + 1:
                                    step(op)
                    dve.wait_ge(xtok_done, i + 1)
                    dve.wait_ge(y_done, 4 * i)
                    dve.wait_ge(xdd_ready, i)
                    for b in range(BATCH):
                        last = nc.vector.tensor_tensor(
                            xdt[:, b, :].rearrange("p (h n) -> p h n", h=NH), xtokp[:, b, :].rearrange("p (h n) -> p h n", h=NH),
                            dt[:, bass.ds(i + b * TPB, 1), :].rearrange("p t h -> p (t h)").unsqueeze(2)
                            .to_broadcast([P, NH, HD]), ALU.mult)
                    last.then_inc(xdt_ready, 1)
                    dve.wait_ge(score_done, i + 1)
                    nc.vector.tensor_tensor(sm[:, :, :], scorep.rearrange("p (b l) -> p b l", b=BATCH),
                                            tri[:, :].unsqueeze(1).to_broadcast([P, BATCH, P]), ALU.mult)\
                        .then_inc(sm_ready, 1)
                    dve.wait_ge(sm_ready, i + 1)
                    for b in range(BATCH):
                        dve.wait_ge(dec_exp, 4 * i + b + 1)
                        dve.wait_ge(y_done, 4 * i + b - 1 if b >= 2 else 4 * i)
                        nc.vector.tensor_tensor(mm[:, b % 2, :, :], le[:, b % 2, 0, :, :],
                                                sm[:, b, :].unsqueeze(1).to_broadcast([P, NH, P]), ALU.mult)
                        nc.vector.tensor_tensor(ce[:, b % 2, :, :], le[:, b % 2, 1, :, :],
                                                xbc[:, 3, b * P:(b + 1) * P].unsqueeze(1).to_broadcast([P, NH, P]),
                                                ALU.mult).then_inc(mix_ready, 1)
                    dve.wait_ge(y_done, 4 * i + 4)
                    dve.wait_ge(out_done, i)
                    for k in range(ZB):
                        last = nc.vector.scalar_tensor_tensor(
                            out=yg[:, k, :], in0=xbc[:, k, :], scalar=dcol[:, k:k + 1],
                            in1=yp[:, k, :, :].rearrange("p b l -> p (b l)"), op0=ALU.mult, op1=ALU.add)
                    step(last)
                    nc.vector.tensor_tensor(yg[:, :, :], yg[:, :, :], zs[:, :, :], ALU.mult).then_inc(yg_ready, 1)
                    dve.wait_ge(new_done, i + 1)
                    for b in range(BATCH):
                        last = nc.vector.tensor_tensor(
                            state[:, b, :].rearrange("p (h n) -> p h n", h=NH), state[:, b, :].rearrange("p (h n) -> p h n", h=NH),
                            carry[:, 1, bass.ds(i + b * TPB, 1), :].rearrange("p t h -> p (t h)").unsqueeze(2)
                            .to_broadcast([P, NH, HD]), ALU.mult)
                    step(last)
                    nc.vector.tensor_tensor(state[:, :, :], state[:, :, :], newp, ALU.add).then_inc(state_ready, 1)
                    x_now = x_all[:, :, :].rearrange("p (b c) n -> p b (c n)", b=BATCH)[:, :, bass.ds(i * DM, DM)]
                    dve.wait_ge(ss_done, i + 1)
                    step(nc.vector.tensor_scalar(rv[:, :], ssp, 1.0 / DIN, EPS_RMS, ALU.mult, ALU.add))
                    inverse_root(nc.vector, step, rv[:, :], r[:, :], rt[:, :], rh[:, :])
                    dve.wait_ge(out_done, i + 1)
                    for b in range(BATCH):
                        last = nc.vector.scalar_tensor_tensor(out=h[:, b, :], in0=outp[:, b, :], scalar=r[:, b:b + 1],
                                                              in1=x_now[:, b, :], op0=ALU.mult, op1=ALU.add)
                    last.then_inc(out_read, 1)
                    dve.wait_ge(out_read, i + 1)
                    layer_norm(nc.vector, step, ns, lambda k: h[:, k, :], lambda k: h[:, k, :], EPS_LN, DM)
                    step(nc.vector.tensor_tensor(h[:, :, :], h[:, :, :], ln_g[:, :].unsqueeze(1)
                                                 .to_broadcast([P, G, DM]), ALU.mult))
                    step(nc.vector.tensor_tensor(h[:, :, :], h[:, :, :], ln_b[:, :].unsqueeze(1)
                                                 .to_broadcast([P, G, DM]), ALU.add))
                    step(nc.vector.tensor_tensor(h[:, :, :], h[:, :, :], x_now, ALU.add))
                    layer_norm(nc.vector, step, ns, lambda k: h[:, k, :], lambda k: x_now[:, k, :], EPS_LN, DM)
                    step.end()
                signals.links = link.count + TPB * MAMBA_LINKS


MAMBA_LINKS = 2 * (TAPS - 1) + 2 + 1 + ROOT_LINKS + 2 * NORM_LINKS + 3

def latent_attention(nc, signals, x_all, ident, d, v_all, o_all, q_dram, k_dram):
    with ExitStack() as ctx:
        def sb(name, shape, dt=F32):
            return ctx.enter_context(nc.sbuf_tensor(name, shape, dt))

        def sem(name):
            return signals.new(name)

        ps = ctx.enter_context(nc.psum_tensor("attn_psum", [P, 8, 512], F32))

        norm1_w = sb("norm1_w", [P, 1])
        wq = sb("wq", [P, 2, DM])
        wdkv = sb("wdkv", [P, LAT])
        wuk = sb("wuk", [LAT, 2, DM])
        wuv = sb("wuv", [LAT, DM])
        lat_g = sb("lat_g", [LAT, 1])
        lat_b = sb("lat_b", [LAT, 1])
        cos = sb("cos", [P, SEQ])
        sin = sb("sin", [P, SEQ])
        identb = sb("identb", [P, P], BF16)
        mask_q = sb("mask_q", [P, P], BF16)
        mask_k = sb("mask_k", [P, P], BF16)

        ss = sb("attn_ss", [P, G])
        rv = sb("attn_rv", [P, G])
        r = sb("attn_r", [P, G])
        rt = sb("attn_rt", [P, G])
        rh = sb("attn_rh", [P, G])
        xs = sb("attn_xs", [P, G, DM])
        xn = sb("attn_xn", [P, G, DM])
        xnT = sb("attn_xnT", [P, W])
        lat = sb("lat", [P, G, LAT])
        latT = sb("latT", [LAT, W])
        ns = NormScratch(sb, "latnorm")
        rot = sb("rot", [P, 2, W])
        rot2 = sb("rot2", [P, 2, W])
        rest = sb("rest", [P, 2, W])
        parts = sb("parts", [P, 2, SPLITS, SEQ], BF16)

        qst = sb("qst", [STACK, SLOTS, 4, SEQ], BF16)
        kst = sb("kst", [STACK, SLOTS, 4, SEQ], BF16)
        vst = sb("vst", [P, 2, TPB, 4, 32])
        neg = sb("neg", [P, 2, 4, TPB])
        nm = sb("nm", [P, 4 * TPB])
        nmr = sb("nmr", [32, P])
        shift = sb("shift", [32, 2, P], BF16)
        pt = sb("pt", [P, 2, 4, 512])
        oc = sb("oc", [P, 512])
        rec = sb("rec", [P, 4, 4])

        loaded, chain = signals.loaded, signals.chain
        folded = sem("attn_folded")
        padded = sem("stacks_padded")
        v_padded = sem("v_padded")
        xn_ready = sem("xn_ready")
        xnT_done = sem("xnT_done")
        xnT_ready = sem("xnT_ready")
        q_done = sem("q_done")
        lat_done = sem("lat_done")
        lat_ready = sem("lat_ready")
        latT_done = sem("latT_done")
        latT_ready = sem("latT_ready")
        k_done = sem("k_done")
        v_done = sem("v_done")
        v_read = sem("v_read")
        rope_ready = sem("rope_ready")
        rot_ready = sem("rot_ready")
        hi_ready = sem("hi_ready")
        rest_ready = sem("rest_ready")
        mid_ready = sem("mid_ready")
        low_ready = sem("low_ready")
        parts_out = [sem(f"parts_out{k}") for k in range(2)]

        stack_loaded = [sem(f"stack_loaded{k}") for k in range(SLOTS)]
        v_staged = sem("v_staged")
        max_done = sem("max_done")
        max_read = sem("max_read")
        nm_ready = sem("nm_ready")
        nmT_done = sem("nmT_done")
        shift_hi = sem("shift_hi")
        shift_rest = sem("shift_rest")
        shift_ready = sem("shift_ready")
        shift_placed = sem("shift_placed")
        st_done = sem("st_done")
        exp_done = sem("exp_done")
        pv_done = sem("pv_done")
        acc_read = sem("acc_read")
        oT_done = sem("oT_done")
        rec_ready = sem("rec_ready")
        o_read = sem("o_read")

        HALVES = SEQ // W
        STEPS = BATCH * HALVES
        NG = BATCH * SLOTS

        units = []
        for t in range(TPB):
            for part in range(2):
                width = min(512, (t + 1) * P - part * 512)
                heads = min(512 // width, 4) if width > 0 else 1
                units += [(t, part, c, heads, width) for c in range(0, 4, heads) if width > 0]
        NU = len(units)
        exps = [(hf, j, max(0, j * P - hf * 512)) for hf in range(HALVES) for j in range(4 * hf + 4)]
        NX = len(exps)
        assert NU % 2 == 0 and NX % 2 == 0

        signals.loads += 16 * 12
        with nc.Block() as block:
            @block.sync
            def _(sp):
                for dst, src in ((norm1_w[:, :], d["norm1_w"]), (wq[:, :, :], d["wq"]), (wdkv[:, :], d["wdkv"]),
                                 (wuk[:, :, :], d["wuk"]), (wuv[:, :], d["wuv"]), (lat_g[:, :], d["lat_g"]),
                                 (lat_b[:, :], d["lat_b"]), (cos[:, :], d["cos"]), (sin[:, :], d["sin"]),
                                 (identb[:, :], d["identb"]), (mask_q[:, :], d["mask_q"]),
                                 (mask_k[:, :], d["mask_k"])):
                    sp.dma_start(dst, src).then_inc(loaded, 16)
                for k in range(SLOTS):
                    sp.dma_start(qst[SROWS:SHIFT_ROW, k, :, :], d["pad"][0:SHIFT_ROW - SROWS, :, :]).then_inc(padded, 16)
                    sp.dma_start(kst[SROWS:STACK, k, :, :], d["pad"]).then_inc(padded, 16)
                with sp.Fori(0, BATCH) as b:
                    for hf in range(HALVES):
                        sp.wait_ge(low_ready, 4 * b + 2 * hf + 2)
                        sl = slice(hf * W, (hf + 1) * W)
                        for g in range(SLOTS):
                            for s, dram in ((0, q_dram), (1, k_dram)):
                                sp.dma_start(
                                    dram[bass.ds(b * SLOTS + g, 1), :, :, sl].rearrange("n s r l -> r (n s) l"),
                                    parts[32 * g:32 * g + 32, s, :, sl]).then_inc(parts_out[hf], 16)

                def load_stacks(n, k):
                    for dram, st in ((q_dram, qst), (k_dram, kst)):
                        for i in range(SPLITS):
                            for j in range(SPLITS):
                                row = (i * SPLITS + j) * AD
                                part = i if dram is q_dram else j
                                sp.dma_start(
                                    st[row:row + AD, k, :, :],
                                    dram[bass.ds(n, 1), part, :, :].rearrange("n (c d) l -> (n d) c l", c=4))\
                                    .then_inc(stack_loaded[k], 16)

                def place_shift(n, k):
                    sp.wait_ge(shift_ready, n + 1)
                    for s in range(SHIFTS):
                        sp.dma_start(qst[SHIFT_ROW + s:SHIFT_ROW + s + 1, k, :, :], shift[:, s, :])\
                            .then_inc(shift_placed, 16)

                for hf in range(HALVES):
                    sp.wait_ge(parts_out[hf], 16 * 2 * SLOTS * BATCH)
                for k in range(SLOTS):
                    load_stacks(k, k)
                place_shift(0, 0)
                with sp.Fori(0, BATCH - 1) as b:
                    for g in range(SLOTS):
                        place_shift(b * SLOTS + g + 1, (g + 1) % SLOTS)
                        sp.wait_ge(pv_done, (b * SLOTS + g + 1) * NX)
                        load_stacks((b + 1) * SLOTS + g, g)
                for g in range(1, SLOTS):
                    place_shift(NG - SLOTS + g, g)

            @block.tensor
            def _(pe):
                pe.wait_ge(loaded, signals.loads)
                pe.wait_ge(folded, 1)
                with pe.Fori(0, BATCH) as b:
                    for hf in range(HALVES):
                        s = HALVES * b + hf
                        pe.wait_ge(xn_ready, s + 1)
                        for t in range(G):
                            last = nc.tensor.transpose(ps[:, 0, t * P:(t + 1) * P], xn[:, t, :], ident[:, :])
                        last.then_inc(xnT_done, 1)
                        pe.wait_ge(xnT_ready, s + 1)
                        pe.wait_ge(lat_ready, s)
                        for t in range(G):
                            last = nc.tensor.matmul(ps[:, 3, t * LAT:(t + 1) * LAT], xnT[:, t * P:(t + 1) * P],
                                                    wdkv[:, :], start=True, stop=True)
                        last.then_inc(lat_done, 1)
                        pe.wait_ge(rope_ready, 2 * s)
                        nc.tensor.matmul(ps[:, 1, :], wq[:, 0, :], xnT[:, :], start=True, stop=True)
                        pe.wait_ge(lat_ready, s + 1)
                        nc.tensor.matmul(ps[:, 2, :], wq[:, 1, :], xnT[:, :], start=True, stop=True).then_inc(q_done, 1)
                        for t in range(G):
                            last = nc.tensor.transpose(ps[0:LAT, 4, t * P:(t + 1) * P], lat[:, t, :], ident[:, :])
                        last.then_inc(latT_done, 1)
                        pe.wait_ge(latT_ready, s + 1)
                        for k in range(2):
                            last = nc.tensor.matmul(ps[:, 5 + k, :], wuk[:, k, :], latT[:, :], start=True, stop=True)
                        last.then_inc(k_done, 1)
                        pe.wait_ge(v_read, s)
                        for t in range(G):
                            last = nc.tensor.matmul(ps[:, 7, t * P:(t + 1) * P], latT[:, t * P:(t + 1) * P], wuv[:, :],
                                                    start=True, stop=True)
                        last.then_inc(v_done, 1)

                pe.wait_ge(rope_ready, 2 * STEPS)
                pe.wait_ge(v_read, STEPS)
                pe.wait_ge(padded, 16 * 2 * SLOTS)

                def maxima(b, g, first=False):
                    n = b * SLOTS + g
                    pe.wait_ge(stack_loaded[g], STACK_DMAS * (b + 1))
                    for u, (t, part, c0, heads, width) in enumerate(units):
                        pe.wait_ge(max_read, n * NU + max(u - 1, 0))
                        diag = part * 512 + width == (t + 1) * P
                        for c in range(heads):
                            out = ps[:, 5 + u % 2, c * width:(c + 1) * width]
                            last = nc.tensor.matmul(
                                out, qst[0:SHIFT_ROW, g, c0 + c, t * P:(t + 1) * P],
                                kst[0:SHIFT_ROW, g, c0 + c, part * 512:part * 512 + width], start=True, stop=not diag)
                            if diag:
                                last = nc.tensor.matmul(out[:, width - P:width], identb[:, :], mask_q[:, :],
                                                        start=False, stop=True)
                        last.then_inc(max_done, 1)
                        yield
                    pe.wait_ge(nm_ready, n + 1)
                    if not first:
                        pe.wait_ge(o_read, 2 * n - 1)
                    nc.tensor.transpose(ps[0:32, 7, 0:P], nm[:, :], ident[:, :]).then_inc(nmT_done, 1)
                    yield

                def exponentials(b, g, final=False):
                    n = b * SLOTS + g

                    def products(u):
                        hf, j, q0 = exps[u]
                        pe.wait_ge(exp_done, 2 * NX * n + 2 * u + 2)
                        if j == 0:
                            pe.wait_ge(acc_read, 2 * n + hf)
                        for c in range(4):
                            last = nc.tensor.matmul(ps[32 * c:32 * c + 32, 4, q0:512], vst[:, g % 2, j, c, :],
                                                    pt[:, u % 2, c, q0:512], start=(j == 0), stop=(j == 4 * hf + 3))
                        last.then_inc(pv_done, 1)

                    def rows_back(hf):
                        pe.wait_ge(acc_read, 2 * n + hf + 1)
                        pe.wait_ge(o_read, 2 * n + hf)
                        if hf == 1 and not final:
                            pe.wait_ge(shift_rest, n + 2)
                        for t in range(4):
                            last = nc.tensor.transpose(ps[:, 7, t * P:(t + 1) * P], oc[:, t * P:(t + 1) * P], ident[:, :])
                        last.then_inc(oT_done, 1)

                    pe.wait_ge(shift_placed, 16 * SHIFTS * (n + 1))
                    pe.wait_ge(v_staged, n + 1)
                    for u, (hf, j, q0) in enumerate(exps):
                        diag = j * P >= hf * 512
                        for pair in range(2):
                            v = 2 * u + pair
                            pe.wait_ge(exp_done, 2 * NX * n + max(v - 1, 0))
                            for c in range(2):
                                out = ps[:, 2 * pair + c, q0:512]
                                last = nc.tensor.matmul(out, kst[0:STACK, g, 2 * pair + c, j * P:(j + 1) * P],
                                                        qst[0:STACK, g, 2 * pair + c, hf * 512 + q0:hf * 512 + 512],
                                                        start=True, stop=not diag)
                                if diag:
                                    last = nc.tensor.matmul(out[:, 0:P], identb[:, :], mask_k[:, :],
                                                            start=False, stop=True)
                            last.then_inc(st_done, 1)
                            yield
                        if u >= 1:
                            products(u - 1)
                            yield
                        if u == BACK_AT:
                            rows_back(0)
                    products(NX - 1)
                    yield
                    rows_back(1)

                def both(running, ahead):
                    for k, _ in enumerate(running):
                        next(ahead, None)
                        if k % 3 == 2:
                            next(ahead, None)
                    assert next(ahead, None) is None

                for _ in maxima(0, 0, first=True):
                    pass
                with pe.Fori(0, BATCH - 1) as b:
                    for g in range(SLOTS):
                        both(exponentials(b, g), maxima(b + (g + 1) // SLOTS, (g + 1) % SLOTS))
                for g in range(SLOTS - 1):
                    both(exponentials(BATCH - 1, g), maxima(BATCH - 1, g + 1))
                for _ in exponentials(BATCH - 1, SLOTS - 1, final=True):
                    pass

            @block.scalar
            def _(act):
                act.wait_ge(loaded, signals.loads)
                with act.Fori(0, BATCH) as b:
                    for hf in range(HALVES):
                        s = HALVES * b + hf
                        act.wait_ge(xnT_done, s + 1)
                        nc.scalar.copy(xnT[:, :], ps[:, 0, :]).then_inc(xnT_ready, 1)
                        act.wait_ge(latT_done, s + 1)
                        nc.scalar.activation(latT[:, :], ps[0:LAT, 4, :], ACT.Identity, bias=lat_b[:, 0:1],
                                             scale=lat_g[:, 0:1]).then_inc(latT_ready, 1)
                        act.wait_ge(v_done, s + 1)
                        vdst = v_all[:, bass.ds(4 * b, 4), 4 * hf:4 * hf + 4, :]
                        nc.scalar.copy(vdst, ps[:, 7, :].rearrange("p (t g m) -> p g t m", t=4, g=4)).then_inc(v_read, 1)
                        for w in range(2):
                            dst = parts[:, w, :, hf * W:(hf + 1) * W]
                            act.wait_ge(rot_ready, 2 * s + w + 1)
                            act.wait_ge(parts_out[hf], 16 * 2 * SLOTS * b)
                            nc.scalar.copy(dst[:, 0, :], rot[:, w, :]).then_inc(hi_ready, 1)
                            act.wait_ge(rest_ready, 2 * s + w + 1)
                            nc.scalar.copy(dst[:, 1, :], rest[:, w, :]).then_inc(mid_ready, 1)

                def keep(n, hf):
                    act.wait_ge(pv_done, NX * n + (4 if hf == 0 else NX))
                    act.wait_ge(oT_done, 2 * n + hf)
                    nc.scalar.copy(oc[:, :], ps[:, 4, :]).then_inc(acc_read, 1)

                with act.Fori(0, NG) as n:
                    for u, (hf, j, q0) in enumerate(exps):
                        for pair in range(2):
                            act.wait_ge(st_done, 2 * NX * n + 2 * u + pair + 1)
                            if pair == 0:
                                act.wait_ge(pv_done, NX * n + max(u - 1, 0))
                            nc.scalar.activation(pt[:, u % 2, 2 * pair:2 * pair + 2, q0:512],
                                                 ps[:, 2 * pair:2 * pair + 2, q0:512], ACT.Exp,
                                                 scale=float(AD) ** -0.5).then_inc(exp_done, 1)
                        if u == 4:
                            keep(n, 0)
                    keep(n, 1)

            @block.gpsimd
            def _(pool):
                with pool.Fori(0, BATCH) as b:
                    for hf in range(HALVES):
                        s = HALVES * b + hf
                        for w in range(2):
                            pool.wait_ge(rope_ready, 2 * s + w + 1)
                            pool.wait_ge(low_ready, 2 * s)
                            nc.gpsimd.tensor_tensor(rot[:, w, :], rot[:, w, :], rot2[:, w, :], ALU.add)\
                                .then_inc(rot_ready, 1)
                            dst = parts[:, w, :, hf * W:(hf + 1) * W]
                            pool.wait_ge(hi_ready, 2 * s + w + 1)
                            nc.gpsimd.tensor_tensor(rest[:, w, :], rot[:, w, :], dst[:, 0, :], ALU.subtract)\
                                .then_inc(rest_ready, 1)
                            pool.wait_ge(mid_ready, 2 * s + w + 1)
                            nc.gpsimd.tensor_tensor(dst[:, 2, :], rest[:, w, :], dst[:, 1, :], ALU.subtract)\
                                .then_inc(low_ready, 1)

                def stage(n, k):
                    nc.gpsimd.tensor_copy(vst[:, k, :, :, 0:AD],
                                          v_all[:, bass.ds(n, 1), :, :].rearrange("p n t (c d) -> p (n t) c d", c=4))\
                        .then_inc(v_staged, 1)

                pool.wait_ge(v_read, STEPS)
                pool.wait_ge(v_padded, 2)
                stage(0, 0)
                stage(1, 1)
                with pool.Fori(1, NG // 2) as m:
                    for k in range(2):
                        pool.wait_ge(pv_done, (2 * m + k - 1) * NX)
                        stage(2 * m + k, k)

            @block.vector
            def _(dve):
                nc.vector.memset(neg[:, :, :, :], -MASKED)
                nc.vector.memset(vst[:, :, :, :, :], 0.0).then_inc(v_padded, 1)
                dve.wait_ge(v_padded, 1)
                nc.vector.memset(vst[:, :, :, :, AD], 1.0).then_inc(v_padded, 1)
                dve.wait_ge(loaded, signals.loads)
                for w in (wq[:, 0, :], wq[:, 1, :], wdkv[:, :]):
                    last = nc.vector.tensor_scalar(w, w, norm1_w[:, 0:1], None, ALU.mult)
                last.then_inc(folded, 1)
                with dve.Fori(0, BATCH) as b:
                    step = Chain(dve, chain, signals.links, b, ATTN_LINKS)
                    for hf in range(HALVES):
                        s = HALVES * b + hf
                        x_now = x_all[:, bass.ds(b * TPB + hf * G, G), :]
                        dve.wait_ge(xnT_done, s)
                        step(nc.vector.tensor_copy(xs[:, :, :], x_now))
                        for t in range(G):
                            last = nc.vector.tensor_tensor_reduce(xn[:, t, :], xs[:, t, :], xs[:, t, :], 1.0, 0.0,
                                                                  ALU.mult, ALU.add, ss[:, t:t + 1])
                        step(last)
                        step(nc.vector.tensor_scalar(rv[:, :], ss[:, :], 1.0 / DM, EPS_RMS2, ALU.mult, ALU.add))
                        inverse_root(nc.vector, step, rv[:, :], r[:, :], rt[:, :], rh[:, :])
                        for t in range(G):
                            last = nc.vector.tensor_scalar(xn[:, t, :], xs[:, t, :], r[:, t:t + 1], None, ALU.mult)
                        last.then_inc(xn_ready, 1)
                        dve.wait_ge(lat_done, s + 1)
                        dve.wait_ge(latT_done, s)
                        layer_norm(nc.vector, step, ns, lambda t: ps[:, 3, t * LAT:(t + 1) * LAT],
                                   lambda t: lat[:, t, :], EPS_LN, LAT, done=lat_ready)
                        dve.wait_ge(q_done, s + 1)
                        dve.wait_ge(low_ready, 2 * s)
                        for w in range(2):
                            if w == 1:
                                dve.wait_ge(k_done, s + 1)
                            pq = ps[:, 1 + 4 * w, :]
                            ps_ = ps[:, 2 + 4 * w, :]
                            sl = slice(hf * W, (hf + 1) * W)
                            nc.vector.tensor_tensor(rot[:, w, :], pq, cos[:, sl], ALU.mult)
                            nc.vector.tensor_tensor(rot2[:, w, :], ps_, sin[:, sl], ALU.mult).then_inc(rope_ready, 1)
                    step.end()
                signals.links += BATCH * ATTN_LINKS

                def maxima(n):
                    for u, (t, part, c0, heads, width) in enumerate(units):
                        dve.wait_ge(max_done, n * NU + u + 1)
                        nc.vector.tensor_reduce(
                            neg[:, part, c0:c0 + heads, t],
                            ps[:, 5 + u % 2, 0:heads * width].rearrange("p (c w) -> p c w", c=heads), AX.X, ALU.max,
                            negate=True).then_inc(max_read, 1)
                        yield
                    dve.wait_ge(max_read, (n + 1) * NU)
                    nc.vector.tensor_tensor(nm[:, :], neg[:, 0, :, :].rearrange("p c t -> p (c t)"),
                                            neg[:, 1, :, :].rearrange("p c t -> p (c t)"), ALU.min).then_inc(nm_ready, 1)
                    yield
                    dve.wait_ge(nmT_done, n + 1)
                    dve.wait_ge(shift_placed, 16 * SHIFTS * n)
                    nc.vector.tensor_copy(shift[:, 0, :], ps[0:32, 7, 0:P]).then_inc(shift_hi, 1)
                    dve.wait_ge(shift_hi, n + 1)
                    nc.vector.tensor_tensor(nmr[:, :], ps[0:32, 7, 0:P], shift[:, 0, :], ALU.subtract).then_inc(shift_rest, 1)
                    dve.wait_ge(shift_rest, n + 1)
                    nc.vector.tensor_copy(shift[:, 1, :], nmr[:, :]).then_inc(shift_ready, 1)

                def norm(n, hf):
                    dve.wait_ge(oT_done, 2 * n + hf + 1)
                    back = ps[:, 7, :].rearrange("p (t c m) -> p t c m", t=4, c=4)
                    nc.vector.reciprocal(rec[:, :, :], back[:, :, :, AD]).then_inc(rec_ready, 1)
                    dve.wait_ge(rec_ready, 2 * n + hf + 1)
                    nc.vector.tensor_tensor(
                        o_all[:, bass.ds(n, 1), 4 * hf:4 * hf + 4, :].rearrange("p n t (c d) -> p (n t) c d", c=4),
                        back[:, :, :, 0:AD], rec[:, :, :].unsqueeze(3).to_broadcast([P, 4, 4, AD]), ALU.mult)\
                        .then_inc(o_read, 1)

                for _ in maxima(0):
                    pass
                with dve.Fori(0, NG - 1) as n:
                    for k, _ in enumerate(maxima(n + 1)):
                        if k == NORM_AT:
                            norm(n, 0)
                    norm(n, 1)
                norm(NG - 1, 0)
                norm(NG - 1, 1)


SLOTS = AH // 4
SHIFTS = 2
STACK = SHIFT_ROW + SHIFTS
STACK_DMAS = 16 * 2 * SPLITS * SPLITS
BACK_AT, NORM_AT = 6, 29
ATTN_LINKS = 2 * (1 + 1 + 1 + ROOT_LINKS + NORM_LINKS - 1)


def experts(nc, signals, x_all, ident, d, o_all):
    with ExitStack() as ctx:
        def sb(name, shape, dt=F32):
            return ctx.enter_context(nc.sbuf_tensor(name, shape, dt))

        def sem(name):
            return signals.new(name)

        ps = ctx.enter_context(nc.psum_tensor("moe_psum", [P, 8, 512], F32))

        norm2_w = sb("norm2_w", [P, 1])
        wo = sb("moe_wo", [P, DM])
        gate_w = sb("gate_w", [P, NE])
        gate_b = sb("gate_b", [P, NE])
        w1 = sb("moe_w1", [P, NE, HID])
        b1 = sb("moe_b1", [P, NE, HID // P])
        w2 = sb("moe_w2", [P, NE, HID // P, DM])
        b2 = sb("moe_b2", [G * NE, G * DM])
        order = sb("order", [P, NE])

        ost = sb("ost", [P, G, DM])
        oT = sb("moe_oT", [P, W])
        x2 = sb("x2", [P, 2, G, DM])
        acc = sb("moe_acc", [P, 2, G, DM])
        xn = sb("moe_xn", [P, G, DM])
        xnT = sb("moe_xnT", [P, 2, W])
        ss = sb("moe_ss", [P, G])
        rv = sb("moe_rv", [P, G])
        r = sb("moe_r", [P, G])
        rt = sb("moe_rt", [P, G])
        rh = sb("moe_rh", [P, G])
        logits = sb("logits", [P, G, NE])
        best = sb("best", [P, G])
        onehot = sb("onehot", [P, 2, G, NE])
        onehotT = sb("onehotT", [G * NE, P])
        hs = sb("moe_hs", [P, 2, HID // P, W])
        ns = NormScratch(sb, "moenorm")

        loaded, chain = signals.loaded, signals.chain
        folded = sem("moe_folded")
        ost_ready = sem("ost_ready")
        oT_done = sem("moe_oT_done")
        oT_ready = sem("moe_oT_ready")
        ao_done = sem("ao_done")
        x2_ready = sem("x2_ready")
        xn_ready = sem("moe_xn_ready")
        xnT_done = sem("moe_xnT_done")
        xnT_ready = sem("moe_xnT_ready")
        gate_done = sem("gate_done")
        gate_read = sem("gate_read")
        onehot_ready = sem("onehot_ready")
        onehotT_done = sem("onehotT_done")
        onehotT_ready = sem("onehotT_ready")
        b2_done = sem("b2_done")
        b2_read = sem("b2_read")
        h_done = sem("moe_h_done")
        h_act = sem("moe_h_act")
        h_dve = sem("moe_h_dve")
        y_done = sem("moe_y_done")
        y_read = sem("moe_y_read")

        HALVES = SEQ // W
        STEPS = BATCH * HALVES
        HB = HID // P
        small = ps[:, 0, :]

        signals.loads += 16 * 9
        with nc.Block() as block:
            @block.sync
            def _(sp):
                for dst, src in ((norm2_w[:, :], d["norm2_w"]), (wo[:, :], d["moe_wo"]), (gate_w[:, :], d["gate_w"]),
                                 (w1[:, :, :], d["moe_w1"]), (b1[:, :, :], d["moe_b1"]), (w2[:, :, :, :], d["moe_w2"]),
                                 (b2[:, :], d["moe_b2"]), (order[:, :], d["order"]),
                                 (gate_b[:, :], d["gate_b"].partition_broadcast(P))):
                    sp.dma_start(dst, src).then_inc(loaded, 16)

            @block.tensor
            def _(pe):
                pe.wait_ge(loaded, signals.loads)
                pe.wait_ge(folded, 1)

                def front(s, hf):
                    pe.wait_ge(ost_ready, s + 1)
                    pe.wait_ge(onehotT_ready, s)
                    for t in range(G):
                        last = nc.tensor.transpose(ps[:, 0, t * P:(t + 1) * P], ost[:, t, :], ident[:, :])
                    last.then_inc(oT_done, 1)
                    yield
                    pe.wait_ge(oT_ready, s + 1)
                    pe.wait_ge(b2_read, s)
                    for t in range(G):
                        last = nc.tensor.matmul(ps[:, 1, t * P:(t + 1) * P], oT[:, t * P:(t + 1) * P], wo[:, :],
                                                start=True, stop=True)
                    last.then_inc(ao_done, 1)
                    yield
                    pe.wait_ge(xn_ready, s + 1)
                    for t in range(G):
                        last = nc.tensor.transpose(ps[:, 2, t * P:(t + 1) * P], xn[:, t, :], ident[:, :])
                    last.then_inc(xnT_done, 1)
                    yield
                    pe.wait_ge(xnT_ready, s + 1)
                    for t in range(G):
                        last = nc.tensor.matmul(small[:, t * NE:(t + 1) * NE], xnT[:, hf, t * P:(t + 1) * P],
                                                gate_w[:, :], start=True, stop=True)
                    last.then_inc(gate_done, 1)
                    yield
                    pe.wait_ge(onehot_ready, s + 1)
                    nc.tensor.transpose(small[0:G * NE, P:2 * P], onehot[:, hf, :, :].rearrange("p t e -> p (t e)"),
                                        ident[:, :]).then_inc(onehotT_done, 1)
                    yield
                    pe.wait_ge(onehotT_ready, s + 1)
                    nc.tensor.matmul(ps[:, 1, :], onehotT[:, :], b2[:, :], start=True, stop=True).then_inc(b2_done, 1)
                    yield

                def expert_steps(s, hf):
                    blocks = [(e, k) for e in range(NE) for k in range(HB)]

                    def hidden(n):
                        e, k = blocks[n]
                        q = n - 3
                        if q < 0:
                            pe.wait_ge(h_act, 8 * s)
                            pe.wait_ge(h_dve, 8 * s)
                        else:
                            pe.wait_ge(h_act if q % 2 == 0 else h_dve, 8 * s + q // 2 + 1)
                        nc.tensor.matmul(ps[:, 3 + n % 3, :], w1[:, e, k * P:(k + 1) * P], xnT[:, hf, :],
                                         start=True, stop=True).then_inc(h_done, 1)

                    def outputs(e):
                        pe.wait_ge(h_act, 8 * s + 2 * e + 2)
                        pe.wait_ge(h_dve, 8 * s + 2 * e + 2)
                        pe.wait_ge(y_read, 4 * s + max(e - 1, 0))
                        for t in range(G):
                            for k in range(HB):
                                last = nc.tensor.matmul(ps[:, 6 + e % 2, t * P:(t + 1) * P],
                                                        hs[:, e % 2, k, t * P:(t + 1) * P], w2[:, e, k, :],
                                                        start=(k == 0), stop=(k == HB - 1))
                        last.then_inc(y_done, 1)

                    for n in range(NE * HB):
                        hidden(n)
                        yield
                        if n % HB == 1 and n > HB:
                            outputs(n // HB - 1)
                            yield
                    outputs(NE - 1)
                    yield

                for _ in front(0, 0):
                    pass
                with pe.Fori(0, BATCH - 1) as b:
                    for hf in range(HALVES):
                        s = HALVES * b + hf
                        ahead = front(s + 1, 1 - hf)
                        for k, _ in enumerate(expert_steps(s, hf)):
                            if k % 3 == 2:
                                next(ahead, None)
                        for _ in ahead:
                            pass
                s = STEPS - 2
                ahead = front(s + 1, 1)
                for k, _ in enumerate(expert_steps(s, 0)):
                    if k % 3 == 2:
                        next(ahead, None)
                for _ in ahead:
                    pass
                for _ in expert_steps(s + 1, 1):
                    pass

            @block.scalar
            def _(act):
                act.wait_ge(loaded, signals.loads)

                def front(s, hf, first=False):
                    act.wait_ge(oT_done, s + 1)
                    nc.scalar.copy(oT[:, :], ps[:, 0, :]).then_inc(oT_ready, 1)
                    yield
                    act.wait_ge(xnT_done, s + 1)
                    if not first:
                        act.wait_ge(h_done, 16 * (s - 1))
                    nc.scalar.copy(xnT[:, hf, :], ps[:, 2, :]).then_inc(xnT_ready, 1)
                    yield
                    act.wait_ge(onehotT_done, s + 1)
                    nc.scalar.copy(onehotT[:, :], small[0:G * NE, P:2 * P]).then_inc(onehotT_ready, 1)
                    yield

                def relus(s):
                    for n in range(0, NE * HB, 2):
                        e, k = n // HB, n % HB
                        act.wait_ge(h_done, 16 * s + n + 1)
                        act.wait_ge(y_done, 4 * s + max(e - 1, 0))
                        nc.scalar.activation(hs[:, e % 2, k, :], ps[:, 3 + n % 3, :], ACT.Relu, bias=b1[:, e, k:k + 1])\
                            .then_inc(h_act, 1)
                        yield

                for _ in front(0, 0, first=True):
                    pass

                def step(s, hf, more=True):
                    ahead = front(s + 1, 1 - hf) if more else iter(())
                    for k, _ in enumerate(relus(s)):
                        if k in ACT_FRONT:
                            next(ahead, None)
                    for _ in ahead:
                        pass

                with act.Fori(0, BATCH - 1) as b:
                    for hf in range(HALVES):
                        step(HALVES * b + hf, hf)
                step(STEPS - 2, 0)
                step(STEPS - 1, 1, more=False)

            @block.vector
            def _(dve):
                dve.wait_ge(loaded, signals.loads)
                nc.vector.tensor_scalar(gate_w[:, :], gate_w[:, :], norm2_w[:, 0:1], None, ALU.mult)
                nc.vector.tensor_scalar(w1[:, :, :], w1[:, :, :], norm2_w[:, 0:1], None, ALU.mult).then_inc(folded, 1)

                def front(b, s, hf, step):
                    x_now = x_all[:, bass.ds(b * TPB + hf * G, G), :]
                    dve.wait_ge(oT_done, s)
                    for g in range(SLOTS):
                        last = nc.vector.tensor_copy(ost[:, :, 32 * g:32 * g + 32],
                                                     o_all[:, bass.ds(b * SLOTS + g, 1), 4 * hf:4 * hf + 4, :]
                                                     .rearrange("p n t m -> p (n t) m"))
                    last.then_inc(ost_ready, 1)
                    yield
                    dve.wait_ge(ao_done, s + 1)
                    dve.wait_ge(xnT_done, s)
                    step(nc.vector.tensor_tensor(x2[:, hf, :, :], ps[:, 1, :].rearrange("p (t n) -> p t n", t=G), x_now,
                                                 ALU.add))
                    for t in range(G):
                        last = nc.vector.tensor_tensor_reduce(xn[:, t, :], x2[:, hf, t, :], x2[:, hf, t, :], 1.0, 0.0,
                                                              ALU.mult, ALU.add, ss[:, t:t + 1])
                    step(last)
                    step(nc.vector.tensor_scalar(rv[:, :], ss[:, :], 1.0 / DM, EPS_RMS2, ALU.mult, ALU.add))
                    inverse_root(nc.vector, step, rv[:, :], r[:, :], rt[:, :], rh[:, :])
                    for t in range(G):
                        last = nc.vector.tensor_scalar(xn[:, t, :], x2[:, hf, t, :], r[:, t:t + 1], None, ALU.mult)
                    last.then_inc(xn_ready, 1)
                    nc.vector.tensor_tensor(acc[:, hf, :, :], x2[:, hf, :, :], x_now, ALU.add)
                    yield
                    dve.wait_ge(gate_done, s + 1)
                    step(nc.vector.tensor_tensor(logits[:, :, :], small[:, 0:G * NE].rearrange("p (t e) -> p t e", t=G),
                                                 gate_b[:, :].unsqueeze(1).to_broadcast([P, G, NE]), ALU.add))
                    step(nc.vector.tensor_reduce(best[:, :], logits[:, :, :], AX.X, ALU.max))
                    step(nc.vector.tensor_tensor(logits[:, :, :], logits[:, :, :],
                                                 best[:, :].unsqueeze(2).to_broadcast([P, G, NE]), ALU.is_equal))
                    step(nc.vector.tensor_tensor(logits[:, :, :], logits[:, :, :],
                                                 order[:, :].unsqueeze(1).to_broadcast([P, G, NE]), ALU.mult))
                    step(nc.vector.tensor_reduce(best[:, :], logits[:, :, :], AX.X, ALU.max))
                    nc.vector.tensor_tensor(onehot[:, hf, :, :], logits[:, :, :],
                                            best[:, :].unsqueeze(2).to_broadcast([P, G, NE]), ALU.is_equal)\
                        .then_inc(onehot_ready, 1)
                    yield
                    dve.wait_ge(b2_done, s + 1)
                    nc.vector.tensor_tensor(acc[:, hf, :, :], acc[:, hf, :, :],
                                            ps[:, 1, :].rearrange("p (t n) -> p t n", t=G), ALU.add).then_inc(b2_read, 1)
                    yield

                def back(b, s, hf, step):
                    def take(e):
                        dve.wait_ge(y_done, 4 * s + e + 1)
                        if e == 0:
                            dve.wait_ge(b2_read, s + 1)
                        else:
                            dve.wait_ge(y_read, 4 * s + e)
                        for t in range(G):
                            last = nc.vector.scalar_tensor_tensor(
                                out=acc[:, hf, t, :], in0=ps[:, 6 + e % 2, t * P:(t + 1) * P],
                                scalar=onehot[:, hf, t, e:e + 1], in1=acc[:, hf, t, :], op0=ALU.mult, op1=ALU.add)
                        last.then_inc(y_read, 1)

                    for n in range(1, NE * HB, 2):
                        e, k = n // HB, n % HB
                        dve.wait_ge(h_done, 16 * s + n + 1)
                        dve.wait_ge(y_done, 4 * s + max(e - 1, 0))
                        nc.vector.tensor_scalar(hs[:, e % 2, k, :], ps[:, 3 + n % 3, :], b1[:, e, k:k + 1], 0.0,
                                                ALU.add, ALU.max).then_inc(h_dve, 1)
                        yield
                        if n in (9, 13):
                            take(n // HB - 2)
                            yield
                    for e in (2, 3):
                        take(e)
                    dve.wait_ge(y_read, 4 * s + 4)
                    x_now = x_all[:, bass.ds(b * TPB + hf * G, G), :]
                    layer_norm(nc.vector, step, ns, lambda t: acc[:, hf, t, :], lambda t: x_now[:, t, :], EPS_LN, DM)

                def both(b, s, hf, step, more=True):
                    ahead = front(b + (1 if hf else 0), s + 1, 1 - hf, step) if more else iter(())
                    for k, _ in enumerate(back(b, s, hf, step)):
                        if k in DVE_FRONT:
                            next(ahead, None)
                    for _ in ahead:
                        pass

                link = Chain(dve, chain, signals.links)
                for _ in front(0, 0, 0, link):
                    pass
                with dve.Fori(0, BATCH - 1) as b:
                    step = Chain(dve, chain, link.start + link.count, b, MOE_LINKS)
                    for hf in range(HALVES):
                        both(b, HALVES * b + hf, hf, step)
                    step.end()
                link = Chain(dve, chain, link.start + link.count + (BATCH - 1) * MOE_LINKS)
                both(BATCH - 1, STEPS - 2, 0, link)
                both(BATCH - 1, STEPS - 1, 1, link, more=False)
                signals.links = link.start + link.count


DVE_FRONT = (0, 2, 5, 8)
ACT_FRONT = (1, 3, 5)
MOE_LINKS = 2 * (1 + 1 + 1 + ROOT_LINKS + 5 + NORM_LINKS)


def flow_attention(nc, signals, x_all, ones, ident, d):
    with ExitStack() as ctx:
        def sb(name, shape, dt=F32):
            return ctx.enter_context(nc.sbuf_tensor("fl_" + name, shape, dt))

        def sem(name):
            return signals.new("fl_" + name)

        ps = ctx.enter_context(nc.psum_tensor("flow_psum", [P, 8, 512], F32))
        PAIR = 2
        seqs = range(PAIR)
        A = [ps[:, 4 * s:4 * s + 2, :] for s in seqs]
        B = [ps[:, 4 * s + 2:4 * s + 4, :] for s in seqs]

        def tiles(banks):
            return banks.rearrange("p k (t n) -> p (k t) n", n=P)

        def rows(banks):
            return banks[:, 0, 0:2 * TPB * AH].rearrange("p (w t h) -> p w t h", w=2, t=TPB)

        wq, wk, wv, wo = (sb(n, [P, DM]) for n in ("wq", "wk", "wv", "wo"))
        bq = sb("bq", [P, 1])
        bk = sb("bk", [P, 1])
        bv = sb("bv", [P, DM])
        bo = sb("bo", [P, DM])
        head = sb("head", [P, AH])
        same = sb("same", [P, DM])

        xs = sb("xs", [P, PAIR, TPB, DM])
        xT = sb("xT", [P, PAIR, SEQ])
        qT = sb("qT", [P, PAIR, SEQ])
        kT = sb("kT", [P, PAIR, SEQ])
        qe = sb("qe", [P, PAIR, SEQ])
        ke = sb("ke", [P, PAIR, SEQ])
        sums = sb("sums", [P, PAIR, 2])
        sume = sb("sume", [P, PAIR, 2])
        blk = sb("blk", [P, PAIR, 2, AH])
        vb = sb("vb", [P, PAIR, TPB, DM])
        ktok = sb("ktok", [P, PAIR, TPB, DM])
        qtok = sb("qtok", [P, PAIR, TPB, DM])
        flow = sb("flow", [P, PAIR, 2, TPB, AH])
        gblk = sb("gblk", [P, PAIR, 2, AH])
        alloc = sb("alloc", [P, PAIR, TPB, AH])
        comp = sb("comp", [P, PAIR, TPB, AH])
        total = sb("total", [P, PAIR, AH])
        weight = sb("weight", [P, PAIR, TPB, AH])
        kv = sb("kv", [P, PAIR, DM])
        ot = sb("ot", [P, PAIR, TPB, DM])
        oT = sb("oT", [P, PAIR, SEQ])
        ns = [NormScratch(sb, f"norm{s}", TPB) for s in seqs]

        loaded, chain = signals.loaded, signals.chain
        names = ("xs_ready", "xT_done", "xT_ready", "q_done", "k_done", "q_ready", "k_ready", "v_done", "v_ready",
                 "ktok_done", "ktok_ready", "qtok_done", "qtok_ready", "sums_ready", "eps_ready", "blk_ready", "flow_done",
                 "flow_ready", "g_done", "gblk_ready", "cons_done", "alloc_ready", "clip_ready", "exp_ready",
                 "total_done", "total_ready", "comp_ready", "vs_ready", "kv_done", "kv_ready", "weight_ready",
                 "o_done", "o_ready", "oT_done", "oT_ready", "out_done")
        done = {n: sem(n) for n in names}

        signals.loads += 16 * 10
        with nc.Block() as block:
            @block.sync
            def _(sp):
                for dst, src in ((wq, "fl_wq"), (wk, "fl_wk"), (wv, "fl_wv"), (wo, "fl_wo"), (bq, "fl_bq"), (bk, "fl_bk"),
                                 (head, "head"), (same, "same")):
                    sp.dma_start(dst[:, :], d[src]).then_inc(loaded, 16)
                for dst, src in ((bv, "fl_bv"), (bo, "fl_bo")):
                    sp.dma_start(dst[:, :], d[src].partition_broadcast(P)).then_inc(loaded, 16)

            @block.tensor
            def _(pe):
                pe.wait_ge(loaded, signals.loads)

                def tile(src, s, t):
                    return src[:, s, t * P:(t + 1) * P]

                with pe.Fori(0, BATCH // PAIR) as m:
                    def wait(name, s):
                        pe.wait_ge(done[name], PAIR * m + s + 1)

                    for s in seqs:
                        wait("xs_ready", s)
                        for t in range(TPB):
                            last = nc.tensor.transpose(tiles(A[s])[:, t, :], xs[:, s, t, :], ident[:, :])
                        last.then_inc(done["xT_done"], 1)
                    for s in seqs:
                        wait("xT_ready", s)
                        for k in range(2):
                            last = nc.tensor.matmul(A[s][:, k, :], wk[:, :], xT[:, s, k * 512:(k + 1) * 512],
                                                    start=True, stop=True)
                        last.then_inc(done["k_done"], 1)
                        for k in range(2):
                            last = nc.tensor.matmul(B[s][:, k, :], wq[:, :], xT[:, s, k * 512:(k + 1) * 512],
                                                    start=True, stop=True)
                        last.then_inc(done["q_done"], 1)
                    for s in seqs:
                        wait("k_ready", s)
                        for t in range(TPB):
                            last = nc.tensor.transpose(tiles(A[s])[:, t, :], tile(kT, s, t), ident[:, :])
                        last.then_inc(done["ktok_done"], 1)
                        wait("q_ready", s)
                        for t in range(TPB):
                            last = nc.tensor.matmul(tiles(B[s])[:, t, :], tile(xT, s, t), wv[:, :], start=True, stop=True)
                        last.then_inc(done["v_done"], 1)
                    for s in seqs:
                        wait("ktok_ready", s)
                        wait("blk_ready", s)
                        for w, src in enumerate((qe, ke)):
                            for t in range(TPB):
                                last = nc.tensor.matmul(rows(A[s])[:, w, t, :], tile(src, s, t), blk[:, s, w, :],
                                                        start=True, stop=True)
                        last.then_inc(done["flow_done"], 1)
                        wait("v_ready", s)
                        for t in range(TPB):
                            last = nc.tensor.transpose(tiles(B[s])[:, t, :], tile(qT, s, t), ident[:, :])
                        last.then_inc(done["qtok_done"], 1)
                    for s in seqs:
                        wait("flow_ready", s)
                        wait("qtok_ready", s)
                        for w, src in enumerate((ktok, qtok)):
                            for t in range(TPB):
                                last = nc.tensor.matmul(B[s][:, 0, w * AH:(w + 1) * AH], src[:, s, t, :],
                                                        flow[:, s, 1 - w, t, :], start=(t == 0), stop=(t == TPB - 1))
                        last.then_inc(done["g_done"], 1)
                    for s in seqs:
                        wait("gblk_ready", s)
                        for w, src in enumerate((qe, ke)):
                            for t in range(TPB):
                                last = nc.tensor.matmul(rows(A[s])[:, w, t, :], tile(src, s, t), gblk[:, s, w, :],
                                                        start=True, stop=True)
                        last.then_inc(done["cons_done"], 1)
                    for s in seqs:
                        wait("exp_ready", s)
                        for t in range(TPB):
                            last = nc.tensor.matmul(B[s][:, 0, 0:AH], ones[:, :], comp[:, s, t, :],
                                                    start=(t == 0), stop=(t == TPB - 1))
                        last.then_inc(done["total_done"], 1)
                    for s in seqs:
                        wait("vs_ready", s)
                        wait("alloc_ready", s)
                        for t in range(TPB):
                            last = nc.tensor.matmul(A[s][:, 0, 0:DM], ktok[:, s, t, :], vb[:, s, t, :],
                                                    start=(t == 0), stop=(t == TPB - 1))
                        last.then_inc(done["kv_done"], 1)
                    for s in seqs:
                        wait("kv_ready", s)
                        for t in range(TPB):
                            last = nc.tensor.matmul(tiles(B[s])[:, t, :], tile(qT, s, t), kv[:, s, :], start=True, stop=True)
                        last.then_inc(done["o_done"], 1)
                    for s in seqs:
                        wait("o_ready", s)
                        for t in range(TPB):
                            last = nc.tensor.transpose(tiles(A[s])[:, t, :], ot[:, s, t, :], ident[:, :])
                        last.then_inc(done["oT_done"], 1)
                    for s in seqs:
                        wait("oT_ready", s)
                        for t in range(TPB):
                            last = nc.tensor.matmul(tiles(B[s])[:, t, :], tile(oT, s, t), wo[:, :], start=True, stop=True)
                        last.then_inc(done["out_done"], 1)

            @block.scalar
            def _(act):
                act.wait_ge(loaded, signals.loads)
                with act.Fori(0, BATCH // PAIR) as m:
                    def wait(name, s):
                        act.wait_ge(done[name], PAIR * m + s + 1)

                    for s in seqs:
                        wait("xT_done", s)
                        nc.scalar.copy(xT[:, s, :], A[s].rearrange("p k n -> p (k n)")).then_inc(done["xT_ready"], 1)
                    for s in seqs:
                        wait("k_done", s)
                        nc.scalar.activation(kT[:, s, :], A[s].rearrange("p k n -> p (k n)"), ACT.Sigmoid, bias=bk[:, 0:1],
                                             accum_out=sums[:, s, 0:1]).then_inc(done["k_ready"], 1)
                        wait("q_done", s)
                        nc.scalar.activation(qT[:, s, :], B[s].rearrange("p k n -> p (k n)"), ACT.Sigmoid, bias=bq[:, 0:1],
                                             accum_out=sums[:, s, 1:2]).then_inc(done["q_ready"], 1)
                    for s in seqs:
                        wait("ktok_done", s)
                        nc.scalar.copy(ktok[:, s, :, :], tiles(A[s])).then_inc(done["ktok_ready"], 1)
                    for s in seqs:
                        wait("qtok_done", s)
                        nc.scalar.copy(qtok[:, s, :, :], tiles(B[s])).then_inc(done["qtok_ready"], 1)
                    for s in seqs:
                        wait("cons_done", s)
                        nc.scalar.activation(alloc[:, s, :, :], rows(A[s])[:, 0, :, :], ACT.Sigmoid)\
                            .then_inc(done["alloc_ready"], 1)
                    for s in seqs:
                        wait("clip_ready", s)
                        nc.scalar.activation(comp[:, s, :, :], comp[:, s, :, :], ACT.Exp).then_inc(done["exp_ready"], 1)
                    for s in seqs:
                        wait("oT_done", s)
                        nc.scalar.copy(oT[:, s, :], A[s].rearrange("p k n -> p (k n)")).then_inc(done["oT_ready"], 1)

            @block.vector
            def _(dve):
                dve.wait_ge(loaded, signals.loads)
                with dve.Fori(0, BATCH // PAIR) as m:
                    step = Chain(dve, chain, signals.links, m, FLOW_LINKS)

                    def wait(name, s):
                        dve.wait_ge(done[name], PAIR * m + s + 1)

                    def x_now(s):
                        return x_all[:, bass.ds(m * (PAIR * TPB) + s * TPB, TPB), :]

                    for s in seqs:
                        nc.vector.tensor_copy(xs[:, s, :, :], x_now(s)).then_inc(done["xs_ready"], 1)
                    for s in seqs:
                        wait("k_ready", s)
                        nc.vector.tensor_scalar(ke[:, s, :], kT[:, s, :], FLOW_EPS, None, ALU.add)
                        wait("q_ready", s)
                        nc.vector.tensor_scalar(qe[:, s, :], qT[:, s, :], FLOW_EPS, None, ALU.add)
                        step(nc.vector.tensor_scalar(sume[:, s, :], sums[:, s, :], FLOW_EPS, None, ALU.add))
                        for w in range(2):
                            last = nc.vector.tensor_scalar(blk[:, s, w, :], head[:, :], sume[:, s, w:w + 1], None, ALU.mult)
                        last.then_inc(done["blk_ready"], 1)
                    for s in seqs:
                        wait("v_done", s)
                        nc.vector.tensor_tensor(vb[:, s, :, :], tiles(B[s]), bv[:, :].unsqueeze(1).to_broadcast([P, TPB, DM]),
                                                ALU.add).then_inc(done["v_ready"], 1)
                    for s in seqs:
                        wait("flow_done", s)
                        nc.vector.reciprocal(flow[:, s, :, :, :], rows(A[s])).then_inc(done["flow_ready"], 1)
                    for s in seqs:
                        wait("g_done", s)
                        nc.vector.scalar_tensor_tensor(
                            out=gblk[:, s, :, :], in0=B[s][:, 0, 0:2 * AH].rearrange("p (w h) -> p w h", w=2), scalar=FLOW_EPS,
                            in1=head[:, :].unsqueeze(1).to_broadcast([P, 2, AH]), op0=ALU.add, op1=ALU.mult)\
                            .then_inc(done["gblk_ready"], 1)
                    for s in seqs:
                        wait("alloc_ready", s)
                        nc.vector.tensor_scalar(comp[:, s, :, :], rows(A[s])[:, 1, :, :], -1.0, 1.0, ALU.max, ALU.min)\
                            .then_inc(done["clip_ready"], 1)
                    for s in seqs:
                        wait("total_done", s)
                        wait("exp_ready", s)
                        step(nc.vector.reciprocal(total[:, s, :], B[s][:, 0, 0:AH]))
                        step(nc.vector.scalar_tensor_tensor(
                            out=comp[:, s, :, :], in0=comp[:, s, :, :], scalar=float(SEQ),
                            in1=total[:, s, :].unsqueeze(1).to_broadcast([P, TPB, AH]), op0=ALU.mult, op1=ALU.mult))
                        split = vb[:, s, :, :].rearrange("p t (h n) -> p (t h) n", h=AH)
                        nc.vector.tensor_tensor(
                            split, split, comp[:, s, :, :].rearrange("p t h -> p (t h)").unsqueeze(2)
                            .to_broadcast([P, TPB * AH, AD]), ALU.mult).then_inc(done["vs_ready"], 1)
                        wait("alloc_ready", s)
                        step(nc.vector.tensor_tensor(weight[:, s, :, :], alloc[:, s, :, :], flow[:, s, 0, :, :], ALU.mult))
                    for s in seqs:
                        wait("kv_done", s)
                        nc.vector.tensor_tensor(kv[:, s, :], A[s][:, 0, 0:DM], same[:, :], ALU.mult)\
                            .then_inc(done["kv_ready"], 1)
                    for s in seqs:
                        wait("o_done", s)
                        nc.vector.tensor_tensor(
                            ot[:, s, :, :].rearrange("p t (h n) -> p (t h) n", h=AH),
                            tiles(B[s]).rearrange("p t (h n) -> p (t h) n", h=AH),
                            weight[:, s, :, :].rearrange("p t h -> p (t h)").unsqueeze(2)
                            .to_broadcast([P, TPB * AH, AD]), ALU.mult).then_inc(done["o_ready"], 1)
                        wait("xT_done", s)
                        step(nc.vector.tensor_tensor(xs[:, s, :, :], xs[:, s, :, :],
                                                     bo[:, :].unsqueeze(1).to_broadcast([P, TPB, DM]), ALU.add))
                    for s in seqs:
                        wait("out_done", s)
                        step(nc.vector.tensor_tensor(xs[:, s, :, :], xs[:, s, :, :], tiles(B[s]), ALU.add))
                        layer_norm(nc.vector, step, ns[s], lambda t: xs[:, s, t, :], lambda t: x_now(s)[:, t, :], EPS_LN, DM, TPB)
                    step.end()
                signals.links += BATCH // PAIR * FLOW_LINKS


FLOW_LINKS = 2 * (1 + 3 + 1 + 1 + NORM_LINKS)


def ternary_mlp(nc, signals, x_all, ones, ident, d, out):
    with ExitStack() as ctx:
        def sb(name, shape, dt=F32):
            return ctx.enter_context(nc.sbuf_tensor("tm_" + name, shape, dt))

        def sem(name):
            return signals.new("tm_" + name)

        ps = ctx.enter_context(nc.psum_tensor("mlp_psum", [P, 8, 512], F32))
        HB = FH // P
        STEPS = TILES // G
        wf = sb("wf", [P, FH])
        wp = sb("wp", [P, HB, DM])
        wf3 = sb("wf3", [P, FH])
        wp3 = sb("wp3", [P, HB, DM])
        low = sb("low", [P, FH])
        asum = sb("asum", [P, 2])
        bound = sb("bound", [P, 2])
        nbound = sb("nbound", [P, 2])
        ln_w = sb("ln_w", [P, HB])
        ln_b = sb("ln_b", [P, HB])

        xs = sb("xs", [P, 2, G, DM])
        xT = sb("xT", [P, 2, W])
        g = sb("g", [P, 2, G, FH])
        nT = sb("nT", [P, HB, W])
        y = sb("y", [P, 2, G, DM])
        ns = NormScratch(sb, "norm_h")
        ns2 = NormScratch(sb, "norm_x")

        loaded, chain = signals.loaded, signals.chain
        sums_ready = sem("sums_ready")
        sums_done = sem("sums_done")
        w_ready = sem("w_ready")
        xs_ready = sem("xs_ready")
        xT_done = sem("xT_done")
        xT_ready = sem("xT_ready")
        h_done = sem("h_done")
        g_ready = sem("g_ready")
        n_ready = sem("n_ready")
        nT_done = sem("nT_done")
        nT_ready = sem("nT_ready")
        y_done = sem("y_done")
        y_read = sem("y_read")
        y_ready = sem("y_ready")
        stored = [sem(f"stored{k}") for k in range(2)]

        signals.loads += 16 * 4
        with nc.Block() as block:
            @block.sync
            def _(sp):
                for dst, src in ((wf[:, :], "wf"), (wp[:, :, :], "wp"), (ln_w[:, :], "tm_ln_w"), (ln_b[:, :], "tm_ln_b")):
                    sp.dma_start(dst, d[src]).then_inc(loaded, 16)
                with sp.Fori(0, STEPS // 2) as m:
                    for hf in range(2):
                        s = 2 * m + hf
                        sp.wait_ge(y_ready, s + 1)
                        sp.dma_start(out[:, bass.ds(s * G, G), :], y[:, hf, :, :]).then_inc(stored[hf], 16)
                for hf in range(2):
                    sp.wait_ge(stored[hf], 16 * (STEPS // 2))

            @block.tensor
            def _(pe):
                pe.wait_ge(sums_ready, 1)
                nc.tensor.matmul(ps[:, 0, 0:2], ones[:, :], asum[:, :], start=True, stop=True).then_inc(sums_done, 1)
                pe.wait_ge(w_ready, 1)

                def front(s, hf):
                    pe.wait_ge(xs_ready, s + 1)
                    for t in range(G):
                        last = nc.tensor.transpose(ps[:, 0, t * P:(t + 1) * P], xs[:, hf, t, :], ident[:, :])
                    last.then_inc(xT_done, 1)
                    pe.wait_ge(xT_ready, s + 1)
                    for t in range(G):
                        pe.wait_ge(g_ready, 4 * s + max(t - 1, 0))
                        nc.tensor.matmul(ps[:, 1 + t % 2, :], xT[:, hf, t * P:(t + 1) * P], wf3[:, :],
                                         start=True, stop=True).then_inc(h_done, 1)

                def back(s, hf):
                    pe.wait_ge(n_ready, s + 1)
                    pe.wait_ge(nT_ready, 4 * s)
                    for k in range(HB):
                        for t in range(G):
                            last = nc.tensor.transpose(ps[:, 3 + k, t * P:(t + 1) * P], g[:, hf, t, k * P:(k + 1) * P],
                                                       ident[:, :])
                        last.then_inc(nT_done, 1)
                    pe.wait_ge(nT_ready, 4 * s + 4)
                    pe.wait_ge(y_read, s)
                    for t in range(G):
                        for k in range(HB):
                            last = nc.tensor.matmul(ps[:, 7, t * P:(t + 1) * P], nT[:, k, t * P:(t + 1) * P], wp3[:, k, :],
                                                    start=(k == 0), stop=(k == HB - 1))
                    last.then_inc(y_done, 1)

                front(0, 0)
                with pe.Fori(0, STEPS // 2 - 1) as m:
                    for hf in range(2):
                        front(2 * m + hf + 1, 1 - hf)
                        back(2 * m + hf, hf)
                front(STEPS - 1, 1)
                back(STEPS - 2, 0)
                back(STEPS - 1, 1)

            @block.scalar
            def _(act):
                act.wait_ge(loaded, signals.loads)

                def front(s, hf):
                    act.wait_ge(xT_done, s + 1)
                    nc.scalar.copy(xT[:, hf, :], ps[:, 0, :]).then_inc(xT_ready, 1)
                    if not isinstance(s, int) or s >= 2:
                        act.wait_ge(nT_done, 4 * (s - 1))
                    for t in range(G):
                        act.wait_ge(h_done, 4 * s + t + 1)
                        nc.scalar.activation(g[:, hf, t, :], ps[:, 1 + t % 2, :], ACT.Gelu).then_inc(g_ready, 1)

                def back(s, hf):
                    act.wait_ge(y_done, s)
                    for k in range(HB):
                        act.wait_ge(nT_done, 4 * s + k + 1)
                        nc.scalar.activation(nT[:, k, :], ps[:, 3 + k, :], ACT.Identity, bias=ln_b[:, k:k + 1],
                                             scale=ln_w[:, k:k + 1]).then_inc(nT_ready, 1)

                front(0, 0)
                with act.Fori(0, STEPS // 2 - 1) as m:
                    for hf in range(2):
                        front(2 * m + hf + 1, 1 - hf)
                        back(2 * m + hf, hf)
                front(STEPS - 1, 1)
                back(STEPS - 2, 0)
                back(STEPS - 1, 1)

            @block.vector
            def _(dve):
                link = Chain(dve, chain, signals.links)
                dve.wait_ge(loaded, signals.loads)
                nc.vector.tensor_reduce(asum[:, 0:1], wf[:, :], AX.X, ALU.add, apply_absolute_value=True)
                nc.vector.tensor_reduce(asum[:, 1:2], wp[:, :, :].rearrange("p k n -> p (k n)"), AX.X, ALU.add,
                                        apply_absolute_value=True).then_inc(sums_ready, 1)
                dve.wait_ge(sums_done, 1)
                link(nc.vector.tensor_scalar(bound[:, :], ps[:, 0, 0:2], 1.0 / (FH * DM), GAMMA_EPS, ALU.mult, ALU.add))
                link(nc.vector.tensor_scalar(bound[:, :], bound[:, :], 0.5, None, ALU.mult))
                link(nc.vector.tensor_scalar(nbound[:, :], bound[:, :], -1.0, None, ALU.mult))
                for n, (w, w3) in enumerate(((wf[:, :], wf3[:, :]),
                                             (wp[:, :, :].rearrange("p k n -> p (k n)"), wp3[:, :, :].rearrange("p k n -> p (k n)")))):
                    link(nc.vector.tensor_scalar(low[:, :], w, nbound[:, n:n + 1], None, ALU.is_lt))
                    link(nc.vector.scalar_tensor_tensor(out=w3, in0=w, scalar=bound[:, n:n + 1], in1=low[:, :],
                                                        op0=ALU.is_gt, op1=ALU.subtract))
                nc.vector.memset(low[:, 0:1], 0.0).then_inc(w_ready, 1)

                def x_now(s):
                    return x_all[:, bass.ds(s * G, G), :]

                def fetch(s, hf):
                    if not isinstance(s, int) or s >= 2:
                        dve.wait_ge(xT_done, s - 1)
                    nc.vector.tensor_copy(xs[:, hf, :, :], x_now(s)).then_inc(xs_ready, 1)

                def front(s, hf, step):
                    dve.wait_ge(g_ready, 4 * s + 4)
                    layer_norm(nc.vector, step, ns, lambda t: g[:, hf, t, :], lambda t: g[:, hf, t, :], EPS_LN, FH, done=n_ready)

                def back(m, hf, step):
                    s = 2 * m + hf
                    dve.wait_ge(y_done, s + 1)
                    dve.wait_ge(stored[hf], 16 * m)
                    nc.vector.tensor_tensor(y[:, hf, :, :], ps[:, 7, :].rearrange("p (t n) -> p t n", t=G), x_now(s), ALU.add)\
                        .then_inc(y_read, 1)
                    dve.wait_ge(y_read, s + 1)
                    layer_norm(nc.vector, step, ns2, lambda t: y[:, hf, t, :], lambda t: y[:, hf, t, :], EPS_LN, DM, done=y_ready)

                fetch(0, 0)
                fetch(1, 1)
                front(0, 0, link)
                fetch(2, 0)
                front(1, 1, link)
                back(0, 0, link)
                fetch(3, 1)
                front(2, 0, link)
                back(0, 1, link)
                with dve.Fori(1, STEPS // 2 - 1) as m:
                    step = Chain(dve, chain, link.start + link.count, m - 1, MLP_LINKS)
                    for hf in range(2):
                        fetch(2 * m + hf + 2, hf)
                        front(2 * m + hf + 1, 1 - hf, step)
                        back(m, hf, step)
                    step.end()
                link = Chain(dve, chain, link.start + link.count + (STEPS // 2 - 2) * MLP_LINKS)
                front(STEPS - 1, 1, link)
                back(STEPS // 2 - 1, 0, link)
                back(STEPS // 2 - 1, 1, link)


MLP_LINKS = 2 * 2 * (NORM_LINKS - 1)

def build(nc, d, out):
    with ExitStack() as ctx:
        def sb(name, shape, dt=F32):
            return ctx.enter_context(nc.sbuf_tensor(name, shape, dt))

        x_all = sb("x_all", [P, TILES, DM])
        tri = sb("tri", [P, P])
        past = sb("past", [P, P])
        ones = sb("ones", [P, P])
        ident = sb("ident", [P, P])
        signals = Signals(nc, ctx)
        with nc.Block() as block:
            @block.vector
            def _(dve):
                nc.vector.memset(ones[:, :], 1.0).then_inc(signals.set_up, 1)
                dve.wait_ge(signals.set_up, 1)
        mamba(nc, signals, x_all, tri, past, ones, ident, d)
        with ExitStack() as layer:
            v_all = layer.enter_context(nc.sbuf_tensor("v_all", [P, BATCH * SLOTS, TPB, 32], F32))
            o_all = layer.enter_context(nc.sbuf_tensor("o_all", [P, BATCH * SLOTS, TPB, 32], F32))
            q_dram = nc.dram_tensor("q_parts", (BATCH * SLOTS, SPLITS, 32, SEQ), BF16).ap()
            k_dram = nc.dram_tensor("k_parts", (BATCH * SLOTS, SPLITS, 32, SEQ), BF16).ap()
            latent_attention(nc, signals, x_all, ident, d, v_all, o_all, q_dram, k_dram)
            experts(nc, signals, x_all, ident, d, o_all)
        flow_attention(nc, signals, x_all, ones, ident, d)
        ternary_mlp(nc, signals, x_all, ones, ident, d, out)


def layouts(inp):
    f = {}
    x = np.asarray(inp["L0_attn_hidden_states"]).reshape(TOK, DM)
    f["x"] = np.ascontiguousarray(x.reshape(TILES, P, DM).transpose(1, 0, 2))
    f["xT"] = np.ascontiguousarray(x.T)
    f["w_in"] = np.asarray(inp["L0_attn_W_in"])
    f["conv_w"] = np.ascontiguousarray(np.asarray(inp["L0_attn_conv_w"]).reshape(NBLK, P, TAPS).transpose(1, 0, 2))
    f["conv_b"] = np.ascontiguousarray(np.asarray(inp["L0_attn_conv_b"]).reshape(NBLK, P).T)
    f["dcol"] = np.ascontiguousarray(np.repeat(np.asarray(inp["L0_attn_D"]), HD).reshape(ZB, P).T)
    f["rms_w"] = np.ascontiguousarray(np.asarray(inp["L0_attn_rms_w"]).reshape(ZB, P).T)
    f["w_out"] = np.ascontiguousarray(np.asarray(inp["L0_attn_W_out"]).reshape(ZB, P, DM).transpose(1, 0, 2))
    f["dt_bias"] = np.asarray(inp["L0_attn_dt_bias"])
    f["a_log"] = np.asarray(inp["L0_attn_A_log"])
    f["m_ln_g"] = np.asarray(inp["L0_attn_ln_g"])
    f["m_ln_b"] = np.asarray(inp["L0_attn_ln_b"])
    row, col = np.arange(P)[:, None], np.arange(P)[None, :]
    f["tri"] = (row <= col).astype(np.float32)
    f["past"] = (row > col).astype(np.float32)
    f["ident"] = np.eye(P, dtype=np.float32)
    f["norm1_w"] = np.asarray(inp["L0_ffn_norm1_w"])[:, None]
    swap = (np.arange(DM) // AD) * AD + (np.arange(DM) % AD + AD // 2) % AD
    wq = np.asarray(inp["L0_ffn_Wq"]).T
    f["wq"] = np.ascontiguousarray(np.stack([wq, wq[:, swap]], 1))
    f["wdkv"] = np.ascontiguousarray(np.asarray(inp["L0_ffn_Wdkv"]).T)
    wuk = np.asarray(inp["L0_ffn_Wuk"]).T
    f["wuk"] = np.ascontiguousarray(np.stack([wuk, wuk[:, swap]], 1))
    f["wuv"] = np.ascontiguousarray(np.asarray(inp["L0_ffn_Wuv"]).T)
    f["lat_g"] = np.asarray(inp["L0_ffn_ln_g"])[:, None]
    f["lat_b"] = np.asarray(inp["L0_ffn_ln_b"])[:, None]
    half = AD // 2
    inv_freq = (1.0 / 10000.0 ** (np.arange(half, dtype=np.float32) / half)).astype(np.float32)
    angle = (np.arange(SEQ, dtype=np.float32)[:, None] * inv_freq[None, :]).astype(np.float32)
    sign = np.where(np.arange(AD) < half, -1.0, 1.0)[:, None]
    f["cos"] = np.tile(np.cos(angle).T, (2 * AH, 1)).astype(np.float32)
    f["sin"] = np.tile(np.tile(np.sin(angle).T, (2, 1)) * sign, (AH, 1)).astype(np.float32)
    f["norm2_w"] = np.asarray(inp["L0_ffn_norm2_w"])[:, None]
    f["moe_wo"] = np.ascontiguousarray(np.asarray(inp["L0_ffn_Wo"]).T)
    f["gate_w"] = np.ascontiguousarray(np.asarray(inp["L0_ffn_gate_w"]).T)
    f["gate_b"] = np.asarray(inp["L0_ffn_gate_b"])
    f["moe_w1"] = np.ascontiguousarray(np.asarray(inp["L0_ffn_W1"]).transpose(2, 0, 1))
    f["moe_b1"] = np.ascontiguousarray(np.asarray(inp["L0_ffn_b1"]).reshape(NE, HID // P, P).transpose(2, 0, 1))
    f["moe_w2"] = np.ascontiguousarray(
        np.asarray(inp["L0_ffn_W2"]).transpose(0, 2, 1).reshape(NE, HID // P, P, DM).transpose(2, 0, 1, 3))
    b2 = np.zeros((G, NE, G, DM), np.float32)
    for t in range(G):
        b2[t, :, t, :] = np.asarray(inp["L0_ffn_b2"])
    f["moe_b2"] = b2.reshape(G * NE, G * DM)
    f["order"] = np.tile(np.arange(NE, 0, -1, dtype=np.float32), (P, 1))
    for n, key in (("fl_wq", "Wq"), ("fl_wk", "Wk"), ("fl_wv", "Wv"), ("fl_wo", "Wo")):
        f[n] = np.asarray(inp["L1_attn_" + key])
    f["fl_bq"] = np.asarray(inp["L1_attn_bq"])[:, None]
    f["fl_bk"] = np.asarray(inp["L1_attn_bk"])[:, None]
    f["fl_bv"] = np.asarray(inp["L1_attn_bv"])
    f["fl_bo"] = np.asarray(inp["L1_attn_bo"])
    f["head"] = (row // AD == np.arange(AH)[None, :]).astype(np.float32)
    f["same"] = (row // AD == col // AD).astype(np.float32)
    f["wf"] = np.ascontiguousarray(np.asarray(inp["L1_ffn_W_fc"]).T)
    f["wp"] = np.ascontiguousarray(np.asarray(inp["L1_ffn_W_proj"]).T.reshape(FH // P, P, DM).transpose(1, 0, 2))
    f["tm_ln_w"] = np.ascontiguousarray(np.asarray(inp["L1_ffn_ln_w"]).reshape(FH // P, P).T)
    f["tm_ln_b"] = np.ascontiguousarray(np.asarray(inp["L1_ffn_ln_b"]).reshape(FH // P, P).T)
    bf16 = mybir.dt.np(BF16)
    f["identb"] = np.eye(P).astype(bf16)
    f["mask_q"] = np.where(col > row, MASKED, 0.0).astype(bf16)
    f["mask_k"] = np.where(row > col, MASKED, 0.0).astype(bf16)
    f["pad"] = np.repeat((np.arange(STACK - SROWS) >= SHIFT_ROW - SROWS), 4 * SEQ).reshape(-1, 4, SEQ).astype(bf16)
    return f


def kernel(**inputs):
    import concourse.bacc as bacc
    from concourse.bass_utils import run_bass_kernel_spmd

    nc = bacc.Bacc("TRN2", target_bir_lowering=False, num_devices=1)
    arrays = layouts(inputs)
    d = {n: nc.dram_tensor("in_" + n, a.shape, mybir.dt.from_np(a.dtype), kind="ExternalInput").ap() for n, a in arrays.items()}
    out = nc.dram_tensor("out", (P, TILES, DM), F32, kind="ExternalOutput").ap()
    build(nc, d, out)
    res = run_bass_kernel_spmd(nc, [{"in_" + n: a for n, a in arrays.items()}], core_ids=[0]).results[0]["out"]
    return res.transpose(1, 0, 2).reshape(BATCH, SEQ, DM)
```

```python
from contextlib import ExitStack

import numpy as np
import concourse.bass as bass
from concourse import mybir

F32 = mybir.dt.float32
BF16 = mybir.dt.bfloat16
I32 = mybir.dt.int32
ACT = mybir.ActivationFunctionType
ALU = mybir.AluOpType
AX = mybir.AxisListType

P = 128
BATCH, SEQ, DM = 4, 1024, 128
TOK = BATCH * SEQ
TILES = TOK // P
TPB = SEQ // P
G = 4
W = G * P

DIN, NST, NH, HD, TAPS = 256, 128, 4, 64, 4
NBLK = (DIN + 2 * NST) // P
ZB = DIN // P
EPS_RMS, EPS_LN = 1e-5, 1e-5

AH, AD, LAT, NE, HID = 16, 8, 64, 4, 512
EPS_RMS2 = 1e-6
SPLITS = 3
SROWS = SPLITS * SPLITS * AD
SHIFT_ROW = 96
MASKED = -1e30

FLOW_EPS = 1e-6
FH = 512
GAMMA_EPS = 1e-6

FREE = 2
MAGIC = 1597463007.0


class Chain:

    def __init__(self, eng, sem, start=0, step=0, per=0):
        self.eng, self.sem, self.start, self.before, self.per = eng, sem, start, start + step * per, per
        self.count = 0

    def __call__(self, instruction):
        self.count += 1
        instruction.then_inc(self.sem, 1)
        self.eng.wait_ge(self.sem, self.before + self.count)

    def end(self):
        assert self.count == self.per, (self.count, self.per)


class Signals:

    def __init__(self, nc, ctx):
        self.nc, self.ctx = nc, ctx
        self.loaded, self.chain = self.new("loaded"), self.new("chain")
        self.loads = self.links = 0
        self.set_up = self.new("set_up")

    def new(self, name):
        return self.ctx.enter_context(self.nc.semaphore(name))


def start_free(eng, *sems):
    for s in sems:
        eng.sem_inc(s, FREE)


def inverse_root(eng, link, v, y, t, h):
    eng.tensor_scalar(h, v, -0.5, None, ALU.mult)
    link(eng.tensor_scalar(y.bitcast(I32), v.bitcast(I32), -0.5, MAGIC, ALU.mult, ALU.add))
    for _ in range(3):
        link(eng.tensor_tensor(t, y, y, ALU.mult))
        link(eng.tensor_tensor(t, t, h, ALU.mult))
        link(eng.scalar_tensor_tensor(out=y, in0=t, scalar=1.5, in1=y, op0=ALU.add, op1=ALU.mult))


ROOT_LINKS = 10


class NormScratch:

    def __init__(self, sb, name, n=G):
        self.st = sb(name + "_stats", [P, n, 6], F32)
        self.sum = sb(name + "_sum", [P, n], F32)
        self.dif = sb(name + "_dif", [P, n], F32)
        self.m2 = sb(name + "_m2", [P, n], F32)
        self.v = sb(name + "_var", [P, n], F32)
        self.y = sb(name + "_rstd", [P, n], F32)
        self.t = sb(name + "_t", [P, n], F32)
        self.h = sb(name + "_h", [P, n], F32)
        self.b = sb(name + "_shift", [P, n], F32)


NORM_LINKS = 4 + ROOT_LINKS + 2


def layer_norm(eng, link, s, src, dst, eps, width, n=G, done=None):
    for k in range(n):
        last = eng.bn_stats(s.st[:, k, :], src(k))
    link(last)
    norm_scales(eng, link, s, eps, width)
    for k in range(n):
        last = eng.tensor_scalar(dst(k), src(k), s.y[:, k:k + 1], s.b[:, k:k + 1], ALU.mult, ALU.add)
    if done is None:
        link(last)
    else:
        last.then_inc(done, 1)


def norm_scales(eng, link, s, eps, width):
    eng.tensor_tensor(s.sum[:, :], s.st[:, :, 1], s.st[:, :, 4], ALU.add)
    eng.tensor_tensor(s.dif[:, :], s.st[:, :, 1], s.st[:, :, 4], ALU.subtract)
    link(eng.scalar_tensor_tensor(out=s.m2[:, :], in0=s.st[:, :, 2], scalar=eps * width, in1=s.st[:, :, 5],
                                  op0=ALU.add, op1=ALU.add))
    link(eng.scalar_tensor_tensor(out=s.dif[:, :], in0=s.dif[:, :], scalar=0.25, in1=s.dif[:, :],
                                  op0=ALU.mult, op1=ALU.mult))
    link(eng.scalar_tensor_tensor(out=s.v[:, :], in0=s.m2[:, :], scalar=1.0 / width, in1=s.dif[:, :],
                                  op0=ALU.mult, op1=ALU.add))
    inverse_root(eng, link, s.v[:, :], s.y[:, :], s.t[:, :], s.h[:, :])
    link(eng.scalar_tensor_tensor(out=s.b[:, :], in0=s.sum[:, :], scalar=-0.5, in1=s.y[:, :],
                                  op0=ALU.mult, op1=ALU.mult))


def mamba(nc, signals, x_all, tri, past, ones, ident, d):
    with ExitStack() as ctx:
        def sb(name, shape, dt=F32):
            return ctx.enter_context(nc.sbuf_tensor(name, shape, dt))

        def sem(name):
            return signals.new(name)

        ps = ctx.enter_context(nc.psum_tensor("mamba_psum", [P, 8, 512], F32))
        proj = [ps[:, 0, :], ps[:, 1, :]]
        outp = ps[:, 0, :].rearrange("p (b n) -> p b n", b=G)
        ssp = ps[:, 1, 0:G]
        decp = ps[:, 2:4, :]
        xtokp = ps[:, 4:6, :].rearrange("p k (b n) -> p (k b) n", n=DIN)
        yp = ps[:, 4:6, :].rearrange("p k (b l) -> p k b l", b=G)
        btokp = ps[:, 6, :]
        scorep = ps[:, 7, :]
        newp = ps[:, 6:8, :].rearrange("p k (b n) -> p (k b) n", n=DIN)

        xT = sb("xT", [P, TOK])
        xTb = xT[:, :].rearrange("p (b l) -> p b l", b=BATCH)
        w_in = sb("w_in", [P, 2 * DIN + 2 * NST + NH])
        conv_w = sb("conv_w", [P, NBLK, TAPS])
        conv_b = sb("conv_b", [P, NBLK])
        dcol = sb("dcol", [P, ZB])
        rms_w = sb("rms_w", [P, ZB])
        w_out = sb("w_out", [P, ZB, DM])
        dt_bias = sb("dt_bias", [P, NH])
        a_log = sb("a_log", [P, NH])
        ln_g = sb("ln_g", [P, DM])
        ln_b = sb("ln_b", [P, DM])

        u = sb("u", [P, TILES, NH])
        au = sb("au", [P, TILES, NH])
        dt = sb("dt", [P, TILES, NH])
        ada = sb("ada", [P, TILES, NH])
        carry = sb("carry", [P, 2, TILES, NH])

        pre = sb("pre", [P, NBLK, BATCH, TAPS - 1 + P])
        cv = sb("cv", [P, NBLK, W])
        xbc = sb("xbc", [P, 2, NBLK, W])
        zs = sb("zs", [P, 2, ZB, W])
        ta = sb("ta", [P, 2, NH, P])
        le = sb("le", [P, 2, 2, NH, P])
        mm = sb("mm", [P, 2, NH, P])
        ce = sb("ce", [P, 2, NH, P])
        xdt = sb("xdt", [P, BATCH, DIN])
        xdd = sb("xdd", [P, BATCH, DIN])
        btok = sb("btok", [P, BATCH, NST])
        sm = sb("sm", [P, BATCH, P])
        state = sb("state", [P, BATCH, DIN])
        yg = sb("yg", [P, ZB, W])
        sq = sb("sq", [P, ZB, W])
        xb = sb("xb", [P, TILES, DM])
        h = sb("h", [P, TILES, DM])
        square = sb("square", [P, TILES])
        r = sb("r", [P, TILES])
        rv = sb("rv", [P, TILES])
        rt = sb("rt", [P, TILES])
        rh = sb("rh", [P, TILES])
        nmean = sb("nmean", [P, TILES])
        ns = NormScratch(sb, "mnorm", TILES)

        loaded, chain = signals.loaded, signals.chain
        first_loaded, x_loaded = sem("first_loaded"), sem("x_loaded")
        dt_raw = sem("dt_raw")
        e_abs = sem("e_abs")
        dt_act = sem("dt_act")
        dt_ready = sem("dt_ready")
        carry_sum = sem("carry_sum")
        carry_ready = sem("carry_ready")
        proj_done = sem("proj_done")
        proj_read = sem("proj_read")
        tail_kept = sem("tail_kept")
        conv_done = sem("conv_done")
        xbc_ready = sem("xbc_ready")
        z_ready = sem("z_ready")
        ta_ready = sem("ta_ready")
        dec_done = sem("dec_done")
        dec_exp = sem("dec_exp")
        mix_ready = sem("mix_ready")
        xtok_done = sem("xtok_done")
        btok_done = sem("btok_done")
        score_done = sem("score_done")
        xdt_ready = sem("xdt_ready")
        xdd_ready = sem("xdd_ready")
        btok_ready = sem("btok_ready")
        sm_ready = sem("sm_ready")
        y_done = sem("y_done")
        new_done = sem("new_done")
        state_ready = sem("state_ready")
        yg_ready = sem("yg_ready")
        sq_ready = sem("sq_ready")
        ss_done = sem("ss_done")
        out_done = sem("out_done")
        out_read = sem("out_read")
        xb_ready = sem("xb_ready")
        scales_ready = sem("scales_ready")
        act_chain = sem("mamba_act_chain")


        with nc.Block() as block:
            @block.sync
            def _(sp):
                sp.dma_start(w_in[:, :], d["w_in"]).then_inc(first_loaded, 16)
                sp.dma_start(xT[:, :], d["xT"]).then_inc(first_loaded, 16)
                sp.wait_ge(first_loaded, 32)
                sp.dma_start(x_all[:, :, :], d["x"]).then_inc(x_loaded, 16)

                start_free(sp, dec_done, dec_exp, mix_ready, new_done, out_done, out_read, ss_done, xbc_ready,
                           xdd_ready, y_done, yg_ready)

            ALL = signals.loads = 16 * 12

            @block.tensor
            def _(pe):
                pe.wait_ge(first_loaded, 32)
                for t in range(TILES):
                    last = nc.tensor.matmul(ps[:, 4, NH * t:NH * t + NH], xT[:, t * P:(t + 1) * P],
                                            w_in[:, 2 * DIN + 2 * NST:], start=True, stop=True)
                last.then_inc(dt_raw, 1)
                pe.wait_ge(dt_ready, 1)
                pe.wait_ge(loaded, ALL)
                flat = ada[:, :, :].rearrange("p t h -> p (t h)")
                nc.tensor.matmul(ps[:, 5, 0:P], past[:, :], flat, start=True, stop=True)
                nc.tensor.matmul(ps[:, 5, P:2 * P], ones[:, :], flat, start=True, stop=True).then_inc(carry_sum, 1)

                def project(i, n):
                    col = DIN + n * P if n < NBLK else (n - NBLK) * P
                    if not (isinstance(i, int) and i == 0 and n < 2):
                        pe.wait_ge(proj_read, 6 * i + n - 1)
                    if n < 2 and not isinstance(i, int):
                        pe.wait_ge(out_read, FREE + i - 1)
                    elif n < 2 and i >= 2:
                        pe.wait_ge(out_read, FREE + i - 1)
                    nc.tensor.matmul(proj[n % 2], w_in[:, col:col + P], xTb[:, :, bass.ds(i * P, P)],
                                     start=True, stop=True).then_inc(proj_done, 1)

                def decays(i, b):
                    pe.wait_ge(ta_ready, 4 * i + b + 1)
                    pe.wait_ge(dec_exp, FREE + 4 * i + b)
                    rhs = ta[:, b % 2, :, :]
                    nc.tensor.matmul(decp[:, 0, :], past[:, :], rhs, start=True, stop=True)
                    nc.tensor.matmul(decp[:, 1, :], ones[:, :], rhs, start=True, stop=True).then_inc(dec_done, 1)

                def step(i, p, more=True):
                    pe.wait_ge(yg_ready, FREE + i)
                    for k in range(ZB):
                        pe.wait_ge(xbc_ready, FREE + 4 * i + k + 1)
                        for b in range(BATCH):
                            last = nc.tensor.transpose(xtokp[:, b, k * P:(k + 1) * P], xbc[:, p, k, b * P:(b + 1) * P],
                                                       ident[:, :])
                    last.then_inc(xtok_done, 1)
                    pe.wait_ge(state_ready, i + 1)
                    pe.wait_ge(xbc_ready, FREE + 4 * i + 3)
                    for b in range(BATCH):
                        last = nc.tensor.transpose(btokp[:, b * P:(b + 1) * P], xbc[:, p, 2, b * P:(b + 1) * P],
                                                   ident[:, :])
                    last.then_inc(btok_done, 1)
                    pe.wait_ge(xbc_ready, FREE + 4 * i + 4)
                    for b in range(BATCH):
                        last = nc.tensor.matmul(scorep[:, b * P:(b + 1) * P], xbc[:, p, 2, b * P:(b + 1) * P],
                                                xbc[:, p, 3, b * P:(b + 1) * P], start=True, stop=True)
                    last.then_inc(score_done, 1)
                    for b in range(BATCH):
                        if b + 1 < BATCH:
                            decays(i, b + 1)
                        if more:
                            project(i + 1, b)
                        if b == 0:
                            pe.wait_ge(xdt_ready, i + 1)
                        pe.wait_ge(mix_ready, FREE + 4 * i + b + 1)
                        for hh in range(NH):
                            out = yp[HD * (hh % 2):HD * (hh % 2) + HD, hh // 2, b, :]
                            nc.tensor.matmul(out, xdt[:, b, hh * HD:(hh + 1) * HD], mm[:, b % 2, hh, :],
                                             start=True, stop=False)
                            last = nc.tensor.matmul(out, state[:, b, hh * HD:(hh + 1) * HD], ce[:, b % 2, hh, :],
                                                    start=False, stop=True)
                        last.then_inc(y_done, 1)
                    pe.wait_ge(btok_ready, i + 1)
                    pe.wait_ge(sm_ready, i + 1)
                    pe.wait_ge(xdd_ready, FREE + i + 1)
                    for b in range(BATCH):
                        last = nc.tensor.matmul(newp[:, b, :], btok[:, b, :], xdd[:, b, :], start=True, stop=True)
                    last.then_inc(new_done, 1)
                    if more:
                        for n in range(NBLK, NBLK + ZB):
                            project(i + 1, n)
                        decays(i + 1, 0)
                    pe.wait_ge(sq_ready, 2 * i + 2)
                    pe.wait_ge(proj_read, 6 * i + (12 if more else 6))
                    for b in range(BATCH):
                        for k in range(ZB):
                            last = nc.tensor.matmul(ssp[:, b:b + 1], sq[:, k, b * P:(b + 1) * P], ones[:, 0:1],
                                                    start=(k == 0), stop=(k == ZB - 1))
                    last.then_inc(ss_done, 1)
                    for b in range(BATCH):
                        for k in range(ZB):
                            last = nc.tensor.matmul(outp[:, b, :], yg[:, k, b * P:(b + 1) * P], w_out[:, k, :],
                                                    start=(k == 0), stop=(k == ZB - 1))
                    last.then_inc(out_done, 1)

                for n in range(NBLK + ZB):
                    project(0, n)
                decays(0, 0)
                with pe.Fori(0, TPB // 2 - 1) as m:
                    for p in range(2):
                        step(2 * m + p, p)
                step(TPB - 2, 0)
                step(TPB - 1, 1, more=False)

            @block.scalar
            def _(act):
                for dst, src in ((dt_bias, d["dt_bias"]), (a_log, d["a_log"]), (ln_g, d["m_ln_g"]),
                                 (ln_b, d["m_ln_b"])):
                    act.dma_start(dst[:, :], src.partition_broadcast(P)).then_inc(loaded, 16)
                for dst, src in ((tri[:, :], d["tri"]), (past[:, :], d["past"]), (ident[:, :], d["ident"]),
                                 (conv_w[:, :, :], d["conv_w"]), (conv_b[:, :], d["conv_b"]),
                                 (dcol[:, :], d["dcol"]), (rms_w[:, :], d["rms_w"]),
                                 (w_out[:, :, :], d["w_out"])):
                    act.dma_start(dst, src).then_inc(loaded, 16)
                act.wait_ge(loaded, ALL)
                nc.scalar.activation(a_log[:, :], a_log[:, :], ACT.Exp).then_inc(dt_act, 1)
                act.wait_ge(e_abs, 1)
                nc.scalar.activation(au[:, :, :], au[:, :, :], ACT.Exp, scale=-1.0).then_inc(act_chain, 1)
                act.wait_ge(act_chain, 1)
                nc.scalar.activation(au[:, :, :], au[:, :, :], ACT.Ln, bias=ones[:, 0:1]).then_inc(dt_act, 1)
                act.wait_ge(carry_sum, 1)
                nc.scalar.activation(carry[:, :, :, :].rearrange("p a t h -> p (a t h)"), ps[:, 5, 0:2 * P],
                                     ACT.Exp).then_inc(carry_ready, 1)

                def copy_in(i, n):
                    if n == 0:
                        act.wait_ge(tail_kept, i + 1)
                    act.wait_ge(proj_done, 6 * i + n + 1)
                    nc.scalar.copy(pre[:, n, :, TAPS - 1:], proj[n % 2].rearrange("p (b l) -> p b l", b=BATCH))\
                        .then_inc(proj_read, 1)

                def gate(i, p):
                    for n in range(ZB):
                        act.wait_ge(proj_done, 6 * i + NBLK + n + 1)
                        nc.scalar.activation(zs[:, p, n, :], proj[(NBLK + n) % 2], ACT.Silu).then_inc(proj_read, 1)

                def silu(i, p, n):
                    act.wait_ge(conv_done, 4 * i + n + 1)
                    nc.scalar.activation(xbc[:, p, n, :], cv[:, n, :], ACT.Silu, bias=conv_b[:, n:n + 1])\
                        .then_inc(xbc_ready, 1)

                def keep_tail():
                    nc.scalar.copy(pre[:, :, :, 0:TAPS - 1], pre[:, :, :, P:P + TAPS - 1]).then_inc(tail_kept, 1)

                def decay(i, b):
                    act.wait_ge(dec_done, FREE + 4 * i + b + 1)
                    act.wait_ge(mix_ready, FREE + 4 * i + max(b - 1, 0))
                    nc.scalar.activation(le[:, b % 2, :, :, :].rearrange("p k h l -> p k (h l)"), decp, ACT.Exp)\
                        .then_inc(dec_exp, 1)

                def step(i, p, more=True):
                    decay(i, 0)
                    act.wait_ge(btok_done, i + 1)
                    act.wait_ge(new_done, FREE + i)
                    nc.scalar.copy(btok[:, :, :].rearrange("p b n -> p (b n)"), btokp).then_inc(btok_ready, 1)
                    for b in range(1, BATCH):
                        if more:
                            copy_in(i + 1, b - 1)
                        decay(i, b)
                    if more:
                        copy_in(i + 1, BATCH - 1)
                        act.wait_ge(yg_ready, FREE + i)
                        gate(i + 1, 1 - p)
                        for n in (0, 1):
                            silu(i + 1, 1 - p, n)
                    act.wait_ge(yg_ready, FREE + i + 1)
                    act.wait_ge(ss_done, FREE + i)
                    for k in range(ZB):
                        nc.scalar.activation(sq[:, k, :], yg[:, k, :], ACT.Square).then_inc(sq_ready, 1)
                    if more:
                        for n in (2, 3):
                            silu(i + 1, 1 - p, n)
                        keep_tail()
                    act.wait_ge(ss_done, FREE + i + 1)
                    nc.scalar.copy(square[:, :].rearrange("p (b c) -> p b c", b=BATCH)[:, :, bass.ds(i, 1)]
                                   .rearrange("p b c -> p (b c)"), ssp)
                    act.wait_ge(out_done, FREE + i + 1)
                    nc.scalar.copy(h[:, :, :].rearrange("p (b c) n -> p b (c n)", b=BATCH)[:, :, bass.ds(i * DM, DM)], outp)\
                        .then_inc(out_read, 1)

                for n in range(NBLK):
                    copy_in(0, n)
                gate(0, 0)
                for n in range(NBLK):
                    silu(0, 0, n)
                keep_tail()
                with act.Fori(0, TPB // 2 - 1) as m:
                    for p in range(2):
                        step(2 * m + p, p)
                step(TPB - 2, 0)
                step(TPB - 1, 1, more=False)
                act.wait_ge(scales_ready, 1)
                for k in range(TILES // 2, TILES):
                    nc.scalar.activation(x_all[:, k, :], h[:, k, :], ACT.Identity, bias=ns.b[:, k:k + 1],
                                         scale=ns.y[:, k:k + 1])

            @block.gpsimd
            def _(pool):
                nc.gpsimd.memset(pre[:, :, :, 0:TAPS - 1], 0.0).then_inc(tail_kept, 1)
                pool.wait_ge(loaded, ALL)
                pool.wait_ge(x_loaded, 16)
                nc.gpsimd.tensor_tensor(xb[:, :, :], x_all[:, :, :], ln_b[:, :].unsqueeze(1).to_broadcast([P, TILES, DM]),
                                        ALU.add).then_inc(xb_ready, 1)
                pool.wait_ge(dt_ready, 1)
                pool.wait_ge(carry_ready, 1)
                with pool.Fori(0, TPB) as i:
                    def spread(b):
                        pool.wait_ge(dec_done, FREE + 4 * i + max(b - 1, 0))
                        nc.gpsimd.tensor_tensor(
                            ta[:, b % 2, :, :], tri[:, :].unsqueeze(1).to_broadcast([P, NH, P]),
                            ada[:, bass.ds(i + b * TPB, 1), :].rearrange("p t h -> p (t h)").unsqueeze(2)
                            .to_broadcast([P, NH, P]), ALU.mult).then_inc(ta_ready, 1)

                    spread(0)
                    spread(1)
                    pool.wait_ge(xdt_ready, i + 1)
                    pool.wait_ge(new_done, FREE + i)
                    for b in range(BATCH):
                        last = nc.gpsimd.tensor_tensor(
                            xdd[:, b, :].rearrange("p (h n) -> p h n", h=NH), xdt[:, b, :].rearrange("p (h n) -> p h n", h=NH),
                            carry[:, 0, bass.ds(i + b * TPB, 1), :].rearrange("p t h -> p (t h)").unsqueeze(2)
                            .to_broadcast([P, NH, HD]), ALU.mult)
                    last.then_inc(xdd_ready, 1)
                    spread(2)
                    spread(3)

            @block.vector
            def _(dve):
                dve.wait_ge(loaded, ALL)
                nc.vector.memset(state[:, :, :], 0.0).then_inc(state_ready, 1)
                link = Chain(dve, chain)
                dve.wait_ge(dt_raw, 1)
                link(nc.vector.tensor_tensor(u[:, :, :], ps[:, 4, 0:TILES * NH].rearrange("p (t h) -> p t h", h=NH),
                                             dt_bias[:, :].unsqueeze(1).to_broadcast([P, TILES, NH]), ALU.add))
                nc.vector.scalar_tensor_tensor(out=au[:, :, :], in0=u[:, :, :], scalar=-1.0, in1=u[:, :, :],
                                               op0=ALU.mult, op1=ALU.max).then_inc(e_abs, 1)
                link(nc.vector.tensor_tensor(w_out[:, :, :], w_out[:, :, :],
                                             rms_w[:, :].unsqueeze(2).to_broadcast([P, ZB, DM]), ALU.mult))
                dve.wait_ge(dt_act, 2)
                link(nc.vector.scalar_tensor_tensor(out=dt[:, :, :], in0=u[:, :, :], scalar=0.0, in1=au[:, :, :],
                                                    op0=ALU.max, op1=ALU.add))
                nc.vector.scalar_tensor_tensor(out=ada[:, :, :], in0=dt[:, :, :], scalar=-1.0,
                                               in1=a_log[:, :].unsqueeze(1).to_broadcast([P, TILES, NH]),
                                               op0=ALU.mult, op1=ALU.mult).then_inc(dt_ready, 1)
                dve.wait_ge(carry_ready, 1)

                def convolve(i, link):
                    dve.wait_ge(tail_kept, i + 1)
                    dve.wait_ge(xbc_ready, FREE + 4 * i)
                    for pair in (0, 2):
                        for tap in range(TAPS):
                            for n in (pair, pair + 1):
                                o = cv[:, n, :].rearrange("p (b l) -> p b l", b=BATCH)
                                src = pre[:, n, :, tap:tap + P]
                                w = conv_w[:, n, tap:tap + 1]
                                if tap == 0:
                                    dve.wait_ge(proj_read, 6 * i + n + 1)
                                    op = nc.vector.tensor_scalar(o, src, w, None, ALU.mult)
                                else:
                                    op = nc.vector.scalar_tensor_tensor(out=o, in0=src, scalar=w, in1=o,
                                                                        op0=ALU.mult, op1=ALU.add)
                                if tap == TAPS - 1:
                                    op.then_inc(conv_done, 1)
                                elif n == pair + 1:
                                    link(op)
                            yield

                def step(i, p, link, more=True):
                    dve.wait_ge(xtok_done, i + 1)
                    dve.wait_ge(y_done, FREE + 4 * i)
                    dve.wait_ge(xdd_ready, FREE + i)
                    for b in range(BATCH):
                        last = nc.vector.tensor_tensor(
                            xdt[:, b, :].rearrange("p (h n) -> p h n", h=NH), xtokp[:, b, :].rearrange("p (h n) -> p h n", h=NH),
                            dt[:, bass.ds(i + b * TPB, 1), :].rearrange("p t h -> p (t h)").unsqueeze(2)
                            .to_broadcast([P, NH, HD]), ALU.mult)
                    last.then_inc(xdt_ready, 1)
                    dve.wait_ge(score_done, i + 1)
                    nc.vector.tensor_tensor(sm[:, :, :], scorep.rearrange("p (b l) -> p b l", b=BATCH),
                                            tri[:, :].unsqueeze(1).to_broadcast([P, BATCH, P]), ALU.mult)\
                        .then_inc(sm_ready, 1)
                    dve.wait_ge(sm_ready, i + 1)
                    ahead = convolve(i + 1, link) if more else iter(())
                    for b in range(BATCH):
                        dve.wait_ge(dec_exp, FREE + 4 * i + b + 1)
                        dve.wait_ge(y_done, FREE + 4 * i + max(b - 1, 0))
                        nc.vector.tensor_tensor(mm[:, b % 2, :, :], le[:, b % 2, 0, :, :],
                                                sm[:, b, :].unsqueeze(1).to_broadcast([P, NH, P]), ALU.mult)
                        nc.vector.tensor_tensor(ce[:, b % 2, :, :], le[:, b % 2, 1, :, :],
                                                xbc[:, p, 3, b * P:(b + 1) * P].unsqueeze(1).to_broadcast([P, NH, P]),
                                                ALU.mult).then_inc(mix_ready, 1)
                        for _ in range(CONV_AT[b]):
                            next(ahead, None)
                    dve.wait_ge(y_done, FREE + 4 * i + 4)
                    dve.wait_ge(out_done, FREE + i)
                    for k in range(ZB):
                        last = nc.vector.scalar_tensor_tensor(
                            out=yg[:, k, :], in0=xbc[:, p, k, :], scalar=dcol[:, k:k + 1],
                            in1=yp[:, k, :, :].rearrange("p b l -> p (b l)"), op0=ALU.mult, op1=ALU.add)
                    link(last)
                    nc.vector.tensor_tensor(yg[:, :, :], yg[:, :, :], zs[:, p, :, :], ALU.mult).then_inc(yg_ready, 1)
                    dve.wait_ge(new_done, FREE + i + 1)
                    for b in range(BATCH):
                        last = nc.vector.tensor_tensor(
                            state[:, b, :].rearrange("p (h n) -> p h n", h=NH), state[:, b, :].rearrange("p (h n) -> p h n", h=NH),
                            carry[:, 1, bass.ds(i + b * TPB, 1), :].rearrange("p t h -> p (t h)").unsqueeze(2)
                            .to_broadcast([P, NH, HD]), ALU.mult)
                    link(last)
                    nc.vector.tensor_tensor(state[:, :, :], state[:, :, :], newp, ALU.add).then_inc(state_ready, 1)
                    for _ in ahead:
                        pass

                for _ in convolve(0, link):
                    pass
                with dve.Fori(0, TPB // 2 - 1) as m:
                    looped = Chain(dve, chain, link.count, m, 2 * MAMBA_LINKS)
                    for p in range(2):
                        step(2 * m + p, p, looped)
                    looped.end()
                link = Chain(dve, chain, link.count + (TPB // 2 - 1) * 2 * MAMBA_LINKS)
                step(TPB - 2, 0, link)
                step(TPB - 1, 1, link, more=False)

                every = range(TILES)
                dve.wait_ge(x_loaded, 16)
                dve.wait_ge(out_read, FREE + TPB)
                link(nc.vector.tensor_scalar(rv[:, :], square[:, :], 1.0 / DIN, EPS_RMS, ALU.mult, ALU.add))
                inverse_root(nc.vector, link, rv[:, :], r[:, :], rt[:, :], rh[:, :])
                for k in every:
                    last = nc.vector.scalar_tensor_tensor(out=h[:, k, :], in0=h[:, k, :], scalar=r[:, k:k + 1],
                                                          in1=x_all[:, k, :], op0=ALU.mult, op1=ALU.add)
                link(last)
                for k in every:
                    last = nc.vector.bn_stats(ns.st[:, k, :], h[:, k, :])
                link(last)
                norm_scales(nc.vector, link, ns, EPS_LN, DM)
                link(nc.vector.tensor_scalar(nmean[:, :], ns.sum[:, :], -0.5, None, ALU.mult))
                dve.wait_ge(xb_ready, 1)
                for k in every:
                    last = nc.vector.scalar_tensor_tensor(out=h[:, k, :], in0=h[:, k, :], scalar=nmean[:, k:k + 1],
                                                          in1=ln_g[:, :], op0=ALU.add, op1=ALU.mult)
                link(last)
                for k in every:
                    last = nc.vector.scalar_tensor_tensor(out=h[:, k, :], in0=h[:, k, :], scalar=ns.y[:, k:k + 1],
                                                          in1=xb[:, k, :], op0=ALU.mult, op1=ALU.add)
                link(last)
                for k in every:
                    last = nc.vector.bn_stats(ns.st[:, k, :], h[:, k, :])
                link(last)
                norm_scales(nc.vector, link, ns, EPS_LN, DM)
                nc.vector.memset(nmean[:, 0:1], 0.0).then_inc(scales_ready, 1)
                for k in range(TILES // 2):
                    nc.vector.tensor_scalar(x_all[:, k, :], h[:, k, :], ns.y[:, k:k + 1], ns.b[:, k:k + 1],
                                            ALU.mult, ALU.add)
                signals.links = link.start + link.count


MAMBA_LINKS = 2 * (TAPS - 1) + 2
CONV_AT = (0, 1, 2, 2)

def latent_attention(nc, signals, x_all, ident, d, v_all, o_all, q_dram, k_dram):
    with ExitStack() as ctx:
        def sb(name, shape, dt=F32):
            return ctx.enter_context(nc.sbuf_tensor(name, shape, dt))

        def sem(name):
            return signals.new(name)

        ps = ctx.enter_context(nc.psum_tensor("attn_psum", [P, 8, 512], F32))

        norm1_w = sb("norm1_w", [P, 1])
        wq = sb("wq", [P, 2, DM])
        wdkv = sb("wdkv", [P, LAT])
        wuk = sb("wuk", [P, 2, DM])
        wuv = sb("wuv", [P, DM])
        lat_g = sb("lat_g", [LAT, 1])
        lat_b = sb("lat_b", [LAT, 1])
        cos = sb("cos", [P, SEQ])
        sin = sb("sin", [P, SEQ])
        identb = sb("identb", [P, P], BF16)
        mask_q = sb("mask_q", [P, P], BF16)
        mask_k = sb("mask_k", [P, P], BF16)

        ss = sb("attn_ss", [P, TILES])
        rv = sb("attn_rv", [P, TILES])
        r = sb("attn_r", [P, TILES])
        rt = sb("attn_rt", [P, TILES])
        rh = sb("attn_rh", [P, TILES])
        xn = sb("attn_xn", [P, 2, G, DM])
        xnT = sb("attn_xnT", [P, 2, W])
        lat_all = sb("lat_all", [P, TILES, LAT])
        lat = xn[:, :, :, 0:LAT]
        latT = sb("latT", [P, 2, W])
        ns = NormScratch(sb, "latnorm", TILES)
        parts = sb("parts", [P, 2, SPLITS, W], BF16)

        qst = sb("qst", [STACK, SLOTS, 4, SEQ], BF16)
        kst = sb("kst", [STACK, SLOTS, 4, SEQ], BF16)
        vst = sb("vst", [P, 2, TPB, 4, 32])
        neg = sb("neg", [P, 2, 4, TPB])
        nm = sb("nm", [P, 4 * TPB])
        nmr = sb("nmr", [32, P])
        shift = sb("shift", [32, 2, P], BF16)
        pt = sb("pt", [P, 2, 4, 512])
        rot = pt[:, :, 0, :]
        rot2 = pt[:, :, 1, :]
        rest = pt[:, :, 2, :]
        oc = sb("oc", [P, 512])
        rec = sb("rec", [P, 4, 4])

        loaded, chain = signals.loaded, signals.chain
        folded = sem("attn_folded")
        padded = sem("stacks_padded")
        v_padded = sem("v_padded")
        xn_ready = sem("xn_ready")
        xnT_done = sem("xnT_done")
        xnT_ready = sem("xnT_ready")
        small_done = sem("small_done")
        small_read = sem("small_read")
        q_done = sem("q_done")
        rope_ready = sem("rope_ready")
        rot_ready = sem("rot_ready")
        hi_ready = sem("hi_ready")
        rest_ready = sem("rest_ready")
        mid_ready = sem("mid_ready")
        low_ready = sem("low_ready")
        parts_out = [sem(f"parts_out{k}") for k in range(2)]

        stack_loaded = [sem(f"stack_loaded{k}") for k in range(SLOTS)]
        v_staged = sem("v_staged")
        max_done = sem("max_done")
        max_read = sem("max_read")
        nm_ready = sem("nm_ready")
        nmT_done = sem("nmT_done")
        shift_hi = sem("shift_hi")
        shift_rest = sem("shift_rest")
        shift_ready = sem("shift_ready")
        shift_placed = sem("shift_placed")
        st_done = sem("st_done")
        exp_done = sem("exp_done")
        pv_done = sem("pv_done")
        acc_read = sem("acc_read")
        oT_done = sem("oT_done")
        rec_ready = sem("rec_ready")
        o_read = sem("o_read")

        HALVES = SEQ // W
        STEPS = BATCH * HALVES
        NG = BATCH * SLOTS

        units = []
        for t in range(TPB):
            for part in range(2):
                width = min(512, (t + 1) * P - part * 512)
                heads = min(512 // width, 4) if width > 0 else 1
                units += [(t, part, c, heads, width) for c in range(0, 4, heads) if width > 0]
        NU = len(units)
        exps = [(hf, j, max(0, j * P - hf * 512)) for hf in range(HALVES) for j in range(4 * hf + 4)]
        NX = len(exps)
        assert NU % 2 == 0 and NX % 2 == 0

        ahead_cost = [EACH + heads * width for t, part, c, heads, width in units] + [W] * (NM_GAP + 1)
        running = []
        for u, (hf, j, q0) in enumerate(exps):
            running += [(u, 2 * (512 - q0))] * 2 + [(u, 4 * (512 - exps[u - 1][2]))]
        take, taken, spent = [], 0, 0
        came_back = {}
        for u, cost in running:
            spent += cost
            due = spent / (PACE * sum(c for _, c in running)) * sum(ahead_cost)
            n0 = taken
            while taken < len(ahead_cost) and (sum(ahead_cost[:taken + 1]) <= due or due >= sum(ahead_cost)):
                taken += 1
            take.append(taken - n0)
            for name, at in (("last", BACK_LAST), ("first", BACK_AT)):
                if u == at + 1:
                    came_back.setdefault(name, taken)
        NORM_LAST, NORM_AT = came_back["last"] + NORM_LAG, came_back["first"] + NORM_LAG

        signals.loads += 16 * 12
        with nc.Block() as block:
            @block.sync
            def _(sp):
                for dst, src in ((norm1_w[:, :], d["norm1_w"]), (wq[:, :, :], d["wq"]), (wdkv[:, :], d["wdkv"]),
                                 (wuk[0:LAT, :, :], d["wuk"]), (wuv[0:LAT, :], d["wuv"]), (lat_g[:, :], d["lat_g"]),
                                 (lat_b[:, :], d["lat_b"]), (cos[:, :], d["cos"]), (sin[:, :], d["sin"]),
                                 (identb[:, :], d["identb"]), (mask_q[:, :], d["mask_q"]),
                                 (mask_k[:, :], d["mask_k"])):
                    sp.dma_start(dst, src).then_inc(loaded, 16)
                start_free(sp, acc_read, exp_done, oT_done, o_read, pv_done, q_done, low_ready, rope_ready, small_read,
                           xnT_done, *parts_out)
                for k in range(SLOTS):
                    sp.dma_start(qst[SROWS:SHIFT_ROW, k, :, :], d["pad"][0:SHIFT_ROW - SROWS, :, :]).then_inc(padded, 16)
                    sp.dma_start(kst[SROWS:STACK, k, :, :], d["pad"]).then_inc(padded, 16)
                def load_stacks(n, k):
                    for dram, st in ((q_dram, qst), (k_dram, kst)):
                        for i in range(SPLITS):
                            for j in range(SPLITS):
                                row = (i * SPLITS + j) * AD
                                part = i if dram is q_dram else j
                                sp.dma_start(
                                    st[row:row + AD, k, :, :],
                                    dram[bass.ds(n, 1), part, :, :].rearrange("n (c d) l -> (n d) c l", c=4))\
                                    .then_inc(stack_loaded[k], 16)

                def place_shift(n, k):
                    sp.wait_ge(shift_ready, n + 1)
                    for s in range(SHIFTS):
                        sp.dma_start(qst[SHIFT_ROW + s:SHIFT_ROW + s + 1, k, :, :], shift[:, s, :])\
                            .then_inc(shift_placed, 16)

                def store_parts(w, b):
                    for hf in range(HALVES):
                        sp.wait_ge(low_ready, FREE + STEPS * w + 2 * b + hf + 1)
                        for g in range(SLOTS):
                            sp.dma_start(
                                (q_dram, k_dram)[w][bass.ds(b * SLOTS + g, 1), :, :, hf * W:(hf + 1) * W]
                                .rearrange("n s r l -> r (n s) l"), parts[32 * g:32 * g + 32, hf, :, :])\
                                .then_inc(parts_out[hf], 16)

                with sp.Fori(0, BATCH) as b:
                    store_parts(0, b)
                for k in range(SLOTS):
                    store_parts(1, k)
                    if k == 0:
                        for hf in range(HALVES):
                            sp.wait_ge(parts_out[hf], FREE + PARTS_DMAS * (BATCH + 1))
                    load_stacks(k, k)
                for hf in range(HALVES):
                    sp.wait_ge(parts_out[hf], FREE + PARTS_DMAS * 2 * BATCH)
                place_shift(0, 0)
                with sp.Fori(0, BATCH - 1) as b:
                    for g in range(SLOTS):
                        place_shift(b * SLOTS + g + 1, (g + 1) % SLOTS)
                        sp.wait_ge(pv_done, FREE + (b * SLOTS + g + 1) * NX)
                        load_stacks((b + 1) * SLOTS + g, g)
                for g in range(1, SLOTS):
                    place_shift(NG - SLOTS + g, g)

            @block.tensor
            def _(pe):
                pe.wait_ge(loaded, signals.loads)
                pe.wait_ge(folded, 2)
                for w in range(2):
                    with pe.Fori(0, BATCH) as b:
                        for hf in range(HALVES):
                            s = STEPS * w + HALVES * b + hf
                            dst = (xnT, latT)[w]
                            pe.wait_ge(xn_ready, s + 1)
                            for t in range(G):
                                last = nc.tensor.transpose(ps[:, hf, t * P:(t + 1) * P], xn[:, hf, t, :], ident[:, :])
                            last.then_inc(xnT_done, 1)
                            pe.wait_ge(xnT_ready, s + 1)
                            pe.wait_ge(small_read, FREE + s - 1)
                            for t in range(G):
                                width, wt = ((LAT, wdkv), (DM, wuv))[w]
                                last = nc.tensor.matmul(ps[:, 2 + hf, t * width:(t + 1) * width],
                                                        dst[:, hf, t * P:(t + 1) * P], wt[:, :], start=True, stop=True)
                            last.then_inc(small_done, 1)
                            pe.wait_ge(rope_ready, FREE + s - 1)
                            for k in range(2):
                                last = nc.tensor.matmul(ps[:, 4 + 2 * hf + k, :], (wq, wuk)[w][:, k, :], dst[:, hf, :],
                                                        start=True, stop=True)
                            last.then_inc(q_done, 1)

                pe.wait_ge(low_ready, FREE + 2 * STEPS)
                pe.wait_ge(small_read, FREE + 2 * STEPS)
                pe.wait_ge(padded, 16 * 2 * SLOTS)

                def maxima(b, g, first=False):
                    n = b * SLOTS + g
                    pe.wait_ge(stack_loaded[g], STACK_DMAS * (b + 1))
                    for u, (t, part, c0, heads, width) in enumerate(units):
                        pe.wait_ge(max_read, n * NU + max(u - 1, 0))
                        diag = part * 512 + width == (t + 1) * P
                        for c in range(heads):
                            out = ps[:, 5 + u % 2, c * width:(c + 1) * width]
                            last = nc.tensor.matmul(
                                out, qst[0:SHIFT_ROW, g, c0 + c, t * P:(t + 1) * P],
                                kst[0:SHIFT_ROW, g, c0 + c, part * 512:part * 512 + width], start=True, stop=not diag)
                            if diag:
                                last = nc.tensor.matmul(out[:, width - P:width], identb[:, :], mask_q[:, :],
                                                        start=False, stop=True)
                        last.then_inc(max_done, 1)
                        yield
                    for _ in range(NM_GAP):
                        yield
                    pe.wait_ge(nm_ready, n + 1)
                    if not first:
                        pe.wait_ge(o_read, FREE + 2 * n - 1)
                    nc.tensor.transpose(ps[0:32, 7, 0:P], nm[:, :], ident[:, :]).then_inc(nmT_done, 1)
                    yield

                def rows_back(n, hf, final=False):
                    pe.wait_ge(acc_read, FREE + 2 * n + hf + 1)
                    pe.wait_ge(o_read, FREE + 2 * n + hf)
                    if hf == 1 and not final:
                        pe.wait_ge(shift_rest, n + 2)
                    for t in range(4):
                        last = nc.tensor.transpose(ps[:, 7, t * P:(t + 1) * P], oc[:, t * P:(t + 1) * P], ident[:, :])
                    last.then_inc(oT_done, 1)

                def products(n, g, u):
                    hf, j, q0 = exps[u]
                    pe.wait_ge(exp_done, FREE + 2 * NX * n + 2 * u + 2)
                    if j == 0:
                        pe.wait_ge(acc_read, FREE + 2 * n + hf)
                    for c in range(4):
                        last = nc.tensor.matmul(ps[32 * c:32 * c + 32, 4, q0:512], vst[:, g % 2, j, c, :],
                                                pt[:, u % 2, c, q0:512], start=(j == 0), stop=(j == 4 * hf + 3))
                    last.then_inc(pv_done, 1)

                def exponentials(b, g, first=False):
                    n = b * SLOTS + g

                    pe.wait_ge(shift_placed, 16 * SHIFTS * (n + 1))
                    pe.wait_ge(v_staged, n + 1)
                    for u, (hf, j, q0) in enumerate(exps):
                        diag = j * P >= hf * 512
                        for pair in range(2):
                            v = 2 * u + pair
                            pe.wait_ge(exp_done, FREE + 2 * NX * n + v - 1)
                            for c in range(2):
                                out = ps[:, 2 * pair + c, q0:512]
                                last = nc.tensor.matmul(out, kst[0:STACK, g, 2 * pair + c, j * P:(j + 1) * P],
                                                        qst[0:STACK, g, 2 * pair + c, hf * 512 + q0:hf * 512 + 512],
                                                        start=True, stop=not diag)
                                if diag:
                                    last = nc.tensor.matmul(out[:, 0:P], identb[:, :], mask_k[:, :],
                                                            start=False, stop=True)
                            last.then_inc(st_done, 1)
                            yield
                        if u >= 1:
                            products(n, g, u - 1)
                        elif not first:
                            products(n - 1, (g - 1) % SLOTS, NX - 1)
                        yield
                        if u == BACK_LAST and not first:
                            rows_back(n - 1, 1)
                        if u == BACK_AT:
                            rows_back(n, 0)

                def both(running, ahead):
                    for k, _ in enumerate(running):
                        for _ in range(take[k]):
                            next(ahead)
                    assert next(ahead, None) is None

                for _ in maxima(0, 0, first=True):
                    pass
                both(exponentials(0, 0, first=True), maxima(0, 1))
                with pe.Fori(0, BATCH - 1) as b:
                    for g in range(1, SLOTS + 1):
                        both(exponentials(b + g // SLOTS, g % SLOTS), maxima(b + (g + 1) // SLOTS, (g + 1) % SLOTS))
                for g in range(1, SLOTS - 1):
                    both(exponentials(BATCH - 1, g), maxima(BATCH - 1, g + 1))
                for _ in exponentials(BATCH - 1, SLOTS - 1):
                    pass
                products(NG - 1, SLOTS - 1, NX - 1)
                rows_back(NG - 1, 1, final=True)

            @block.scalar
            def _(act):
                act.wait_ge(loaded, signals.loads)
                def front(w, b, hf):
                    s = STEPS * w + HALVES * b + hf
                    act.wait_ge(xnT_done, FREE + s + 1)
                    act.wait_ge(q_done, FREE + s - 1)
                    if w == 0:
                        nc.scalar.copy(xnT[:, hf, :], ps[:, hf, :]).then_inc(xnT_ready, 1)
                    else:
                        nc.scalar.activation(latT[0:LAT, hf, :], ps[0:LAT, hf, :], ACT.Identity, bias=lat_b[:, 0:1],
                                             scale=lat_g[:, 0:1]).then_inc(xnT_ready, 1)
                    act.wait_ge(small_done, s + 1)
                    if w == 0:
                        nc.scalar.copy(lat_all[:, bass.ds(b * TPB + hf * G, G), :],
                                       ps[:, 2 + hf, 0:G * LAT].rearrange("p (t n) -> p t n", t=G)).then_inc(small_read, 1)
                    else:
                        vdst = v_all[:, bass.ds(4 * b, 4), 4 * hf:4 * hf + 4, :]
                        nc.scalar.copy(vdst, ps[:, 2 + hf, :].rearrange("p (t g m) -> p g t m", t=4, g=4))\
                            .then_inc(small_read, 1)

                def back(w, b, hf):
                    s = STEPS * w + HALVES * b + hf
                    act.wait_ge(rot_ready, s + 1)
                    act.wait_ge(parts_out[hf], FREE + PARTS_DMAS * (BATCH * w + b))
                    nc.scalar.copy(parts[:, hf, 0, :], rot[:, hf, :]).then_inc(hi_ready, 1)
                    act.wait_ge(rest_ready, s + 1)
                    nc.scalar.copy(parts[:, hf, 1, :], rest[:, hf, :]).then_inc(mid_ready, 1)

                for w in range(2):
                    front(w, 0, 0)
                    with act.Fori(0, BATCH - 1) as b:
                        front(w, b, 1)
                        back(w, b, 0)
                        front(w, b + 1, 0)
                        back(w, b, 1)
                    front(w, BATCH - 1, 1)
                    back(w, BATCH - 1, 0)
                    back(w, BATCH - 1, 1)

                def keep(n, hf):
                    act.wait_ge(pv_done, FREE + NX * n + (4 if hf == 0 else NX))
                    act.wait_ge(oT_done, FREE + 2 * n + hf)
                    nc.scalar.copy(oc[:, :], ps[:, 4, :]).then_inc(acc_read, 1)

                def group(n, first=False):
                    for u, (hf, j, q0) in enumerate(exps):
                        for pair in range(2):
                            act.wait_ge(st_done, 2 * NX * n + 2 * u + pair + 1)
                            if pair == 0:
                                act.wait_ge(pv_done, FREE + NX * n + u - 1)
                            nc.scalar.activation(pt[:, u % 2, 2 * pair:2 * pair + 2, q0:512],
                                                 ps[:, 2 * pair:2 * pair + 2, q0:512], ACT.Exp,
                                                 scale=float(AD) ** -0.5).then_inc(exp_done, 1)
                        if u == 0 and not first:
                            keep(n - 1, 1)
                        if u == 4:
                            keep(n, 0)

                group(0, first=True)
                with act.Fori(1, NG) as n:
                    group(n)
                keep(NG - 1, 1)

            @block.gpsimd
            def _(pool):
                for w in range(2):
                    with pool.Fori(0, BATCH) as b:
                        for hf in range(HALVES):
                            s = STEPS * w + HALVES * b + hf
                            pool.wait_ge(hi_ready, s + 1)
                            nc.gpsimd.tensor_tensor(rest[:, hf, :], rot[:, hf, :], parts[:, hf, 0, :], ALU.subtract)\
                                .then_inc(rest_ready, 1)
                            pool.wait_ge(mid_ready, s + 1)
                            nc.gpsimd.tensor_tensor(parts[:, hf, 2, :], rest[:, hf, :], parts[:, hf, 1, :], ALU.subtract)\
                                .then_inc(low_ready, 1)

                def stage(n, k):
                    nc.gpsimd.tensor_copy(vst[:, k, :, :, 0:AD],
                                          v_all[:, bass.ds(n, 1), :, :].rearrange("p n t (c d) -> p (n t) c d", c=4))\
                        .then_inc(v_staged, 1)

                pool.wait_ge(small_read, FREE + 2 * STEPS)
                pool.wait_ge(v_padded, 2)
                stage(0, 0)
                stage(1, 1)
                with pool.Fori(1, NG // 2) as m:
                    for k in range(2):
                        pool.wait_ge(pv_done, FREE + (2 * m + k - 1) * NX)
                        stage(2 * m + k, k)

            @block.vector
            def _(dve):
                nc.vector.memset(neg[:, :, :, :], -MASKED)
                nc.vector.memset(vst[:, :, :, :, :], 0.0).then_inc(v_padded, 1)
                dve.wait_ge(v_padded, 1)
                nc.vector.memset(vst[:, :, :, :, AD], 1.0).then_inc(v_padded, 1)
                nc.vector.memset(wuk[LAT:P, :, :], 0.0)
                nc.vector.memset(wuv[LAT:P, :], 0.0)
                nc.vector.memset(latT[LAT:P, :, :], 0.0).then_inc(folded, 1)
                link = Chain(dve, chain, signals.links)
                squares = o_all[:, :, :, :].rearrange("p n t m -> p (n t m)").rearrange("p (k n) -> p k n", k=TILES)
                for k in range(TILES):
                    last = nc.vector.tensor_tensor_reduce(squares[:, k, :], x_all[:, k, :], x_all[:, k, :], 1.0,
                                                          0.0, ALU.mult, ALU.add, ss[:, k:k + 1])
                link(last)
                link(nc.vector.tensor_scalar(rv[:, :], ss[:, :], 1.0 / DM, EPS_RMS2, ALU.mult, ALU.add))
                inverse_root(nc.vector, link, rv[:, :], r[:, :], rt[:, :], rh[:, :])
                dve.wait_ge(loaded, signals.loads)
                for weight in (wq[:, 0, :], wq[:, 1, :], wdkv[:, :]):
                    last = nc.vector.tensor_scalar(weight, weight, norm1_w[:, 0:1], None, ALU.mult)
                last.then_inc(folded, 1)

                def front(w, b, hf):
                    s = STEPS * w + HALVES * b + hf
                    dve.wait_ge(xnT_done, FREE + s - 1)
                    for t in range(G):
                        k = bass.ds(b * TPB + (hf * G + t), 1)
                        if w == 0:
                            last = nc.vector.tensor_scalar(xn[:, hf, t, :], x_all[:, k, :].rearrange("p k n -> p (k n)"),
                                                           r[:, k], None, ALU.mult)
                        else:
                            last = nc.vector.tensor_scalar(lat[:, hf, t, :], lat_all[:, k, :].rearrange("p k n -> p (k n)"),
                                                           ns.y[:, k], ns.b[:, k], ALU.mult, ALU.add)
                    last.then_inc(xn_ready, 1)

                def back(w, b, hf):
                    s = STEPS * w + HALVES * b + hf
                    sl = slice(hf * W, (hf + 1) * W)
                    dve.wait_ge(q_done, FREE + s + 1)
                    dve.wait_ge(low_ready, FREE + s - 1)
                    nc.vector.tensor_tensor(rot[:, hf, :], ps[:, 4 + 2 * hf, :], cos[:, sl], ALU.mult)
                    nc.vector.tensor_tensor(rot2[:, hf, :], ps[:, 5 + 2 * hf, :], sin[:, sl], ALU.mult)\
                        .then_inc(rope_ready, 1)
                    dve.wait_ge(rope_ready, FREE + s + 1)
                    nc.vector.tensor_tensor(rot[:, hf, :], rot[:, hf, :], rot2[:, hf, :], ALU.add).then_inc(rot_ready, 1)

                for w in range(2):
                    if w == 1:
                        dve.wait_ge(small_read, FREE + STEPS)
                        for k in range(TILES):
                            last = nc.vector.bn_stats(ns.st[:, k, :], lat_all[:, k, :])
                        link(last)
                        norm_scales(nc.vector, link, ns, EPS_LN, LAT)
                    front(w, 0, 0)
                    with dve.Fori(0, BATCH - 1) as b:
                        front(w, b, 1)
                        back(w, b, 0)
                        front(w, b + 1, 0)
                        back(w, b, 1)
                    front(w, BATCH - 1, 1)
                    back(w, BATCH - 1, 0)
                    back(w, BATCH - 1, 1)
                signals.links = link.start + link.count

                def maxima(n):
                    for u, (t, part, c0, heads, width) in enumerate(units):
                        dve.wait_ge(max_done, n * NU + u + 1)
                        nc.vector.tensor_reduce(
                            neg[:, part, c0:c0 + heads, t],
                            ps[:, 5 + u % 2, 0:heads * width].rearrange("p (c w) -> p c w", c=heads), AX.X, ALU.max,
                            negate=True).then_inc(max_read, 1)
                        yield
                    dve.wait_ge(max_read, (n + 1) * NU)
                    nc.vector.tensor_tensor(nm[:, :], neg[:, 0, :, :].rearrange("p c t -> p (c t)"),
                                            neg[:, 1, :, :].rearrange("p c t -> p (c t)"), ALU.min).then_inc(nm_ready, 1)
                    yield
                    dve.wait_ge(nmT_done, n + 1)
                    dve.wait_ge(shift_placed, 16 * SHIFTS * n)
                    nc.vector.tensor_copy(shift[:, 0, :], ps[0:32, 7, 0:P]).then_inc(shift_hi, 1)
                    dve.wait_ge(shift_hi, n + 1)
                    nc.vector.tensor_tensor(nmr[:, :], ps[0:32, 7, 0:P], shift[:, 0, :], ALU.subtract).then_inc(shift_rest, 1)
                    dve.wait_ge(shift_rest, n + 1)
                    nc.vector.tensor_copy(shift[:, 1, :], nmr[:, :]).then_inc(shift_ready, 1)

                def norm(n, hf):
                    dve.wait_ge(oT_done, FREE + 2 * n + hf + 1)
                    back = ps[:, 7, :].rearrange("p (t c m) -> p t c m", t=4, c=4)
                    nc.vector.reciprocal(rec[:, :, :], back[:, :, :, AD]).then_inc(rec_ready, 1)
                    dve.wait_ge(rec_ready, 2 * n + hf + 1)
                    nc.vector.tensor_tensor(
                        o_all[:, bass.ds(n, 1), 4 * hf:4 * hf + 4, :].rearrange("p n t (c d) -> p (n t) c d", c=4),
                        back[:, :, :, 0:AD], rec[:, :, :].unsqueeze(3).to_broadcast([P, 4, 4, AD]), ALU.mult)\
                        .then_inc(o_read, 1)

                for _ in maxima(0):
                    pass
                def group(n, first=False):
                    for k, _ in enumerate(maxima(n + 1)):
                        if k == NORM_LAST and not first:
                            norm(n - 1, 1)
                        if k == NORM_AT:
                            norm(n, 0)

                group(0, first=True)
                with dve.Fori(1, NG - 1) as n:
                    group(n)
                norm(NG - 2, 1)
                norm(NG - 1, 0)
                norm(NG - 1, 1)


SLOTS = AH // 4
SHIFTS = 2
STACK = SHIFT_ROW + SHIFTS
STACK_DMAS = 16 * 2 * SPLITS * SPLITS
BACK_LAST, BACK_AT, NORM_LAG = 1, 6, 1
NM_GAP, PACE, EACH = 0, 0.82, 0
PARTS_DMAS = 16 * SLOTS


def experts(nc, signals, x_all, ident, d, o_all):
    with ExitStack() as ctx:
        def sb(name, shape, dt=F32):
            return ctx.enter_context(nc.sbuf_tensor(name, shape, dt))

        def sem(name):
            return signals.new(name)

        ps = ctx.enter_context(nc.psum_tensor("moe_psum", [P, 8, 512], F32))

        norm2_w = sb("norm2_w", [P, 1])
        wo = sb("moe_wo", [P, DM])
        gate_w = sb("gate_w", [P, NE])
        gate_b = sb("gate_b", [P, NE])
        w1 = sb("moe_w1", [P, NE, HID])
        b1 = sb("moe_b1", [P, NE, HID // P])
        w2 = sb("moe_w2", [P, NE, HID // P, DM])
        b2 = sb("moe_b2", [G * NE, G * DM])
        order = sb("order", [P, NE])

        ost = sb("ost", [P, G, DM])
        oT = sb("moe_oT", [P, W])
        x2 = sb("x2", [P, 2, G, DM])
        acc = sb("moe_acc", [P, 2, G, DM])
        xn = sb("moe_xn", [P, G, DM])
        xnT = sb("moe_xnT", [P, 2, W])
        ss = sb("moe_ss", [P, G])
        rv = sb("moe_rv", [P, G])
        r = sb("moe_r", [P, G])
        rt = sb("moe_rt", [P, G])
        rh = sb("moe_rh", [P, G])
        logits = sb("logits", [P, G, NE])
        best = sb("best", [P, G])
        onehot = sb("onehot", [P, 2, G, NE])
        onehotT = sb("onehotT", [G * NE, P])
        hs = sb("moe_hs", [P, 2, HID // P, W])
        ns = NormScratch(sb, "moenorm")

        loaded, chain = signals.loaded, signals.chain
        folded = sem("moe_folded")
        ost_ready = sem("ost_ready")
        oT_done = sem("moe_oT_done")
        oT_ready = sem("moe_oT_ready")
        ao_done = sem("ao_done")
        x2_ready = sem("x2_ready")
        xn_ready = sem("moe_xn_ready")
        xnT_done = sem("moe_xnT_done")
        xnT_ready = sem("moe_xnT_ready")
        gate_done = sem("gate_done")
        gate_read = sem("gate_read")
        onehot_ready = sem("onehot_ready")
        onehotT_done = sem("onehotT_done")
        onehotT_ready = sem("onehotT_ready")
        b2_done = sem("b2_done")
        b2_read = sem("b2_read")
        h_done = sem("moe_h_done")
        h_act = sem("moe_h_act")
        h_dve = sem("moe_h_dve")
        y_done = sem("moe_y_done")
        y_read = sem("moe_y_read")

        HALVES = SEQ // W
        STEPS = BATCH * HALVES
        HB = HID // P
        small = ps[:, 0, :]

        signals.loads += 16 * 9
        with nc.Block() as block:
            @block.sync
            def _(sp):
                for dst, src in ((norm2_w[:, :], d["norm2_w"]), (wo[:, :], d["moe_wo"]), (gate_w[:, :], d["gate_w"]),
                                 (w1[:, :, :], d["moe_w1"]), (b1[:, :, :], d["moe_b1"]), (w2[:, :, :, :], d["moe_w2"]),
                                 (b2[:, :], d["moe_b2"]), (order[:, :], d["order"]),
                                 (gate_b[:, :], d["gate_b"].partition_broadcast(P))):
                    sp.dma_start(dst, src).then_inc(loaded, 16)
                start_free(sp, h_act, h_done, h_dve, y_done, y_read)

            @block.tensor
            def _(pe):
                pe.wait_ge(loaded, signals.loads)
                pe.wait_ge(folded, 1)

                def front(s, hf):
                    pe.wait_ge(ost_ready, s + 1)
                    pe.wait_ge(onehotT_ready, s)
                    for t in range(G):
                        last = nc.tensor.transpose(ps[:, 0, t * P:(t + 1) * P], ost[:, t, :], ident[:, :])
                    last.then_inc(oT_done, 1)
                    yield
                    pe.wait_ge(oT_ready, s + 1)
                    pe.wait_ge(b2_read, s)
                    for t in range(G):
                        last = nc.tensor.matmul(ps[:, 1, t * P:(t + 1) * P], oT[:, t * P:(t + 1) * P], wo[:, :],
                                                start=True, stop=True)
                    last.then_inc(ao_done, 1)
                    yield
                    pe.wait_ge(xn_ready, s + 1)
                    for t in range(G):
                        last = nc.tensor.transpose(ps[:, 0, t * P:(t + 1) * P], xn[:, t, :], ident[:, :])
                    last.then_inc(xnT_done, 1)
                    yield
                    pe.wait_ge(xnT_ready, s + 1)
                    for t in range(G):
                        last = nc.tensor.matmul(small[:, t * NE:(t + 1) * NE], xnT[:, hf, t * P:(t + 1) * P],
                                                gate_w[:, :], start=True, stop=True)
                    last.then_inc(gate_done, 1)
                    yield
                    pe.wait_ge(onehot_ready, s + 1)
                    nc.tensor.transpose(small[0:G * NE, P:2 * P], onehot[:, hf, :, :].rearrange("p t e -> p (t e)"),
                                        ident[:, :]).then_inc(onehotT_done, 1)
                    yield
                    pe.wait_ge(onehotT_ready, s + 1)
                    nc.tensor.matmul(ps[:, 1, :], onehotT[:, :], b2[:, :], start=True, stop=True).then_inc(b2_done, 1)
                    yield

                def expert_steps(s, hf):
                    blocks = [(e, k) for e in range(NE) for k in range(HB)]

                    def hidden(n):
                        e, k = blocks[n]
                        pe.wait_ge(h_act if n % 2 == 0 else h_dve, FREE + 8 * s + (n - 4) // 2 + 1)
                        nc.tensor.matmul(ps[:, 2 + n % 4, :], w1[:, e, k * P:(k + 1) * P], xnT[:, hf, :],
                                         start=True, stop=True).then_inc(h_done, 1)

                    def outputs(e):
                        pe.wait_ge(h_act, FREE + 8 * s + 2 * e + 2)
                        pe.wait_ge(h_dve, FREE + 8 * s + 2 * e + 2)
                        pe.wait_ge(y_read, FREE + 4 * s + max(e - 1, 0))
                        for t in range(G):
                            for k in range(HB):
                                last = nc.tensor.matmul(ps[:, 6 + e % 2, t * P:(t + 1) * P],
                                                        hs[:, e % 2, k, t * P:(t + 1) * P], w2[:, e, k, :],
                                                        start=(k == 0), stop=(k == HB - 1))
                        last.then_inc(y_done, 1)

                    for n in range(NE * HB):
                        hidden(n)
                        yield
                        if n % HB == HB - 1 and n > HB:
                            outputs(n // HB - 1)
                            yield
                    outputs(NE - 1)
                    yield

                for _ in front(0, 0):
                    pass
                with pe.Fori(0, BATCH - 1) as b:
                    for hf in range(HALVES):
                        s = HALVES * b + hf
                        ahead = front(s + 1, 1 - hf)
                        for k, _ in enumerate(expert_steps(s, hf)):
                            if k in PE_FRONT:
                                next(ahead, None)
                        for _ in ahead:
                            pass
                s = STEPS - 2
                ahead = front(s + 1, 1)
                for k, _ in enumerate(expert_steps(s, 0)):
                    if k in PE_FRONT:
                        next(ahead, None)
                for _ in ahead:
                    pass
                for _ in expert_steps(s + 1, 1):
                    pass

            @block.scalar
            def _(act):
                act.wait_ge(loaded, signals.loads)

                def front(s, hf, first=False):
                    act.wait_ge(oT_done, s + 1)
                    nc.scalar.copy(oT[:, :], ps[:, 0, :]).then_inc(oT_ready, 1)
                    yield
                    act.wait_ge(xnT_done, s + 1)
                    if not first:
                        act.wait_ge(h_done, FREE + 16 * (s - 1))
                    nc.scalar.copy(xnT[:, hf, :], ps[:, 0, :]).then_inc(xnT_ready, 1)
                    yield
                    act.wait_ge(onehotT_done, s + 1)
                    nc.scalar.copy(onehotT[:, :], small[0:G * NE, P:2 * P]).then_inc(onehotT_ready, 1)
                    yield

                def relus(s):
                    for n in range(0, NE * HB, 2):
                        e, k = n // HB, n % HB
                        act.wait_ge(h_done, FREE + 16 * s + n + 1)
                        act.wait_ge(y_done, FREE + 4 * s + max(e - 1, 0))
                        nc.scalar.activation(hs[:, e % 2, k, :], ps[:, 2 + n % 4, :], ACT.Relu, bias=b1[:, e, k:k + 1])\
                            .then_inc(h_act, 1)
                        yield

                for _ in front(0, 0, first=True):
                    pass

                def step(s, hf, more=True):
                    ahead = front(s + 1, 1 - hf) if more else iter(())
                    for k, _ in enumerate(relus(s)):
                        if k in ACT_FRONT:
                            next(ahead, None)
                    for _ in ahead:
                        pass

                with act.Fori(0, BATCH - 1) as b:
                    for hf in range(HALVES):
                        step(HALVES * b + hf, hf)
                step(STEPS - 2, 0)
                step(STEPS - 1, 1, more=False)

            @block.vector
            def _(dve):
                dve.wait_ge(loaded, signals.loads)
                nc.vector.tensor_scalar(gate_w[:, :], gate_w[:, :], norm2_w[:, 0:1], None, ALU.mult)
                nc.vector.tensor_scalar(w1[:, :, :], w1[:, :, :], norm2_w[:, 0:1], None, ALU.mult).then_inc(folded, 1)

                def front(b, s, hf, step):
                    x_now = x_all[:, bass.ds(b * TPB + hf * G, G), :]
                    dve.wait_ge(oT_done, s)
                    for g in range(SLOTS):
                        last = nc.vector.tensor_copy(ost[:, :, 32 * g:32 * g + 32],
                                                     o_all[:, bass.ds(b * SLOTS + g, 1), 4 * hf:4 * hf + 4, :]
                                                     .rearrange("p n t m -> p (n t) m"))
                    last.then_inc(ost_ready, 1)
                    yield
                    dve.wait_ge(ao_done, s + 1)
                    dve.wait_ge(xnT_done, s)
                    step(nc.vector.tensor_tensor(x2[:, hf, :, :], ps[:, 1, :].rearrange("p (t n) -> p t n", t=G), x_now,
                                                 ALU.add))
                    for t in range(G):
                        last = nc.vector.tensor_tensor_reduce(xn[:, t, :], x2[:, hf, t, :], x2[:, hf, t, :], 1.0, 0.0,
                                                              ALU.mult, ALU.add, ss[:, t:t + 1])
                    step(last)
                    step(nc.vector.tensor_scalar(rv[:, :], ss[:, :], 1.0 / DM, EPS_RMS2, ALU.mult, ALU.add))
                    inverse_root(nc.vector, step, rv[:, :], r[:, :], rt[:, :], rh[:, :])
                    for t in range(G):
                        last = nc.vector.tensor_scalar(xn[:, t, :], x2[:, hf, t, :], r[:, t:t + 1], None, ALU.mult)
                    last.then_inc(xn_ready, 1)
                    nc.vector.tensor_tensor(acc[:, hf, :, :], x2[:, hf, :, :], x_now, ALU.add)
                    yield
                    dve.wait_ge(gate_done, s + 1)
                    step(nc.vector.tensor_tensor(logits[:, :, :], small[:, 0:G * NE].rearrange("p (t e) -> p t e", t=G),
                                                 gate_b[:, :].unsqueeze(1).to_broadcast([P, G, NE]), ALU.add))
                    step(nc.vector.tensor_reduce(best[:, :], logits[:, :, :], AX.X, ALU.max))
                    step(nc.vector.tensor_tensor(logits[:, :, :], logits[:, :, :],
                                                 best[:, :].unsqueeze(2).to_broadcast([P, G, NE]), ALU.is_equal))
                    step(nc.vector.tensor_tensor(logits[:, :, :], logits[:, :, :],
                                                 order[:, :].unsqueeze(1).to_broadcast([P, G, NE]), ALU.mult))
                    step(nc.vector.tensor_reduce(best[:, :], logits[:, :, :], AX.X, ALU.max))
                    nc.vector.tensor_tensor(onehot[:, hf, :, :], logits[:, :, :],
                                            best[:, :].unsqueeze(2).to_broadcast([P, G, NE]), ALU.is_equal)\
                        .then_inc(onehot_ready, 1)
                    yield
                    dve.wait_ge(b2_done, s + 1)
                    nc.vector.tensor_tensor(acc[:, hf, :, :], acc[:, hf, :, :],
                                            ps[:, 1, :].rearrange("p (t n) -> p t n", t=G), ALU.add).then_inc(b2_read, 1)
                    yield

                def back(b, s, hf, step):
                    def take(e):
                        dve.wait_ge(y_done, FREE + 4 * s + e + 1)
                        if e == 0:
                            dve.wait_ge(b2_read, s + 1)
                        else:
                            dve.wait_ge(y_read, FREE + 4 * s + e)
                        for t in range(G):
                            last = nc.vector.scalar_tensor_tensor(
                                out=acc[:, hf, t, :], in0=ps[:, 6 + e % 2, t * P:(t + 1) * P],
                                scalar=onehot[:, hf, t, e:e + 1], in1=acc[:, hf, t, :], op0=ALU.mult, op1=ALU.add)
                        last.then_inc(y_read, 1)

                    for n in range(1, NE * HB, 2):
                        e, k = n // HB, n % HB
                        dve.wait_ge(h_done, FREE + 16 * s + n + 1)
                        dve.wait_ge(y_done, FREE + 4 * s + max(e - 1, 0))
                        nc.vector.tensor_scalar(hs[:, e % 2, k, :], ps[:, 2 + n % 4, :], b1[:, e, k:k + 1], 0.0,
                                                ALU.add, ALU.max).then_inc(h_dve, 1)
                        yield
                        if n in (9, 13):
                            take(n // HB - 2)
                            yield
                    for e in (2, 3):
                        take(e)

                def finish(b, s, hf, step):
                    dve.wait_ge(y_read, FREE + 4 * s + 4)
                    for t in range(G):
                        last = nc.vector.bn_stats(ns.st[:, t, :], acc[:, hf, t, :])
                    step(last)
                    yield
                    norm_scales(nc.vector, step, ns, EPS_LN, DM)
                    yield
                    x_now = x_all[:, bass.ds(b * TPB + hf * G, G), :]
                    for t in range(G):
                        last = nc.vector.tensor_scalar(x_now[:, t, :], acc[:, hf, t, :], ns.y[:, t:t + 1], ns.b[:, t:t + 1],
                                                       ALU.mult, ALU.add)
                    step(last)
                    yield

                def both(b, s, hf, step, more=True, first=False):
                    ahead = front(b + (1 if hf else 0), s + 1, 1 - hf, step) if more else iter(())
                    behind = iter(()) if first else finish(b - (0 if hf else 1), s - 1, 1 - hf, step)
                    for k, _ in enumerate(back(b, s, hf, step)):
                        for _ in range(DVE_FRONT.count(k)):
                            next(ahead, None)
                        for _ in range(DVE_FINISH.count(k)):
                            next(behind, None)
                    for _ in ahead:
                        pass

                link = Chain(dve, chain, signals.links)
                for _ in front(0, 0, 0, link):
                    pass
                both(0, 0, 0, link, first=True)
                with dve.Fori(0, BATCH - 1) as b:
                    step = Chain(dve, chain, link.start + link.count, b, MOE_LINKS)
                    both(b, HALVES * b + 1, 1, step)
                    both(b + 1, HALVES * b + 2, 0, step)
                    step.end()
                link = Chain(dve, chain, link.start + link.count + (BATCH - 1) * MOE_LINKS)
                both(BATCH - 1, STEPS - 1, 1, link, more=False)
                for _ in finish(BATCH - 1, STEPS - 1, 1, link):
                    pass
                signals.links = link.start + link.count


PE_FRONT = (3, 5, 10, 12, 15, 17)
DVE_FRONT, DVE_FINISH = (0, 2, 6, 9), (0, 1, 1)
ACT_FRONT = (1, 4, 6)
MOE_LINKS = 2 * (1 + 1 + 1 + ROOT_LINKS + 5 + NORM_LINKS)


def flow_attention(nc, signals, x_all, ones, ident, d):
    with ExitStack() as ctx:
        def sb(name, shape, dt=F32):
            return ctx.enter_context(nc.sbuf_tensor("fl_" + name, shape, dt))

        def sem(name):
            return signals.new("fl_" + name)

        ps = ctx.enter_context(nc.psum_tensor("flow_psum", [P, 8, 512], F32))
        PAIR = 2
        seqs = range(PAIR)
        A = [ps[:, 4 * s:4 * s + 2, :] for s in seqs]
        B = [ps[:, 4 * s + 2:4 * s + 4, :] for s in seqs]

        def tiles(banks):
            return banks.rearrange("p k (t n) -> p (k t) n", n=P)

        def rows(banks):
            return banks[:, 0, 0:2 * TPB * AH].rearrange("p (w t h) -> p w t h", w=2, t=TPB)

        wq, wk, wv, wo = (sb(n, [P, DM]) for n in ("wq", "wk", "wv", "wo"))
        bq = sb("bq", [P, 1])
        bk = sb("bk", [P, 1])
        bv = sb("bv", [P, DM])
        bo = sb("bo", [P, DM])
        head = sb("head", [P, AH])
        same = sb("same", [P, DM])

        xs = sb("xs", [P, PAIR, TPB, DM])
        xT = sb("xT", [P, PAIR, SEQ])
        qT = sb("qT", [P, PAIR, SEQ])
        kT = sb("kT", [P, PAIR, SEQ])
        qe = sb("qe", [P, PAIR, SEQ])
        ke = sb("ke", [P, PAIR, SEQ])
        sums = sb("sums", [P, PAIR, 2])
        sume = sb("sume", [P, PAIR, 2])
        blk = sb("blk", [P, PAIR, 2, AH])
        vb = sb("vb", [P, PAIR, TPB, DM])
        ktok = sb("ktok", [P, PAIR, TPB, DM])
        qtok = sb("qtok", [P, PAIR, TPB, DM])
        flow = sb("flow", [P, PAIR, 2, TPB, AH])
        gblk = sb("gblk", [P, PAIR, 2, AH])
        alloc = sb("alloc", [P, PAIR, TPB, AH])
        comp = sb("comp", [P, PAIR, TPB, AH])
        total = sb("total", [P, PAIR, AH])
        weight = sb("weight", [P, PAIR, TPB, AH])
        kv = sb("kv", [P, PAIR, DM])
        ot = sb("ot", [P, PAIR, TPB, DM])
        oT = sb("oT", [P, PAIR, SEQ])
        ns = [NormScratch(sb, f"norm{s}", TPB) for s in seqs]

        loaded, chain = signals.loaded, signals.chain
        names = ("xs_ready", "xT_done", "xT_ready", "q_done", "k_done", "q_ready", "k_ready", "v_done", "v_ready",
                 "ktok_done", "ktok_ready", "qtok_done", "qtok_ready", "sums_ready", "eps_ready", "blk_ready", "flow_done",
                 "flow_ready", "g_done", "gblk_ready", "cons_done", "alloc_ready", "clip_ready", "exp_ready",
                 "total_done", "total_ready", "comp_ready", "vs_ready", "kv_done", "kv_ready", "weight_ready",
                 "o_done", "o_ready", "oT_done", "oT_ready", "out_done")
        done = {n: sem(n) for n in names}

        signals.loads += 16 * 10
        with nc.Block() as block:
            @block.sync
            def _(sp):
                for dst, src in ((wq, "fl_wq"), (wk, "fl_wk"), (wv, "fl_wv"), (wo, "fl_wo"), (bq, "fl_bq"), (bk, "fl_bk"),
                                 (head, "head"), (same, "same")):
                    sp.dma_start(dst[:, :], d[src]).then_inc(loaded, 16)
                for dst, src in ((bv, "fl_bv"), (bo, "fl_bo")):
                    sp.dma_start(dst[:, :], d[src].partition_broadcast(P)).then_inc(loaded, 16)

            @block.tensor
            def _(pe):
                pe.wait_ge(loaded, signals.loads)

                def tile(src, s, t):
                    return src[:, s, t * P:(t + 1) * P]

                with pe.Fori(0, BATCH // PAIR) as m:
                    def wait(name, s):
                        pe.wait_ge(done[name], PAIR * m + s + 1)

                    for s in seqs:
                        wait("xs_ready", s)
                        for t in range(TPB):
                            last = nc.tensor.transpose(tiles(A[s])[:, t, :], xs[:, s, t, :], ident[:, :])
                        last.then_inc(done["xT_done"], 1)
                    for s in seqs:
                        wait("xT_ready", s)
                        for k in range(2):
                            last = nc.tensor.matmul(A[s][:, k, :], wk[:, :], xT[:, s, k * 512:(k + 1) * 512],
                                                    start=True, stop=True)
                        last.then_inc(done["k_done"], 1)
                        for k in range(2):
                            last = nc.tensor.matmul(B[s][:, k, :], wq[:, :], xT[:, s, k * 512:(k + 1) * 512],
                                                    start=True, stop=True)
                        last.then_inc(done["q_done"], 1)
                    for s in seqs:
                        wait("k_ready", s)
                        for t in range(TPB):
                            last = nc.tensor.transpose(tiles(A[s])[:, t, :], tile(kT, s, t), ident[:, :])
                        last.then_inc(done["ktok_done"], 1)
                        wait("q_ready", s)
                        for t in range(TPB):
                            last = nc.tensor.matmul(tiles(B[s])[:, t, :], tile(xT, s, t), wv[:, :], start=True, stop=True)
                        last.then_inc(done["v_done"], 1)
                    for s in seqs:
                        wait("ktok_ready", s)
                        wait("blk_ready", s)
                        for w, src in enumerate((qe, ke)):
                            for t in range(TPB):
                                last = nc.tensor.matmul(rows(A[s])[:, w, t, :], tile(src, s, t), blk[:, s, w, :],
                                                        start=True, stop=True)
                        last.then_inc(done["flow_done"], 1)
                        wait("v_ready", s)
                        for t in range(TPB):
                            last = nc.tensor.transpose(tiles(B[s])[:, t, :], tile(qT, s, t), ident[:, :])
                        last.then_inc(done["qtok_done"], 1)
                    for s in seqs:
                        wait("flow_ready", s)
                        wait("qtok_ready", s)
                        for w, src in enumerate((ktok, qtok)):
                            for t in range(TPB):
                                last = nc.tensor.matmul(B[s][:, 0, w * AH:(w + 1) * AH], src[:, s, t, :],
                                                        flow[:, s, 1 - w, t, :], start=(t == 0), stop=(t == TPB - 1))
                        last.then_inc(done["g_done"], 1)
                    for s in seqs:
                        wait("gblk_ready", s)
                        for w, src in enumerate((qe, ke)):
                            for t in range(TPB):
                                last = nc.tensor.matmul(rows(A[s])[:, w, t, :], tile(src, s, t), gblk[:, s, w, :],
                                                        start=True, stop=True)
                        last.then_inc(done["cons_done"], 1)
                    for s in seqs:
                        wait("exp_ready", s)
                        for t in range(TPB):
                            last = nc.tensor.matmul(B[s][:, 0, 0:AH], ones[:, :], comp[:, s, t, :],
                                                    start=(t == 0), stop=(t == TPB - 1))
                        last.then_inc(done["total_done"], 1)
                    for s in seqs:
                        wait("vs_ready", s)
                        wait("alloc_ready", s)
                        for t in range(TPB):
                            last = nc.tensor.matmul(A[s][:, 0, 0:DM], ktok[:, s, t, :], vb[:, s, t, :],
                                                    start=(t == 0), stop=(t == TPB - 1))
                        last.then_inc(done["kv_done"], 1)
                    for s in seqs:
                        wait("kv_ready", s)
                        for t in range(TPB):
                            last = nc.tensor.matmul(tiles(B[s])[:, t, :], tile(qT, s, t), kv[:, s, :], start=True, stop=True)
                        last.then_inc(done["o_done"], 1)
                    for s in seqs:
                        wait("o_ready", s)
                        for t in range(TPB):
                            last = nc.tensor.transpose(tiles(A[s])[:, t, :], ot[:, s, t, :], ident[:, :])
                        last.then_inc(done["oT_done"], 1)
                    for s in seqs:
                        wait("oT_ready", s)
                        for t in range(TPB):
                            last = nc.tensor.matmul(tiles(B[s])[:, t, :], tile(oT, s, t), wo[:, :], start=True, stop=True)
                        last.then_inc(done["out_done"], 1)

            @block.scalar
            def _(act):
                act.wait_ge(loaded, signals.loads)
                with act.Fori(0, BATCH // PAIR) as m:
                    def wait(name, s):
                        act.wait_ge(done[name], PAIR * m + s + 1)

                    for s in seqs:
                        wait("xT_done", s)
                        nc.scalar.copy(xT[:, s, :], A[s].rearrange("p k n -> p (k n)")).then_inc(done["xT_ready"], 1)
                    for s in seqs:
                        wait("k_done", s)
                        nc.scalar.activation(kT[:, s, :], A[s].rearrange("p k n -> p (k n)"), ACT.Sigmoid, bias=bk[:, 0:1],
                                             accum_out=sums[:, s, 0:1]).then_inc(done["k_ready"], 1)
                        wait("q_done", s)
                        nc.scalar.activation(qT[:, s, :], B[s].rearrange("p k n -> p (k n)"), ACT.Sigmoid, bias=bq[:, 0:1],
                                             accum_out=sums[:, s, 1:2]).then_inc(done["q_ready"], 1)
                    for s in seqs:
                        wait("ktok_done", s)
                        nc.scalar.copy(ktok[:, s, :, :], tiles(A[s])).then_inc(done["ktok_ready"], 1)
                    for s in seqs:
                        wait("qtok_done", s)
                        nc.scalar.copy(qtok[:, s, :, :], tiles(B[s])).then_inc(done["qtok_ready"], 1)
                    for s in seqs:
                        wait("cons_done", s)
                        nc.scalar.activation(alloc[:, s, :, :], rows(A[s])[:, 0, :, :], ACT.Sigmoid)\
                            .then_inc(done["alloc_ready"], 1)
                    for s in seqs:
                        wait("clip_ready", s)
                        nc.scalar.activation(comp[:, s, :, :], comp[:, s, :, :], ACT.Exp).then_inc(done["exp_ready"], 1)
                    for s in seqs:
                        wait("oT_done", s)
                        nc.scalar.copy(oT[:, s, :], A[s].rearrange("p k n -> p (k n)")).then_inc(done["oT_ready"], 1)

            @block.vector
            def _(dve):
                dve.wait_ge(loaded, signals.loads)
                with dve.Fori(0, BATCH // PAIR) as m:
                    step = Chain(dve, chain, signals.links, m, FLOW_LINKS)

                    def wait(name, s):
                        dve.wait_ge(done[name], PAIR * m + s + 1)

                    def x_now(s):
                        return x_all[:, bass.ds(m * (PAIR * TPB) + s * TPB, TPB), :]

                    for s in seqs:
                        nc.vector.tensor_copy(xs[:, s, :, :], x_now(s)).then_inc(done["xs_ready"], 1)
                    for s in seqs:
                        wait("k_ready", s)
                        nc.vector.tensor_scalar(ke[:, s, :], kT[:, s, :], FLOW_EPS, None, ALU.add)
                        wait("q_ready", s)
                        nc.vector.tensor_scalar(qe[:, s, :], qT[:, s, :], FLOW_EPS, None, ALU.add)
                        step(nc.vector.tensor_scalar(sume[:, s, :], sums[:, s, :], FLOW_EPS, None, ALU.add))
                        for w in range(2):
                            last = nc.vector.tensor_scalar(blk[:, s, w, :], head[:, :], sume[:, s, w:w + 1], None, ALU.mult)
                        last.then_inc(done["blk_ready"], 1)
                    for s in seqs:
                        wait("v_done", s)
                        nc.vector.tensor_tensor(vb[:, s, :, :], tiles(B[s]), bv[:, :].unsqueeze(1).to_broadcast([P, TPB, DM]),
                                                ALU.add).then_inc(done["v_ready"], 1)
                    for s in seqs:
                        wait("flow_done", s)
                        nc.vector.reciprocal(flow[:, s, :, :, :], rows(A[s])).then_inc(done["flow_ready"], 1)
                    for s in seqs:
                        wait("g_done", s)
                        nc.vector.scalar_tensor_tensor(
                            out=gblk[:, s, :, :], in0=B[s][:, 0, 0:2 * AH].rearrange("p (w h) -> p w h", w=2), scalar=FLOW_EPS,
                            in1=head[:, :].unsqueeze(1).to_broadcast([P, 2, AH]), op0=ALU.add, op1=ALU.mult)\
                            .then_inc(done["gblk_ready"], 1)
                    for s in seqs:
                        wait("alloc_ready", s)
                        nc.vector.tensor_scalar(comp[:, s, :, :], rows(A[s])[:, 1, :, :], -1.0, 1.0, ALU.max, ALU.min)\
                            .then_inc(done["clip_ready"], 1)
                    for s in seqs:
                        wait("total_done", s)
                        wait("exp_ready", s)
                        step(nc.vector.reciprocal(total[:, s, :], B[s][:, 0, 0:AH]))
                        step(nc.vector.scalar_tensor_tensor(
                            out=comp[:, s, :, :], in0=comp[:, s, :, :], scalar=float(SEQ),
                            in1=total[:, s, :].unsqueeze(1).to_broadcast([P, TPB, AH]), op0=ALU.mult, op1=ALU.mult))
                        split = vb[:, s, :, :].rearrange("p t (h n) -> p (t h) n", h=AH)
                        nc.vector.tensor_tensor(
                            split, split, comp[:, s, :, :].rearrange("p t h -> p (t h)").unsqueeze(2)
                            .to_broadcast([P, TPB * AH, AD]), ALU.mult).then_inc(done["vs_ready"], 1)
                        wait("alloc_ready", s)
                        step(nc.vector.tensor_tensor(weight[:, s, :, :], alloc[:, s, :, :], flow[:, s, 0, :, :], ALU.mult))
                    for s in seqs:
                        wait("kv_done", s)
                        nc.vector.tensor_tensor(kv[:, s, :], A[s][:, 0, 0:DM], same[:, :], ALU.mult)\
                            .then_inc(done["kv_ready"], 1)
                    for s in seqs:
                        wait("o_done", s)
                        nc.vector.tensor_tensor(
                            ot[:, s, :, :].rearrange("p t (h n) -> p (t h) n", h=AH),
                            tiles(B[s]).rearrange("p t (h n) -> p (t h) n", h=AH),
                            weight[:, s, :, :].rearrange("p t h -> p (t h)").unsqueeze(2)
                            .to_broadcast([P, TPB * AH, AD]), ALU.mult).then_inc(done["o_ready"], 1)
                        wait("xT_done", s)
                        step(nc.vector.tensor_tensor(xs[:, s, :, :], xs[:, s, :, :],
                                                     bo[:, :].unsqueeze(1).to_broadcast([P, TPB, DM]), ALU.add))
                    for s in seqs:
                        wait("out_done", s)
                        step(nc.vector.tensor_tensor(xs[:, s, :, :], xs[:, s, :, :], tiles(B[s]), ALU.add))
                        layer_norm(nc.vector, step, ns[s], lambda t: xs[:, s, t, :], lambda t: x_now(s)[:, t, :], EPS_LN, DM, TPB)
                    step.end()
                signals.links += BATCH // PAIR * FLOW_LINKS


FLOW_LINKS = 2 * (1 + 3 + 1 + 1 + NORM_LINKS)


def ternary_mlp(nc, signals, x_all, ones, ident, d, out):
    with ExitStack() as ctx:
        def sb(name, shape, dt=F32):
            return ctx.enter_context(nc.sbuf_tensor("tm_" + name, shape, dt))

        def sem(name):
            return signals.new("tm_" + name)

        ps = ctx.enter_context(nc.psum_tensor("mlp_psum", [P, 8, 512], F32))
        HB = FH // P
        STEPS = TILES // G
        wf = sb("wf", [P, FH])
        wp = sb("wp", [P, HB, DM])
        wf3 = sb("wf3", [P, FH])
        wp3 = sb("wp3", [P, HB, DM])
        low = sb("low", [P, FH])
        asum = sb("asum", [P, 2])
        bound = sb("bound", [P, 2])
        nbound = sb("nbound", [P, 2])
        ln_w = sb("ln_w", [P, HB])
        ln_b = sb("ln_b", [P, HB])

        xs = sb("xs", [P, 2, G, DM])
        xT = sb("xT", [P, 2, W])
        g = sb("g", [P, 2, G, FH])
        nT = sb("nT", [P, HB, W])
        y = sb("y", [P, 2, G, DM])
        ns = NormScratch(sb, "norm_h")
        ns2 = NormScratch(sb, "norm_x")

        loaded, chain = signals.loaded, signals.chain
        sums_ready = sem("sums_ready")
        sums_done = sem("sums_done")
        w_ready = sem("w_ready")
        xs_ready = sem("xs_ready")
        xT_done = sem("xT_done")
        xT_ready = sem("xT_ready")
        h_done = sem("h_done")
        g_ready = sem("g_ready")
        n_ready = sem("n_ready")
        nT_done = sem("nT_done")
        nT_ready = sem("nT_ready")
        y_done = sem("y_done")
        y_read = sem("y_read")
        y_ready = sem("y_ready")
        stored = [sem(f"stored{k}") for k in range(2)]

        signals.loads += 16 * 4
        with nc.Block() as block:
            @block.sync
            def _(sp):
                for dst, src in ((wf[:, :], "wf"), (wp[:, :, :], "wp"), (ln_w[:, :], "tm_ln_w"), (ln_b[:, :], "tm_ln_b")):
                    sp.dma_start(dst, d[src]).then_inc(loaded, 16)
                start_free(sp, nT_done, nT_ready, y_done, y_read)
                with sp.Fori(0, STEPS // 2) as m:
                    for hf in range(2):
                        s = 2 * m + hf
                        sp.wait_ge(y_ready, s + 1)
                        sp.dma_start(out[:, bass.ds(s * G, G), :], y[:, hf, :, :]).then_inc(stored[hf], 16)
                for hf in range(2):
                    sp.wait_ge(stored[hf], 16 * (STEPS // 2))

            @block.tensor
            def _(pe):
                pe.wait_ge(sums_ready, 1)
                nc.tensor.matmul(ps[:, 0, 0:2], ones[:, :], asum[:, :], start=True, stop=True).then_inc(sums_done, 1)
                pe.wait_ge(w_ready, 1)

                def front(s, hf):
                    pe.wait_ge(xs_ready, s + 1)
                    for t in range(G):
                        last = nc.tensor.transpose(ps[:, 0, t * P:(t + 1) * P], xs[:, hf, t, :], ident[:, :])
                    last.then_inc(xT_done, 1)
                    pe.wait_ge(xT_ready, s + 1)
                    for t in range(G):
                        pe.wait_ge(g_ready, 4 * s + max(t - 1, 0))
                        nc.tensor.matmul(ps[:, 1 + t % 2, :], xT[:, hf, t * P:(t + 1) * P], wf3[:, :],
                                         start=True, stop=True).then_inc(h_done, 1)

                def back(s, hf):
                    pe.wait_ge(n_ready, s + 1)
                    pe.wait_ge(nT_ready, FREE + 4 * s)
                    for k in range(HB):
                        for t in range(G):
                            last = nc.tensor.transpose(ps[:, 3 + k, t * P:(t + 1) * P], g[:, hf, t, k * P:(k + 1) * P],
                                                       ident[:, :])
                        last.then_inc(nT_done, 1)
                    pe.wait_ge(nT_ready, FREE + 4 * s + 4)
                    pe.wait_ge(y_read, FREE + s)
                    for t in range(G):
                        for k in range(HB):
                            last = nc.tensor.matmul(ps[:, 7, t * P:(t + 1) * P], nT[:, k, t * P:(t + 1) * P], wp3[:, k, :],
                                                    start=(k == 0), stop=(k == HB - 1))
                    last.then_inc(y_done, 1)

                front(0, 0)
                with pe.Fori(0, STEPS // 2 - 1) as m:
                    for hf in range(2):
                        front(2 * m + hf + 1, 1 - hf)
                        back(2 * m + hf, hf)
                front(STEPS - 1, 1)
                back(STEPS - 2, 0)
                back(STEPS - 1, 1)

            @block.scalar
            def _(act):
                act.wait_ge(loaded, signals.loads)

                def front(s, hf):
                    act.wait_ge(xT_done, s + 1)
                    nc.scalar.copy(xT[:, hf, :], ps[:, 0, :]).then_inc(xT_ready, 1)
                    if not isinstance(s, int) or s >= 2:
                        act.wait_ge(nT_done, FREE + 4 * (s - 1))
                    for t in range(G):
                        act.wait_ge(h_done, 4 * s + t + 1)
                        nc.scalar.activation(g[:, hf, t, :], ps[:, 1 + t % 2, :], ACT.Gelu).then_inc(g_ready, 1)

                def back(s, hf):
                    act.wait_ge(y_done, FREE + s)
                    for k in range(HB):
                        act.wait_ge(nT_done, FREE + 4 * s + k + 1)
                        nc.scalar.activation(nT[:, k, :], ps[:, 3 + k, :], ACT.Identity, bias=ln_b[:, k:k + 1],
                                             scale=ln_w[:, k:k + 1]).then_inc(nT_ready, 1)

                front(0, 0)
                with act.Fori(0, STEPS // 2 - 1) as m:
                    for hf in range(2):
                        front(2 * m + hf + 1, 1 - hf)
                        back(2 * m + hf, hf)
                front(STEPS - 1, 1)
                back(STEPS - 2, 0)
                back(STEPS - 1, 1)

            @block.vector
            def _(dve):
                link = Chain(dve, chain, signals.links)
                dve.wait_ge(loaded, signals.loads)
                nc.vector.tensor_reduce(asum[:, 0:1], wf[:, :], AX.X, ALU.add, apply_absolute_value=True)
                nc.vector.tensor_reduce(asum[:, 1:2], wp[:, :, :].rearrange("p k n -> p (k n)"), AX.X, ALU.add,
                                        apply_absolute_value=True).then_inc(sums_ready, 1)
                dve.wait_ge(sums_done, 1)
                link(nc.vector.tensor_scalar(bound[:, :], ps[:, 0, 0:2], 1.0 / (FH * DM), GAMMA_EPS, ALU.mult, ALU.add))
                link(nc.vector.tensor_scalar(bound[:, :], bound[:, :], 0.5, None, ALU.mult))
                link(nc.vector.tensor_scalar(nbound[:, :], bound[:, :], -1.0, None, ALU.mult))
                for n, (w, w3) in enumerate(((wf[:, :], wf3[:, :]),
                                             (wp[:, :, :].rearrange("p k n -> p (k n)"), wp3[:, :, :].rearrange("p k n -> p (k n)")))):
                    link(nc.vector.tensor_scalar(low[:, :], w, nbound[:, n:n + 1], None, ALU.is_lt))
                    link(nc.vector.scalar_tensor_tensor(out=w3, in0=w, scalar=bound[:, n:n + 1], in1=low[:, :],
                                                        op0=ALU.is_gt, op1=ALU.subtract))
                nc.vector.memset(low[:, 0:1], 0.0).then_inc(w_ready, 1)

                def x_now(s):
                    return x_all[:, bass.ds(s * G, G), :]

                def fetch(s, hf):
                    if not isinstance(s, int) or s >= 2:
                        dve.wait_ge(xT_done, s - 1)
                    nc.vector.tensor_copy(xs[:, hf, :, :], x_now(s)).then_inc(xs_ready, 1)

                def front(s, hf, step):
                    dve.wait_ge(g_ready, 4 * s + 4)
                    layer_norm(nc.vector, step, ns, lambda t: g[:, hf, t, :], lambda t: g[:, hf, t, :], EPS_LN, FH, done=n_ready)

                def back(m, hf, step):
                    s = 2 * m + hf
                    dve.wait_ge(y_done, FREE + s + 1)
                    dve.wait_ge(stored[hf], 16 * m)
                    nc.vector.tensor_tensor(y[:, hf, :, :], ps[:, 7, :].rearrange("p (t n) -> p t n", t=G), x_now(s), ALU.add)\
                        .then_inc(y_read, 1)
                    dve.wait_ge(y_read, FREE + s + 1)
                    layer_norm(nc.vector, step, ns2, lambda t: y[:, hf, t, :], lambda t: y[:, hf, t, :], EPS_LN, DM, done=y_ready)

                fetch(0, 0)
                fetch(1, 1)
                front(0, 0, link)
                fetch(2, 0)
                front(1, 1, link)
                back(0, 0, link)
                fetch(3, 1)
                front(2, 0, link)
                back(0, 1, link)
                with dve.Fori(1, STEPS // 2 - 1) as m:
                    step = Chain(dve, chain, link.start + link.count, m - 1, MLP_LINKS)
                    for hf in range(2):
                        fetch(2 * m + hf + 2, hf)
                        front(2 * m + hf + 1, 1 - hf, step)
                        back(m, hf, step)
                    step.end()
                link = Chain(dve, chain, link.start + link.count + (STEPS // 2 - 2) * MLP_LINKS)
                front(STEPS - 1, 1, link)
                back(STEPS // 2 - 1, 0, link)
                back(STEPS // 2 - 1, 1, link)


MLP_LINKS = 2 * 2 * (NORM_LINKS - 1)

def build(nc, d, out):
    with ExitStack() as ctx:
        def sb(name, shape, dt=F32):
            return ctx.enter_context(nc.sbuf_tensor(name, shape, dt))

        x_all = sb("x_all", [P, TILES, DM])
        tri = sb("tri", [P, P])
        past = sb("past", [P, P])
        ones = sb("ones", [P, P])
        ident = sb("ident", [P, P])
        signals = Signals(nc, ctx)
        with nc.Block() as block:
            @block.vector
            def _(dve):
                nc.vector.memset(ones[:, :], 1.0).then_inc(signals.set_up, 1)
                dve.wait_ge(signals.set_up, 1)
        mamba(nc, signals, x_all, tri, past, ones, ident, d)
        with ExitStack() as layer:
            v_all = layer.enter_context(nc.sbuf_tensor("v_all", [P, BATCH * SLOTS, TPB, 32], F32))
            o_all = layer.enter_context(nc.sbuf_tensor("o_all", [P, BATCH * SLOTS, TPB, 32], F32))
            q_dram = nc.dram_tensor("q_parts", (BATCH * SLOTS, SPLITS, 32, SEQ), BF16).ap()
            k_dram = nc.dram_tensor("k_parts", (BATCH * SLOTS, SPLITS, 32, SEQ), BF16).ap()
            latent_attention(nc, signals, x_all, ident, d, v_all, o_all, q_dram, k_dram)
            experts(nc, signals, x_all, ident, d, o_all)
        flow_attention(nc, signals, x_all, ones, ident, d)
        ternary_mlp(nc, signals, x_all, ones, ident, d, out)


def layouts(inp):
    f = {}
    x = np.asarray(inp["L0_attn_hidden_states"]).reshape(TOK, DM)
    f["x"] = np.ascontiguousarray(x.reshape(TILES, P, DM).transpose(1, 0, 2))
    f["xT"] = np.ascontiguousarray(x.T)
    f["w_in"] = np.asarray(inp["L0_attn_W_in"])
    f["conv_w"] = np.ascontiguousarray(np.asarray(inp["L0_attn_conv_w"]).reshape(NBLK, P, TAPS).transpose(1, 0, 2))
    f["conv_b"] = np.ascontiguousarray(np.asarray(inp["L0_attn_conv_b"]).reshape(NBLK, P).T)
    f["dcol"] = np.ascontiguousarray(np.repeat(np.asarray(inp["L0_attn_D"]), HD).reshape(ZB, P).T)
    f["rms_w"] = np.ascontiguousarray(np.asarray(inp["L0_attn_rms_w"]).reshape(ZB, P).T)
    f["w_out"] = np.ascontiguousarray(np.asarray(inp["L0_attn_W_out"]).reshape(ZB, P, DM).transpose(1, 0, 2))
    f["dt_bias"] = np.asarray(inp["L0_attn_dt_bias"])
    f["a_log"] = np.asarray(inp["L0_attn_A_log"])
    f["m_ln_g"] = np.asarray(inp["L0_attn_ln_g"])
    f["m_ln_b"] = np.asarray(inp["L0_attn_ln_b"])
    row, col = np.arange(P)[:, None], np.arange(P)[None, :]
    f["tri"] = (row <= col).astype(np.float32)
    f["past"] = (row > col).astype(np.float32)
    f["ident"] = np.eye(P, dtype=np.float32)
    f["norm1_w"] = np.asarray(inp["L0_ffn_norm1_w"])[:, None]
    swap = (np.arange(DM) // AD) * AD + (np.arange(DM) % AD + AD // 2) % AD
    wq = np.asarray(inp["L0_ffn_Wq"]).T
    f["wq"] = np.ascontiguousarray(np.stack([wq, wq[:, swap]], 1))
    f["wdkv"] = np.ascontiguousarray(np.asarray(inp["L0_ffn_Wdkv"]).T)
    wuk = np.asarray(inp["L0_ffn_Wuk"]).T
    f["wuk"] = np.ascontiguousarray(np.stack([wuk, wuk[:, swap]], 1))
    f["wuv"] = np.ascontiguousarray(np.asarray(inp["L0_ffn_Wuv"]).T)
    f["lat_g"] = np.asarray(inp["L0_ffn_ln_g"])[:, None]
    f["lat_b"] = np.asarray(inp["L0_ffn_ln_b"])[:, None]
    half = AD // 2
    inv_freq = (1.0 / 10000.0 ** (np.arange(half, dtype=np.float32) / half)).astype(np.float32)
    angle = (np.arange(SEQ, dtype=np.float32)[:, None] * inv_freq[None, :]).astype(np.float32)
    sign = np.where(np.arange(AD) < half, -1.0, 1.0)[:, None]
    f["cos"] = np.tile(np.cos(angle).T, (2 * AH, 1)).astype(np.float32)
    f["sin"] = np.tile(np.tile(np.sin(angle).T, (2, 1)) * sign, (AH, 1)).astype(np.float32)
    f["norm2_w"] = np.asarray(inp["L0_ffn_norm2_w"])[:, None]
    f["moe_wo"] = np.ascontiguousarray(np.asarray(inp["L0_ffn_Wo"]).T)
    f["gate_w"] = np.ascontiguousarray(np.asarray(inp["L0_ffn_gate_w"]).T)
    f["gate_b"] = np.asarray(inp["L0_ffn_gate_b"])
    f["moe_w1"] = np.ascontiguousarray(np.asarray(inp["L0_ffn_W1"]).transpose(2, 0, 1))
    f["moe_b1"] = np.ascontiguousarray(np.asarray(inp["L0_ffn_b1"]).reshape(NE, HID // P, P).transpose(2, 0, 1))
    f["moe_w2"] = np.ascontiguousarray(
        np.asarray(inp["L0_ffn_W2"]).transpose(0, 2, 1).reshape(NE, HID // P, P, DM).transpose(2, 0, 1, 3))
    b2 = np.zeros((G, NE, G, DM), np.float32)
    for t in range(G):
        b2[t, :, t, :] = np.asarray(inp["L0_ffn_b2"])
    f["moe_b2"] = b2.reshape(G * NE, G * DM)
    f["order"] = np.tile(np.arange(NE, 0, -1, dtype=np.float32), (P, 1))
    for n, key in (("fl_wq", "Wq"), ("fl_wk", "Wk"), ("fl_wv", "Wv"), ("fl_wo", "Wo")):
        f[n] = np.asarray(inp["L1_attn_" + key])
    f["fl_bq"] = np.asarray(inp["L1_attn_bq"])[:, None]
    f["fl_bk"] = np.asarray(inp["L1_attn_bk"])[:, None]
    f["fl_bv"] = np.asarray(inp["L1_attn_bv"])
    f["fl_bo"] = np.asarray(inp["L1_attn_bo"])
    f["head"] = (row // AD == np.arange(AH)[None, :]).astype(np.float32)
    f["same"] = (row // AD == col // AD).astype(np.float32)
    f["wf"] = np.ascontiguousarray(np.asarray(inp["L1_ffn_W_fc"]).T)
    f["wp"] = np.ascontiguousarray(np.asarray(inp["L1_ffn_W_proj"]).T.reshape(FH // P, P, DM).transpose(1, 0, 2))
    f["tm_ln_w"] = np.ascontiguousarray(np.asarray(inp["L1_ffn_ln_w"]).reshape(FH // P, P).T)
    f["tm_ln_b"] = np.ascontiguousarray(np.asarray(inp["L1_ffn_ln_b"]).reshape(FH // P, P).T)
    bf16 = mybir.dt.np(BF16)
    f["identb"] = np.eye(P).astype(bf16)
    f["mask_q"] = np.where(col > row, MASKED, 0.0).astype(bf16)
    f["mask_k"] = np.where(row > col, MASKED, 0.0).astype(bf16)
    f["pad"] = np.repeat((np.arange(STACK - SROWS) >= SHIFT_ROW - SROWS), 4 * SEQ).reshape(-1, 4, SEQ).astype(bf16)
    return f


def kernel(**inputs):
    import concourse.bacc as bacc
    from concourse.bass_utils import run_bass_kernel_spmd

    nc = bacc.Bacc("TRN2", target_bir_lowering=False, num_devices=1)
    arrays = layouts(inputs)
    d = {n: nc.dram_tensor("in_" + n, a.shape, mybir.dt.from_np(a.dtype), kind="ExternalInput").ap() for n, a in arrays.items()}
    out = nc.dram_tensor("out", (P, TILES, DM), F32, kind="ExternalOutput").ap()
    build(nc, d, out)
    res = run_bass_kernel_spmd(nc, [{"in_" + n: a for n, a in arrays.items()}], core_ids=[0]).results[0]["out"]
    return res.transpose(1, 0, 2).reshape(BATCH, SEQ, DM)
```

```python
from contextlib import ExitStack

import numpy as np
import concourse.bass as bass
from concourse import mybir

F32 = mybir.dt.float32
BF16 = mybir.dt.bfloat16
I32 = mybir.dt.int32
ACT = mybir.ActivationFunctionType
ALU = mybir.AluOpType
AX = mybir.AxisListType

P = 128
BATCH, SEQ, DM = 4, 1024, 128
TOK = BATCH * SEQ
TILES = TOK // P
TPB = SEQ // P
G = 4
W = G * P

DIN, NST, NH, HD, TAPS = 256, 128, 4, 64, 4
NBLK = (DIN + 2 * NST) // P
ZB = DIN // P
EPS_RMS, EPS_LN = 1e-5, 1e-5

AH, AD, LAT, NE, HID = 16, 8, 64, 4, 512
EPS_RMS2 = 1e-6
SPLITS = 3
SROWS = SPLITS * SPLITS * AD
SHIFT_ROW = 96
MASKED = -1e30

FLOW_EPS = 1e-6
FH = 512
GAMMA_EPS = 1e-6

FREE = 2
MAGIC = 1597463007.0


class Chain:

    def __init__(self, eng, sem, start=0, step=0, per=0):
        self.eng, self.sem, self.start, self.before, self.per = eng, sem, start, start + step * per, per
        self.count = 0

    def __call__(self, instruction):
        self.count += 1
        instruction.then_inc(self.sem, 1)
        self.eng.wait_ge(self.sem, self.before + self.count)

    def end(self):
        assert self.count == self.per, (self.count, self.per)


class Signals:

    def __init__(self, nc, ctx):
        self.nc, self.ctx = nc, ctx
        self.loaded, self.chain = self.new("loaded"), self.new("chain")
        self.loads = self.links = 0
        self.set_up = self.new("set_up")

    def new(self, name):
        return self.ctx.enter_context(self.nc.semaphore(name))


def start_free(eng, *sems):
    for s in sems:
        eng.sem_inc(s, FREE)


def inverse_root(eng, link, v, y, t, h):
    link(eng.tensor_scalar(y.bitcast(I32), v.bitcast(I32), -0.5, MAGIC, ALU.mult, ALU.add))
    link(eng.tensor_tensor(h, v, y, ALU.mult))
    for k in range(3):
        link(eng.scalar_tensor_tensor(out=t, in0=h, scalar=-0.5, in1=y, op0=ALU.mult, op1=ALU.mult))
        if k < 2:
            eng.scalar_tensor_tensor(out=h, in0=t, scalar=1.5, in1=h, op0=ALU.add, op1=ALU.mult)
        link(eng.scalar_tensor_tensor(out=y, in0=t, scalar=1.5, in1=y, op0=ALU.add, op1=ALU.mult))


ROOT_LINKS = 8


class NormScratch:

    def __init__(self, sb, name, n=G):
        self.n = n
        self.st = sb(name + "_stats", [P, n, 6], F32)
        self.sum = sb(name + "_sum", [P, n], F32)
        self.dif = sb(name + "_dif", [P, n], F32)
        self.m2 = sb(name + "_m2", [P, n], F32)
        self.v = sb(name + "_var", [P, n], F32)
        self.y = sb(name + "_rstd", [P, n], F32)
        self.t = sb(name + "_t", [P, n], F32)
        self.h = sb(name + "_h", [P, n], F32)
        self.b = sb(name + "_shift", [P, n], F32)


NORM_LINKS = 4 + ROOT_LINKS + 2


def layer_norm(eng, link, s, src, dst, eps, width, n=G, done=None):
    for k in range(n):
        last = eng.bn_stats(s.st[:, k, :], src(k))
    link(last)
    norm_scales(eng, link, s, eps, width)
    for k in range(n):
        last = eng.tensor_scalar(dst(k), src(k), s.y[:, k:k + 1], s.b[:, k:k + 1], ALU.mult, ALU.add)
    if done is None:
        link(last)
    else:
        last.then_inc(done, 1)


def norm_scales(eng, link, s, eps, *widths):
    n = s.n // len(widths)
    eng.tensor_tensor(s.sum[:, :], s.st[:, :, 1], s.st[:, :, 4], ALU.add)
    eng.tensor_tensor(s.dif[:, :], s.st[:, :, 1], s.st[:, :, 4], ALU.subtract)
    for k, width in enumerate(widths):
        last = eng.scalar_tensor_tensor(out=s.m2[:, k * n:(k + 1) * n], in0=s.st[:, k * n:(k + 1) * n, 2],
                                        scalar=eps * width, in1=s.st[:, k * n:(k + 1) * n, 5], op0=ALU.add, op1=ALU.add)
    link(last)
    link(eng.scalar_tensor_tensor(out=s.dif[:, :], in0=s.dif[:, :], scalar=0.25, in1=s.dif[:, :],
                                  op0=ALU.mult, op1=ALU.mult))
    for k, width in enumerate(widths):
        sl = slice(k * n, (k + 1) * n)
        last = eng.scalar_tensor_tensor(out=s.v[:, sl], in0=s.m2[:, sl], scalar=1.0 / width, in1=s.dif[:, sl],
                                        op0=ALU.mult, op1=ALU.add)
    link(last)
    inverse_root(eng, link, s.v[:, :], s.y[:, :], s.t[:, :], s.h[:, :])
    link(eng.scalar_tensor_tensor(out=s.b[:, :], in0=s.sum[:, :], scalar=-0.5, in1=s.y[:, :],
                                  op0=ALU.mult, op1=ALU.mult))


def mamba(nc, signals, x_all, tri, past, ones, ident, d):
    with ExitStack() as ctx:
        def sb(name, shape, dt=F32):
            return ctx.enter_context(nc.sbuf_tensor(name, shape, dt))

        def sem(name):
            return signals.new(name)

        ps = ctx.enter_context(nc.psum_tensor("mamba_psum", [P, 8, 512], F32))
        proj = [ps[:, 0, :], ps[:, 1, :]]
        outp = ps[:, 0, :].rearrange("p (b n) -> p b n", b=G)
        ssp = ps[:, 1, 0:G]
        decp = ps[:, 2:4, :]
        xtokp = ps[:, 4:6, :].rearrange("p k (b n) -> p (k b) n", n=DIN)
        yp = ps[:, 4:6, :].rearrange("p k (b l) -> p k b l", b=G)
        btokp = ps[:, 6, :]
        scorep = ps[:, 7, :]
        newp = ps[:, 6:8, :].rearrange("p k (b n) -> p (k b) n", n=DIN)

        xT = sb("xT", [P, TOK])
        xTb = xT[:, :].rearrange("p (b l) -> p b l", b=BATCH)
        w_in = sb("w_in", [P, 2 * DIN + 2 * NST])
        w_dt = sb("w_dt", [P, 32])
        dtT = sb("dtT", [P, SEQ])
        conv_w = sb("conv_w", [P, NBLK, TAPS])
        conv_b = sb("conv_b", [P, NBLK])
        dcol = sb("dcol", [P, ZB])
        rms_w = sb("rms_w", [P, ZB])
        w_out = sb("w_out", [P, ZB, DM])
        dt_bias = sb("dt_bias", [P, NH])
        a_log = sb("a_log", [P, NH])
        ln_g = sb("ln_g", [P, DM])
        ln_b = sb("ln_b", [P, DM])

        u = sb("u", [P, TILES, NH])
        au = sb("au", [P, TILES, NH])
        dt = sb("dt", [P, TILES, NH])
        ada = sb("ada", [P, TILES, NH])
        carry = sb("carry", [P, 2, TILES, NH])

        pre = sb("pre", [P, NBLK, BATCH, TAPS - 1 + P])
        cv = sb("cv", [P, NBLK, W])
        xbc = sb("xbc", [P, 2, NBLK, W])
        zs = sb("zs", [P, 2, ZB, W])
        ta = sb("ta", [P, 2, NH, P])
        le = sb("le", [P, 2, 2, NH, P])
        mm = sb("mm", [P, 2, NH, P])
        ce = sb("ce", [P, 2, NH, P])
        xdt = sb("xdt", [P, BATCH, DIN])
        xdd = sb("xdd", [P, BATCH, DIN])
        btok = sb("btok", [P, BATCH, NST])
        sm = sb("sm", [P, BATCH, P])
        state = sb("state", [P, BATCH, DIN])
        yg = sb("yg", [P, ZB, W])
        sq = sb("sq", [P, ZB, W])
        xb = sb("xb", [P, TILES, DM])
        h = sb("h", [P, TILES, DM])
        square = sb("square", [P, TILES])
        r = sb("r", [P, TILES])
        rv = sb("rv", [P, TILES])
        rt = sb("rt", [P, TILES])
        rh = sb("rh", [P, TILES])
        nmean = sb("nmean", [P, TILES])
        ns = NormScratch(sb, "mnorm", TILES)

        loaded, chain = signals.loaded, signals.chain
        first_loaded, x_loaded = sem("first_loaded"), sem("x_loaded")
        dt_heads = sem("dt_heads")
        dt_copied = sem("dt_copied")
        dt_raw = sem("dt_raw")
        e_abs = sem("e_abs")
        dt_act = sem("dt_act")
        dt_ready = sem("dt_ready")
        carry_sum = sem("carry_sum")
        carry_ready = sem("carry_ready")
        proj_done = sem("proj_done")
        proj_read = sem("proj_read")
        tail_kept = sem("tail_kept")
        conv_done = sem("conv_done")
        xbc_ready = sem("xbc_ready")
        ta_ready = sem("ta_ready")
        dec_done = sem("dec_done")
        dec_exp = sem("dec_exp")
        mix_ready = sem("mix_ready")
        xtok_done = sem("xtok_done")
        btok_done = sem("btok_done")
        score_done = sem("score_done")
        xdt_ready = sem("xdt_ready")
        xdd_ready = sem("xdd_ready")
        btok_ready = sem("btok_ready")
        sm_ready = sem("sm_ready")
        y_done = sem("y_done")
        new_done = sem("new_done")
        state_ready = sem("state_ready")
        yg_ready = sem("yg_ready")
        sq_ready = sem("sq_ready")
        ss_done = sem("ss_done")
        out_done = sem("out_done")
        out_read = sem("out_read")
        xb_ready = sem("xb_ready")
        scales_ready = sem("scales_ready")
        act_chain = sem("mamba_act_chain")

        with nc.Block() as block:
            @block.sync
            def _(sp):
                sp.dma_start(w_in[:, :], d["w_in"]).then_inc(first_loaded, 16)
                sp.dma_start(xT[:, :], d["xT"]).then_inc(first_loaded, 16)
                sp.dma_start(w_dt[:, :], d["w_dt"]).then_inc(first_loaded, 16)
                sp.wait_ge(first_loaded, 48)
                sp.dma_start(x_all[:, :, :], d["x"]).then_inc(x_loaded, 16)

                start_free(sp, dec_done, dec_exp, mix_ready, new_done, out_done, out_read, ss_done, xbc_ready,
                           xdd_ready, y_done, yg_ready)

            ALL = signals.loads = 16 * 12

            @block.tensor
            def _(pe):
                pe.wait_ge(first_loaded, 48)
                for k in range(SEQ // 512):
                    for b in range(BATCH):
                        last = nc.tensor.matmul(ps[32 * b:32 * b + 32, 4 + k, :], w_dt[:, :],
                                                xTb[:, b, k * 512:(k + 1) * 512], start=True, stop=True)
                last.then_inc(dt_heads, 1)

                def project(i, n):
                    col = DIN + n * P if n < NBLK else (n - NBLK) * P
                    if not (isinstance(i, int) and i == 0 and n < 2):
                        pe.wait_ge(proj_read, 6 * i + n - 1)
                    if n < 2 and not isinstance(i, int):
                        pe.wait_ge(out_read, FREE + i - 1)
                    elif n < 2 and i >= 2:
                        pe.wait_ge(out_read, FREE + i - 1)
                    nc.tensor.matmul(proj[n % 2], w_in[:, col:col + P], xTb[:, :, bass.ds(i * P, P)],
                                     start=True, stop=True).then_inc(proj_done, 1)

                def decays(i, b):
                    pe.wait_ge(ta_ready, 4 * i + b + 1)
                    pe.wait_ge(dec_exp, FREE + 4 * i + b)
                    rhs = ta[:, b % 2, :, :]
                    nc.tensor.matmul(decp[:, 0, :], past[:, :], rhs, start=True, stop=True)
                    nc.tensor.matmul(decp[:, 1, :], ones[:, :], rhs, start=True, stop=True).then_inc(dec_done, 1)

                def step(i, p, more=True):
                    pe.wait_ge(yg_ready, FREE + i)
                    for k in range(ZB):
                        pe.wait_ge(xbc_ready, FREE + 4 * i + k + 1)
                        for b in range(BATCH):
                            last = nc.tensor.transpose(xtokp[:, b, k * P:(k + 1) * P], xbc[:, p, k, b * P:(b + 1) * P],
                                                       ident[:, :])
                    last.then_inc(xtok_done, 1)
                    pe.wait_ge(state_ready, i + 1)
                    pe.wait_ge(xbc_ready, FREE + 4 * i + 3)
                    for b in range(BATCH):
                        last = nc.tensor.transpose(btokp[:, b * P:(b + 1) * P], xbc[:, p, 2, b * P:(b + 1) * P],
                                                   ident[:, :])
                    last.then_inc(btok_done, 1)
                    pe.wait_ge(xbc_ready, FREE + 4 * i + 4)
                    for b in range(BATCH):
                        last = nc.tensor.matmul(scorep[:, b * P:(b + 1) * P], xbc[:, p, 2, b * P:(b + 1) * P],
                                                xbc[:, p, 3, b * P:(b + 1) * P], start=True, stop=True)
                    last.then_inc(score_done, 1)
                    for b in range(BATCH):
                        if b + 1 < BATCH:
                            decays(i, b + 1)
                        if more:
                            project(i + 1, b)
                        if b == 0:
                            pe.wait_ge(xdt_ready, i + 1)
                        pe.wait_ge(mix_ready, FREE + 4 * i + b + 1)
                        for hh in range(NH):
                            out = yp[HD * (hh % 2):HD * (hh % 2) + HD, hh // 2, b, :]
                            nc.tensor.matmul(out, xdt[:, b, hh * HD:(hh + 1) * HD], mm[:, b % 2, hh, :],
                                             start=True, stop=False)
                            last = nc.tensor.matmul(out, state[:, b, hh * HD:(hh + 1) * HD], ce[:, b % 2, hh, :],
                                                    start=False, stop=True)
                        last.then_inc(y_done, 1)
                    pe.wait_ge(btok_ready, i + 1)
                    pe.wait_ge(sm_ready, i + 1)
                    pe.wait_ge(xdd_ready, FREE + i + 1)
                    for b in range(BATCH):
                        last = nc.tensor.matmul(newp[:, b, :], btok[:, b, :], xdd[:, b, :], start=True, stop=True)
                    last.then_inc(new_done, 1)
                    if more:
                        for n in range(NBLK, NBLK + ZB):
                            project(i + 1, n)
                        decays(i + 1, 0)
                    pe.wait_ge(sq_ready, 2 * i + 2)
                    pe.wait_ge(proj_read, 6 * i + (12 if more else 6))
                    for b in range(BATCH):
                        for k in range(ZB):
                            last = nc.tensor.matmul(ssp[:, b:b + 1], sq[:, k, b * P:(b + 1) * P], ones[:, 0:1],
                                                    start=(k == 0), stop=(k == ZB - 1))
                    last.then_inc(ss_done, 1)
                    for b in range(BATCH):
                        for k in range(ZB):
                            last = nc.tensor.matmul(outp[:, b, :], yg[:, k, b * P:(b + 1) * P], w_out[:, k, :],
                                                    start=(k == 0), stop=(k == ZB - 1))
                    last.then_inc(out_done, 1)

                for n in range(NBLK):
                    project(0, n)
                pe.wait_ge(loaded, ALL)
                pe.wait_ge(dt_copied, 1)
                for c in range(TPB):
                    last = nc.tensor.transpose(ps[:, 6 + c // 4, c % 4 * P:(c % 4 + 1) * P], dtT[:, c * P:(c + 1) * P],
                                               ident[:, :])
                last.then_inc(dt_raw, 1)
                pe.wait_ge(dt_ready, 1)
                pe.wait_ge(loaded, ALL)
                flat = ada[:, :, :].rearrange("p t h -> p (t h)")
                nc.tensor.matmul(ps[:, 5, 0:P], past[:, :], flat, start=True, stop=True)
                nc.tensor.matmul(ps[:, 5, P:2 * P], ones[:, :], flat, start=True, stop=True).then_inc(carry_sum, 1)
                for n in range(NBLK, NBLK + ZB):
                    project(0, n)
                decays(0, 0)
                with pe.Fori(0, TPB // 2 - 1) as m:
                    for p in range(2):
                        step(2 * m + p, p)
                step(TPB - 2, 0)
                step(TPB - 1, 1, more=False)

            @block.scalar
            def _(act):
                for dst, src in ((dt_bias, d["dt_bias"]), (a_log, d["a_log"]), (ln_g, d["m_ln_g"]),
                                 (ln_b, d["m_ln_b"])):
                    act.dma_start(dst[:, :], src.partition_broadcast(P)).then_inc(loaded, 16)
                for dst, src in ((tri[:, :], d["tri"]), (past[:, :], d["past"]), (ident[:, :], d["ident"]),
                                 (conv_w[:, :, :], d["conv_w"]), (conv_b[:, :], d["conv_b"]),
                                 (dcol[:, :], d["dcol"]), (rms_w[:, :], d["rms_w"]),
                                 (w_out[:, :, :], d["w_out"])):
                    act.dma_start(dst, src).then_inc(loaded, 16)

                def copy_in(i, n):
                    if n == 0:
                        act.wait_ge(tail_kept, i + 1)
                    act.wait_ge(proj_done, 6 * i + n + 1)
                    nc.scalar.copy(pre[:, n, :, TAPS - 1:], proj[n % 2].rearrange("p (b l) -> p b l", b=BATCH))\
                        .then_inc(proj_read, 1)

                def gate(i, p):
                    for n in range(ZB):
                        act.wait_ge(proj_done, 6 * i + NBLK + n + 1)
                        nc.scalar.activation(zs[:, p, n, :], proj[(NBLK + n) % 2], ACT.Silu).then_inc(proj_read, 1)

                def silu(i, p, n):
                    act.wait_ge(conv_done, 4 * i + n + 1)
                    nc.scalar.activation(xbc[:, p, n, :], cv[:, n, :], ACT.Silu, bias=conv_b[:, n:n + 1])\
                        .then_inc(xbc_ready, 1)

                def keep_tail():
                    nc.scalar.copy(pre[:, :, :, 0:TAPS - 1], pre[:, :, :, P:P + TAPS - 1]).then_inc(tail_kept, 1)

                def decay(i, b):
                    act.wait_ge(dec_done, FREE + 4 * i + b + 1)
                    act.wait_ge(mix_ready, FREE + 4 * i + max(b - 1, 0))
                    nc.scalar.activation(le[:, b % 2, :, :, :].rearrange("p k h l -> p k (h l)"), decp, ACT.Exp)\
                        .then_inc(dec_exp, 1)

                def step(i, p, more=True):
                    decay(i, 0)
                    act.wait_ge(btok_done, i + 1)
                    act.wait_ge(new_done, FREE + i)
                    nc.scalar.copy(btok[:, :, :].rearrange("p b n -> p (b n)"), btokp).then_inc(btok_ready, 1)
                    for b in range(1, BATCH):
                        decay(i, b)
                        if more:
                            copy_in(i + 1, b - 1)
                    if more:
                        copy_in(i + 1, BATCH - 1)
                        act.wait_ge(yg_ready, FREE + i)
                        gate(i + 1, 1 - p)
                        for n in (0, 1):
                            silu(i + 1, 1 - p, n)
                    act.wait_ge(yg_ready, FREE + i + 1)
                    act.wait_ge(ss_done, FREE + i)
                    for k in range(ZB):
                        nc.scalar.activation(sq[:, k, :], yg[:, k, :], ACT.Square).then_inc(sq_ready, 1)
                    if more:
                        for n in (2, 3):
                            silu(i + 1, 1 - p, n)
                        keep_tail()
                    act.wait_ge(ss_done, FREE + i + 1)
                    nc.scalar.copy(square[:, :].rearrange("p (b c) -> p b c", b=BATCH)[:, :, bass.ds(i, 1)]
                                   .rearrange("p b c -> p (b c)"), ssp)
                    act.wait_ge(out_done, FREE + i + 1)
                    nc.scalar.copy(h[:, :, :].rearrange("p (b c) n -> p b (c n)", b=BATCH)[:, :, bass.ds(i * DM, DM)], outp)\
                        .then_inc(out_read, 1)

                act.wait_ge(dt_heads, 1)
                nc.scalar.copy(dtT[:, :], ps[:, 4:6, :].rearrange("p k n -> p (k n)")).then_inc(dt_copied, 1)
                for n in range(NBLK):
                    copy_in(0, n)
                act.wait_ge(loaded, ALL)
                nc.scalar.activation(a_log[:, :], a_log[:, :], ACT.Exp).then_inc(dt_act, 1)
                act.wait_ge(e_abs, 1)
                nc.scalar.activation(au[:, :, :], au[:, :, :], ACT.Exp, scale=-1.0).then_inc(act_chain, 1)
                act.wait_ge(act_chain, 1)
                nc.scalar.activation(au[:, :, :], au[:, :, :], ACT.Ln, bias=ones[:, 0:1]).then_inc(dt_act, 1)
                act.wait_ge(carry_sum, 1)
                nc.scalar.activation(carry[:, :, :, :].rearrange("p a t h -> p (a t h)"), ps[:, 5, 0:2 * P],
                                     ACT.Exp).then_inc(carry_ready, 1)
                gate(0, 0)
                for n in range(NBLK):
                    silu(0, 0, n)
                keep_tail()
                with act.Fori(0, TPB // 2 - 1) as m:
                    for p in range(2):
                        step(2 * m + p, p)
                step(TPB - 2, 0)
                step(TPB - 1, 1, more=False)
                act.wait_ge(scales_ready, 1)
                for k in range(TILES // 2, TILES):
                    nc.scalar.activation(x_all[:, k, :], h[:, k, :], ACT.Identity, bias=ns.b[:, k:k + 1],
                                         scale=ns.y[:, k:k + 1])

            @block.gpsimd
            def _(pool):
                nc.gpsimd.memset(pre[:, :, :, 0:TAPS - 1], 0.0).then_inc(tail_kept, 1)
                pool.wait_ge(loaded, ALL)
                pool.wait_ge(x_loaded, 16)
                nc.gpsimd.tensor_tensor(xb[:, :, :], x_all[:, :, :], ln_b[:, :].unsqueeze(1).to_broadcast([P, TILES, DM]),
                                        ALU.add).then_inc(xb_ready, 1)
                pool.wait_ge(dt_ready, 1)
                pool.wait_ge(carry_ready, 1)
                with pool.Fori(0, TPB) as i:
                    def spread(b):
                        pool.wait_ge(dec_done, FREE + 4 * i + max(b - 1, 0))
                        nc.gpsimd.tensor_tensor(
                            ta[:, b % 2, :, :], tri[:, :].unsqueeze(1).to_broadcast([P, NH, P]),
                            ada[:, bass.ds(i + b * TPB, 1), :].rearrange("p t h -> p (t h)").unsqueeze(2)
                            .to_broadcast([P, NH, P]), ALU.mult).then_inc(ta_ready, 1)

                    spread(0)
                    spread(1)
                    pool.wait_ge(xdt_ready, i + 1)
                    pool.wait_ge(new_done, FREE + i)
                    for b in range(BATCH):
                        last = nc.gpsimd.tensor_tensor(
                            xdd[:, b, :].rearrange("p (h n) -> p h n", h=NH), xdt[:, b, :].rearrange("p (h n) -> p h n", h=NH),
                            carry[:, 0, bass.ds(i + b * TPB, 1), :].rearrange("p t h -> p (t h)").unsqueeze(2)
                            .to_broadcast([P, NH, HD]), ALU.mult)
                    last.then_inc(xdd_ready, 1)
                    spread(2)
                    spread(3)

            @block.vector
            def _(dve):
                dve.wait_ge(loaded, ALL)
                nc.vector.memset(state[:, :, :], 0.0).then_inc(state_ready, 1)
                link = Chain(dve, chain)

                def convolve(i, link):
                    dve.wait_ge(tail_kept, i + 1)
                    dve.wait_ge(xbc_ready, FREE + 4 * i)
                    for pair in (0, 2):
                        for tap in range(TAPS):
                            for n in (pair, pair + 1):
                                o = cv[:, n, :].rearrange("p (b l) -> p b l", b=BATCH)
                                src = pre[:, n, :, tap:tap + P]
                                w = conv_w[:, n, tap:tap + 1]
                                if tap == 0:
                                    dve.wait_ge(proj_read, 6 * i + n + 1)
                                    op = nc.vector.tensor_scalar(o, src, w, None, ALU.mult)
                                else:
                                    op = nc.vector.scalar_tensor_tensor(out=o, in0=src, scalar=w, in1=o,
                                                                        op0=ALU.mult, op1=ALU.add)
                                if tap == TAPS - 1:
                                    op.then_inc(conv_done, 1)
                                elif n == pair + 1:
                                    link(op)
                            yield

                def step(i, p, link, more=True):
                    dve.wait_ge(xtok_done, i + 1)
                    dve.wait_ge(y_done, FREE + 4 * i)
                    dve.wait_ge(xdd_ready, FREE + i)
                    for b in range(BATCH):
                        last = nc.vector.tensor_tensor(
                            xdt[:, b, :].rearrange("p (h n) -> p h n", h=NH), xtokp[:, b, :].rearrange("p (h n) -> p h n", h=NH),
                            dt[:, bass.ds(i + b * TPB, 1), :].rearrange("p t h -> p (t h)").unsqueeze(2)
                            .to_broadcast([P, NH, HD]), ALU.mult)
                    last.then_inc(xdt_ready, 1)
                    dve.wait_ge(score_done, i + 1)
                    nc.vector.tensor_tensor(sm[:, :, :], scorep.rearrange("p (b l) -> p b l", b=BATCH),
                                            tri[:, :].unsqueeze(1).to_broadcast([P, BATCH, P]), ALU.mult)\
                        .then_inc(sm_ready, 1)
                    dve.wait_ge(sm_ready, i + 1)
                    ahead = convolve(i + 1, link) if more else iter(())
                    for b in range(BATCH):
                        dve.wait_ge(dec_exp, FREE + 4 * i + b + 1)
                        dve.wait_ge(y_done, FREE + 4 * i + max(b - 1, 0))
                        nc.vector.tensor_tensor(mm[:, b % 2, :, :], le[:, b % 2, 0, :, :],
                                                sm[:, b, :].unsqueeze(1).to_broadcast([P, NH, P]), ALU.mult)
                        nc.vector.tensor_tensor(ce[:, b % 2, :, :], le[:, b % 2, 1, :, :],
                                                xbc[:, p, 3, b * P:(b + 1) * P].unsqueeze(1).to_broadcast([P, NH, P]),
                                                ALU.mult).then_inc(mix_ready, 1)
                        for _ in range(CONV_AT[b]):
                            next(ahead, None)
                    dve.wait_ge(y_done, FREE + 4 * i + 4)
                    dve.wait_ge(out_done, FREE + i)
                    for k in range(ZB):
                        last = nc.vector.scalar_tensor_tensor(
                            out=yg[:, k, :], in0=xbc[:, p, k, :], scalar=dcol[:, k:k + 1],
                            in1=yp[:, k, :, :].rearrange("p b l -> p (b l)"), op0=ALU.mult, op1=ALU.add)
                    link(last)
                    nc.vector.tensor_tensor(yg[:, :, :], yg[:, :, :], zs[:, p, :, :], ALU.mult).then_inc(yg_ready, 1)
                    dve.wait_ge(new_done, FREE + i + 1)
                    for b in range(BATCH):
                        last = nc.vector.tensor_tensor(
                            state[:, b, :].rearrange("p (h n) -> p h n", h=NH), state[:, b, :].rearrange("p (h n) -> p h n", h=NH),
                            carry[:, 1, bass.ds(i + b * TPB, 1), :].rearrange("p t h -> p (t h)").unsqueeze(2)
                            .to_broadcast([P, NH, HD]), ALU.mult)
                    link(last)
                    nc.vector.tensor_tensor(state[:, :, :], state[:, :, :], newp, ALU.add).then_inc(state_ready, 1)
                    for _ in ahead:
                        pass

                conv = convolve(0, link)
                next(conv)
                dve.wait_ge(dt_raw, 1)
                raw = ps[:, 6:8, :].rearrange("p k (c b m) -> p b (k c) m", c=4, b=BATCH)
                for b in range(BATCH):
                    last = nc.vector.tensor_tensor(u[:, b * TPB:(b + 1) * TPB, :], raw[:, b, :, 0:NH],
                                                   dt_bias[:, :].unsqueeze(1).to_broadcast([P, TPB, NH]), ALU.add)
                link(last)
                nc.vector.scalar_tensor_tensor(out=au[:, :, :], in0=u[:, :, :], scalar=-1.0, in1=u[:, :, :],
                                               op0=ALU.mult, op1=ALU.max).then_inc(e_abs, 1)
                link(nc.vector.tensor_tensor(w_out[:, :, :], w_out[:, :, :],
                                             rms_w[:, :].unsqueeze(2).to_broadcast([P, ZB, DM]), ALU.mult))
                for _ in range(DT_CONV):
                    next(conv)
                dve.wait_ge(dt_act, 2)
                link(nc.vector.scalar_tensor_tensor(out=dt[:, :, :], in0=u[:, :, :], scalar=0.0, in1=au[:, :, :],
                                                    op0=ALU.max, op1=ALU.add))
                nc.vector.scalar_tensor_tensor(out=ada[:, :, :], in0=dt[:, :, :], scalar=-1.0,
                                               in1=a_log[:, :].unsqueeze(1).to_broadcast([P, TILES, NH]),
                                               op0=ALU.mult, op1=ALU.mult).then_inc(dt_ready, 1)
                for _ in conv:
                    pass
                dve.wait_ge(carry_ready, 1)
                with dve.Fori(0, TPB // 2 - 1) as m:
                    looped = Chain(dve, chain, link.count, m, 2 * MAMBA_LINKS)
                    for p in range(2):
                        step(2 * m + p, p, looped)
                    looped.end()
                link = Chain(dve, chain, link.count + (TPB // 2 - 1) * 2 * MAMBA_LINKS)
                step(TPB - 2, 0, link)
                step(TPB - 1, 1, link, more=False)

                every = range(TILES)
                dve.wait_ge(x_loaded, 16)
                dve.wait_ge(out_read, FREE + TPB)
                link(nc.vector.tensor_scalar(rv[:, :], square[:, :], 1.0 / DIN, EPS_RMS, ALU.mult, ALU.add))
                inverse_root(nc.vector, link, rv[:, :], r[:, :], rt[:, :], rh[:, :])
                for k in every:
                    last = nc.vector.scalar_tensor_tensor(out=h[:, k, :], in0=h[:, k, :], scalar=r[:, k:k + 1],
                                                          in1=x_all[:, k, :], op0=ALU.mult, op1=ALU.add)
                link(last)
                for k in every:
                    last = nc.vector.bn_stats(ns.st[:, k, :], h[:, k, :])
                link(last)
                norm_scales(nc.vector, link, ns, EPS_LN, DM)
                link(nc.vector.tensor_scalar(nmean[:, :], ns.sum[:, :], -0.5, None, ALU.mult))
                dve.wait_ge(xb_ready, 1)
                for k in every:
                    last = nc.vector.scalar_tensor_tensor(out=h[:, k, :], in0=h[:, k, :], scalar=nmean[:, k:k + 1],
                                                          in1=ln_g[:, :], op0=ALU.add, op1=ALU.mult)
                link(last)
                for k in every:
                    last = nc.vector.scalar_tensor_tensor(out=h[:, k, :], in0=h[:, k, :], scalar=ns.y[:, k:k + 1],
                                                          in1=xb[:, k, :], op0=ALU.mult, op1=ALU.add)
                link(last)
                for k in every:
                    last = nc.vector.bn_stats(ns.st[:, k, :], h[:, k, :])
                link(last)
                norm_scales(nc.vector, link, ns, EPS_LN, DM)
                nc.vector.memset(nmean[:, 0:1], 0.0).then_inc(scales_ready, 1)
                for k in range(TILES // 2):
                    nc.vector.tensor_scalar(x_all[:, k, :], h[:, k, :], ns.y[:, k:k + 1], ns.b[:, k:k + 1],
                                            ALU.mult, ALU.add)
                signals.links = link.start + link.count


MAMBA_LINKS = 2 * (TAPS - 1) + 2
DT_CONV = 2
CONV_AT = (0, 0, 2, 2)

def latent_attention(nc, signals, x_all, ident, d, v_all, o_all, q_dram, k_dram, arena, later):
    with ExitStack() as ctx:
        def sb(name, shape, dt=F32):
            return ctx.enter_context(nc.sbuf_tensor(name, shape, dt))

        def sem(name):
            return signals.new(name)

        ps = ctx.enter_context(nc.psum_tensor("attn_psum", [P, 8, 512], F32))

        norm1_w = sb("norm1_w", [P, 1])
        wq = sb("wq", [P, 2, DM])
        wdkv = sb("wdkv", [P, LAT])
        wuk = sb("wuk", [P, 2, DM])
        wuv = sb("wuv", [P, DM])
        lat_g = sb("lat_g", [LAT, 1])
        lat_b = sb("lat_b", [LAT, 1])
        cos = arena[:, 0:SEQ]
        sin = arena[:, SEQ:2 * SEQ]
        identb = sb("identb", [P, P], BF16)
        mask_q = sb("mask_q", [P, P], BF16)
        mask_k = sb("mask_k", [P, P], BF16)

        ss = sb("attn_ss", [P, TILES])
        rv = sb("attn_rv", [P, TILES])
        r = sb("attn_r", [P, TILES])
        rt = sb("attn_rt", [P, TILES])
        rh = sb("attn_rh", [P, TILES])
        xn = arena[:, 2 * SEQ:3 * SEQ].rearrange("p (k t n) -> p k t n", k=2, t=G)
        xnT = arena[:, 3 * SEQ:4 * SEQ].rearrange("p (k n) -> p k n", k=2)
        lat_all = sb("lat_all", [P, TILES, LAT])
        lat = xn[:, :, :, 0:LAT]
        latT = sb("latT", [P, 2, W])
        ns = NormScratch(sb, "latnorm", TILES)
        parts = sb("parts", [P, 2, SPLITS, W], BF16)

        qst = sb("qst", [STACK, SLOTS, 4, SEQ], BF16)
        kst = sb("kst", [STACK, SLOTS, 4, SEQ], BF16)
        vst = sb("vst", [P, 2, TPB, 4, 32])
        neg = sb("neg", [P, 2, 4, TPB])
        nm = sb("nm", [P, 4 * TPB])
        nmr = sb("nmr", [32, P])
        shift = sb("shift", [32, 2, P], BF16)
        pt = sb("pt", [P, 2, 4, 512])
        rot = pt[:, :, 0, :]
        rot2 = pt[:, :, 1, :]
        rest = pt[:, :, 2, :]
        oc = sb("oc", [P, 512])
        rec = sb("rec", [P, 4, 4])

        loaded, chain = signals.loaded, signals.chain
        folded = sem("attn_folded")
        padded = sem("stacks_padded")
        v_padded = sem("v_padded")
        xn_ready = sem("xn_ready")
        xnT_done = sem("xnT_done")
        xnT_ready = sem("xnT_ready")
        small_done = sem("small_done")
        small_read = sem("small_read")
        stats_ready = sem("stats_ready")
        q_done = sem("q_done")
        rope_ready = sem("rope_ready")
        rot_ready = sem("rot_ready")
        hi_ready = sem("hi_ready")
        rest_ready = sem("rest_ready")
        mid_ready = sem("mid_ready")
        low_ready = sem("low_ready")
        parts_out = [sem(f"parts_out{k}") for k in range(2)]

        stack_loaded = [sem(f"stack_loaded{k}") for k in range(SLOTS)]
        v_staged = sem("v_staged")
        max_done = sem("max_done")
        max_read = sem("max_read")
        nm_ready = sem("nm_ready")
        nmT_done = sem("nmT_done")
        shift_hi = sem("shift_hi")
        shift_rest = sem("shift_rest")
        shift_ready = sem("shift_ready")
        shift_placed = sem("shift_placed")
        st_done = sem("st_done")
        exp_done = sem("exp_done")
        pv_done = sem("pv_done")
        acc_read = sem("acc_read")
        oT_done = sem("oT_done")
        rec_ready = sem("rec_ready")
        o_read = sem("o_read")

        HALVES = SEQ // W
        STEPS = BATCH * HALVES
        NG = BATCH * SLOTS

        units = []
        for t in range(TPB):
            for part in range(2):
                width = min(512, (t + 1) * P - part * 512)
                heads = min(512 // width, 4) if width > 0 else 1
                units += [(t, part, c, heads, width) for c in range(0, 4, heads) if width > 0]
        while len(units) % len(MAX_BANKS):
            k = next(k for k, unit in enumerate(units) if unit[3] > 1)
            t, part, c0, heads, width = units[k]
            units[k:k + 1] = [(t, part, c0 + c, heads // 2, width) for c in (0, heads // 2)]
        NU = len(units)
        exps = [(hf, j, max(0, j * P - hf * 512)) for hf in range(HALVES) for j in range(4 * hf + 4)]
        NX = len(exps)
        assert NX % 2 == 0 and 4 * NX % ST_BANKS == 0

        ahead_cost = [heads * width for t, part, c, heads, width in units] + [W] * (NM_GAP + 1)
        running = []
        for u, (hf, j, q0) in enumerate(exps):
            running += [(u, 2 * (512 - q0))] * 2 + [(u, 4 * (512 - exps[u - 1][2]))]
        take, taken, spent = [], 0, 0
        came_back = {}
        for u, cost in running:
            spent += cost
            due = spent / (PACE * sum(c for _, c in running)) * sum(ahead_cost)
            n0 = taken
            while taken < len(ahead_cost) and (sum(ahead_cost[:taken + 1]) <= due or due >= sum(ahead_cost)):
                taken += 1
            take.append(taken - n0)
            for name, at in (("last", BACK_LAST), ("first", BACK_AT)):
                if u == at + 1:
                    came_back.setdefault(name, taken)
        NORM_LAST, NORM_AT = came_back["last"] + NORM_LAG, came_back["first"] + NORM_LAG

        signals.loads += 16 * 12
        with nc.Block() as block:
            @block.sync
            def _(sp):
                for dst, src in ((norm1_w[:, :], d["norm1_w"]), (wq[:, :, :], d["wq"]), (wdkv[:, :], d["wdkv"]),
                                 (wuk[0:LAT, :, :], d["wuk"]), (wuv[0:LAT, :], d["wuv"]), (lat_g[:, :], d["lat_g"]),
                                 (lat_b[:, :], d["lat_b"]), (cos[:, :], d["cos"]), (sin[:, :], d["sin"]),
                                 (identb[:, :], d["identb"]), (mask_q[:, :], d["mask_q"]),
                                 (mask_k[:, :], d["mask_k"])):
                    sp.dma_start(dst, src).then_inc(loaded, 16)
                start_free(sp, acc_read, exp_done, oT_done, o_read, pv_done, q_done, low_ready, rope_ready, small_read,
                           xnT_done, *parts_out)
                for k in range(SLOTS):
                    sp.dma_start(qst[SROWS:SHIFT_ROW, k, :, :], d["pad"][0:SHIFT_ROW - SROWS, :, :]).then_inc(padded, 16)
                    sp.dma_start(kst[SROWS:STACK, k, :, :], d["pad"]).then_inc(padded, 16)
                def load_stacks(n, k, which=((q_dram, qst), (k_dram, kst))):
                    for dram, st in which:
                        for i in range(SPLITS):
                            for j in range(SPLITS):
                                row = (i * SPLITS + j) * AD
                                part = i if dram is q_dram else j
                                sp.dma_start(
                                    st[row:row + AD, k, :, :],
                                    dram[bass.ds(n, 1), part, :, :].rearrange("n (c d) l -> (n d) c l", c=4))\
                                    .then_inc(stack_loaded[k], 16)

                def place_shift(n, k):
                    sp.wait_ge(shift_ready, n + 1)
                    for s in range(SHIFTS):
                        sp.dma_start(qst[SHIFT_ROW + s:SHIFT_ROW + s + 1, k, :, :], shift[:, s, :])\
                            .then_inc(shift_placed, 16)

                def store_parts(w, b):
                    for hf in range(HALVES):
                        sp.wait_ge(low_ready, FREE + STEPS * w + 2 * b + hf + 1)
                        for g in range(SLOTS):
                            sp.dma_start(
                                (q_dram, k_dram)[w][bass.ds(b * SLOTS + g, 1), :, :, hf * W:(hf + 1) * W]
                                .rearrange("n s r l -> r (n s) l"), parts[32 * g:32 * g + 32, hf, :, :])\
                                .then_inc(parts_out[hf], 16)

                with sp.Fori(0, BATCH) as b:
                    store_parts(0, b)
                for hf in range(HALVES):
                    sp.wait_ge(parts_out[hf], FREE + PARTS_DMAS * BATCH)
                load_stacks(0, 0, ((q_dram, qst),))
                for b in range(BATCH):
                    store_parts(1, b)
                    if b == 0:
                        for hf in range(HALVES):
                            sp.wait_ge(parts_out[hf], FREE + PARTS_DMAS * (BATCH + 1))
                        load_stacks(0, 0, ((k_dram, kst),))
                load_stacks(1, 1)
                for hf in range(HALVES):
                    sp.wait_ge(parts_out[hf], FREE + PARTS_DMAS * 2 * BATCH)
                place_shift(0, 0)
                for k in range(2, SLOTS):
                    load_stacks(k, k)
                with sp.Fori(0, BATCH - 1) as b:
                    for g in range(SLOTS):
                        place_shift(b * SLOTS + g + 1, (g + 1) % SLOTS)
                        sp.wait_ge(pv_done, FREE + (b * SLOTS + g + 1) * NX)
                        load_stacks((b + 1) * SLOTS + g, g)
                for g in range(1, SLOTS):
                    place_shift(NG - SLOTS + g, g)

            @block.tensor
            def _(pe):
                pe.wait_ge(loaded, signals.loads)
                pe.wait_ge(folded, 2)
                def turn(w, b, hf):
                    s = STEPS * w + HALVES * b + hf
                    pe.wait_ge(xn_ready, s + 1)
                    for t in range(G):
                        last = nc.tensor.transpose(ps[:, hf, t * P:(t + 1) * P], xn[:, hf, t, :], ident[:, :])
                    last.then_inc(xnT_done, 1)

                def project(w, b, hf):
                    s = STEPS * w + HALVES * b + hf
                    dst = (xnT, latT)[w]
                    pe.wait_ge(xnT_ready, s + 1)
                    pe.wait_ge(small_read, FREE + s - 1)
                    for t in range(G):
                        width, wt = ((LAT, wdkv), (DM, wuv))[w]
                        last = nc.tensor.matmul(ps[:, 2 + hf, t * width:(t + 1) * width],
                                                dst[:, hf, t * P:(t + 1) * P], wt[:, :], start=True, stop=True)
                    last.then_inc(small_done, 1)
                    pe.wait_ge(rope_ready, FREE + s - 1)
                    for k in range(2):
                        last = nc.tensor.matmul(ps[:, 4 + 2 * hf + k, :], (wq, wuk)[w][:, k, :], dst[:, hf, :],
                                                start=True, stop=True)
                    last.then_inc(q_done, 1)

                for w in range(2):
                    turn(w, 0, 0)
                    with pe.Fori(0, BATCH - 1) as b:
                        turn(w, b, 1)
                        project(w, b, 0)
                        turn(w, b + 1, 0)
                        project(w, b, 1)
                    turn(w, BATCH - 1, 1)
                    project(w, BATCH - 1, 0)
                    project(w, BATCH - 1, 1)

                pe.wait_ge(low_ready, FREE + 2 * STEPS)
                pe.wait_ge(small_read, FREE + 2 * STEPS)
                pe.wait_ge(padded, 16 * 2 * SLOTS)

                def maxima(b, g, first=False):
                    n = b * SLOTS + g
                    pe.wait_ge(stack_loaded[g], STACK_DMAS * (b + 1))
                    for u, (t, part, c0, heads, width) in enumerate(units):
                        pe.wait_ge(max_read, max(u - 2, 0) if first else n * NU + u - 2)
                        diag = part * 512 + width == (t + 1) * P
                        for c in range(heads):
                            out = ps[:, MAX_BANKS[u % len(MAX_BANKS)], c * width:(c + 1) * width]
                            last = nc.tensor.matmul(
                                out, qst[0:SHIFT_ROW, g, c0 + c, t * P:(t + 1) * P],
                                kst[0:SHIFT_ROW, g, c0 + c, part * 512:part * 512 + width], start=True, stop=not diag)
                            if diag:
                                last = nc.tensor.matmul(out[:, width - P:width], identb[:, :], mask_q[:, :],
                                                        start=False, stop=True)
                        last.then_inc(max_done, 1)
                        yield
                    for _ in range(NM_GAP):
                        yield
                    pe.wait_ge(nm_ready, n + 1)
                    if not first:
                        pe.wait_ge(o_read, FREE + 2 * n - 1)
                    nc.tensor.transpose(ps[0:32, 7, 0:P], nm[:, :], ident[:, :]).then_inc(nmT_done, 1)
                    yield

                def rows_back(n, hf, final=False):
                    pe.wait_ge(acc_read, FREE + 2 * n + hf + 1)
                    pe.wait_ge(o_read, FREE + 2 * n + hf)
                    if hf == 1 and not final:
                        pe.wait_ge(shift_rest, n + 2)
                    for t in range(4):
                        last = nc.tensor.transpose(ps[:, 7, t * P:(t + 1) * P], oc[:, t * P:(t + 1) * P], ident[:, :])
                    last.then_inc(oT_done, 1)

                def products(n, g, u):
                    hf, j, q0 = exps[u]
                    pe.wait_ge(exp_done, FREE + 4 * (NX * n + u + 1))
                    if j == 0:
                        pe.wait_ge(acc_read, FREE + 2 * n + hf)
                    for c in range(4):
                        last = nc.tensor.matmul(ps[32 * c:32 * c + 32, 4, q0:512], vst[:, g % 2, j, c, :],
                                                pt[:, u % 2, c, q0:512], start=(j == 0), stop=(j == 4 * hf + 3))
                    last.then_inc(pv_done, 1)

                def exponentials(b, g, first=False):
                    n = b * SLOTS + g

                    pe.wait_ge(shift_placed, 16 * SHIFTS * (n + 1))
                    pe.wait_ge(v_staged, n + 1)
                    for u, (hf, j, q0) in enumerate(exps):
                        diag = j * P >= hf * 512
                        for c in range(4):
                            v = 4 * u + c
                            pe.wait_ge(exp_done, FREE + 4 * NX * n + v - 2)
                            out = ps[:, v % ST_BANKS, q0:512]
                            last = nc.tensor.matmul(out, kst[0:STACK, g, c, j * P:(j + 1) * P],
                                                    qst[0:STACK, g, c, hf * 512 + q0:hf * 512 + 512],
                                                    start=True, stop=not diag)
                            if diag:
                                last = nc.tensor.matmul(out[:, 0:P], identb[:, :], mask_k[:, :], start=False, stop=True)
                            last.then_inc(st_done, 1)
                            if c % 2 == 1:
                                yield
                        if u >= 1:
                            products(n, g, u - 1)
                        elif not first:
                            products(n - 1, (g - 1) % SLOTS, NX - 1)
                        yield
                        if u == BACK_LAST and not first:
                            rows_back(n - 1, 1)
                        if u == BACK_AT:
                            rows_back(n, 0)

                def both(running, ahead):
                    for k, _ in enumerate(running):
                        for _ in range(take[k]):
                            next(ahead)
                    assert next(ahead, None) is None

                for _ in maxima(0, 0, first=True):
                    pass
                both(exponentials(0, 0, first=True), maxima(0, 1))
                with pe.Fori(0, BATCH - 1) as b:
                    for g in range(1, SLOTS + 1):
                        both(exponentials(b + g // SLOTS, g % SLOTS), maxima(b + (g + 1) // SLOTS, (g + 1) % SLOTS))
                for g in range(1, SLOTS - 1):
                    both(exponentials(BATCH - 1, g), maxima(BATCH - 1, g + 1))
                for _ in exponentials(BATCH - 1, SLOTS - 1):
                    pass
                products(NG - 1, SLOTS - 1, NX - 1)
                rows_back(NG - 1, 1, final=True)

            @block.scalar
            def _(act):
                act.wait_ge(loaded, signals.loads)
                def copy_turned(w, b, hf):
                    s = STEPS * w + HALVES * b + hf
                    act.wait_ge(xnT_done, FREE + s + 1)
                    act.wait_ge(q_done, FREE + s - 1)
                    if w == 0:
                        nc.scalar.copy(xnT[:, hf, :], ps[:, hf, :]).then_inc(xnT_ready, 1)
                    else:
                        nc.scalar.activation(latT[0:LAT, hf, :], ps[0:LAT, hf, :], ACT.Identity, bias=lat_b[:, 0:1],
                                             scale=lat_g[:, 0:1]).then_inc(xnT_ready, 1)

                def copy_small(w, b, hf):
                    s = STEPS * w + HALVES * b + hf
                    act.wait_ge(small_done, s + 1)
                    if w == 0:
                        nc.scalar.copy(lat_all[:, bass.ds(b * TPB + hf * G, G), :],
                                       ps[:, 2 + hf, 0:G * LAT].rearrange("p (t n) -> p t n", t=G)).then_inc(small_read, 1)
                    else:
                        vdst = v_all[:, bass.ds(4 * b, 4), 4 * hf:4 * hf + 4, :]
                        nc.scalar.copy(vdst, ps[:, 2 + hf, :].rearrange("p (t g m) -> p g t m", t=4, g=4))\
                            .then_inc(small_read, 1)

                def back(w, b, hf):
                    s = STEPS * w + HALVES * b + hf
                    act.wait_ge(rot_ready, s + 1)
                    act.wait_ge(parts_out[hf], FREE + PARTS_DMAS * (BATCH * w + b))
                    nc.scalar.copy(parts[:, hf, 0, :], rot[:, hf, :]).then_inc(hi_ready, 1)
                    act.wait_ge(rest_ready, s + 1)
                    nc.scalar.copy(parts[:, hf, 1, :], rest[:, hf, :]).then_inc(mid_ready, 1)

                act.wait_ge(folded, 2)
                for w in range(2):
                    copy_turned(w, 0, 0)
                    copy_turned(w, 0, 1)
                    copy_small(w, 0, 0)
                    with act.Fori(0, BATCH - 1) as b:
                        copy_turned(w, b + 1, 0)
                        copy_small(w, b, 1)
                        back(w, b, 0)
                        copy_turned(w, b + 1, 1)
                        copy_small(w, b + 1, 0)
                        back(w, b, 1)
                    copy_small(w, BATCH - 1, 1)
                    back(w, BATCH - 1, 0)
                    back(w, BATCH - 1, 1)

                act.wait_ge(low_ready, FREE + 2 * STEPS)
                later.load(act, loaded)

                def keep(n, hf):
                    act.wait_ge(pv_done, FREE + NX * n + (4 if hf == 0 else NX))
                    act.wait_ge(oT_done, FREE + 2 * n + hf)
                    nc.scalar.copy(oc[:, :], ps[:, 4, :]).then_inc(acc_read, 1)

                def group(n, first=False):
                    for u, (hf, j, q0) in enumerate(exps):
                        for c in range(4):
                            act.wait_ge(st_done, 4 * (NX * n + u) + c + 1)
                            if c == 0:
                                act.wait_ge(pv_done, FREE + NX * n + u - 1)
                            nc.scalar.activation(pt[:, u % 2, c, q0:512], ps[:, (4 * u + c) % ST_BANKS, q0:512], ACT.Exp,
                                                 scale=float(AD) ** -0.5).then_inc(exp_done, 1)
                        if u == 0 and not first:
                            keep(n - 1, 1)
                        if u == 4:
                            keep(n, 0)

                group(0, first=True)
                with act.Fori(1, NG) as n:
                    group(n)
                keep(NG - 1, 1)

            @block.gpsimd
            def _(pool):
                nc.gpsimd.memset(latT[:, :, :], 0.0).then_inc(folded, 1)
                nc.gpsimd.memset(neg[:, :, :, :], -MASKED)
                nc.gpsimd.memset(vst[:, :, :, :, :], 0.0).then_inc(v_padded, 1)
                pool.wait_ge(v_padded, 1)
                nc.gpsimd.memset(vst[:, :, :, :, AD], 1.0).then_inc(v_padded, 1)
                for w in range(2):
                    with pool.Fori(0, BATCH) as b:
                        for hf in range(HALVES):
                            s = STEPS * w + HALVES * b + hf
                            pool.wait_ge(hi_ready, s + 1)
                            nc.gpsimd.tensor_tensor(rest[:, hf, :], rot[:, hf, :], parts[:, hf, 0, :], ALU.subtract)\
                                .then_inc(rest_ready, 1)
                            pool.wait_ge(mid_ready, s + 1)
                            nc.gpsimd.tensor_tensor(parts[:, hf, 2, :], rest[:, hf, :], parts[:, hf, 1, :], ALU.subtract)\
                                .then_inc(low_ready, 1)

                def stage(n, k):
                    nc.gpsimd.tensor_copy(vst[:, k, :, :, 0:AD],
                                          v_all[:, bass.ds(n, 1), :, :].rearrange("p n t (c d) -> p (n t) c d", c=4))\
                        .then_inc(v_staged, 1)

                pool.wait_ge(small_read, FREE + 2 * STEPS)
                pool.wait_ge(v_padded, 2)
                stage(0, 0)
                stage(1, 1)
                with pool.Fori(1, NG // 2) as m:
                    for k in range(2):
                        pool.wait_ge(pv_done, FREE + (2 * m + k - 1) * NX)
                        stage(2 * m + k, k)

            @block.vector
            def _(dve):
                link = Chain(dve, chain, signals.links)
                squares = o_all[:, :, :, :].rearrange("p n t m -> p (n t m)").rearrange("p (k n) -> p k n", k=TILES)
                for k in range(TILES):
                    last = nc.vector.tensor_tensor_reduce(squares[:, k, :], x_all[:, k, :], x_all[:, k, :], 1.0,
                                                          0.0, ALU.mult, ALU.add, ss[:, k:k + 1])
                link(last)
                link(nc.vector.tensor_scalar(rv[:, :], ss[:, :], 1.0 / DM, EPS_RMS2, ALU.mult, ALU.add))
                inverse_root(nc.vector, link, rv[:, :], r[:, :], rt[:, :], rh[:, :])
                dve.wait_ge(loaded, signals.loads)
                nc.vector.memset(wuk[LAT:P, :, :], 0.0)
                nc.vector.memset(wuv[LAT:P, :], 0.0)
                for weight in (wq[:, 0, :], wq[:, 1, :], wdkv[:, :]):
                    last = nc.vector.tensor_scalar(weight, weight, norm1_w[:, 0:1], None, ALU.mult)
                last.then_inc(folded, 1)

                def front(w, b, hf):
                    s = STEPS * w + HALVES * b + hf
                    dve.wait_ge(xnT_done, FREE + s - 1)
                    for t in range(G):
                        k = bass.ds(b * TPB + (hf * G + t), 1)
                        if w == 0:
                            last = nc.vector.tensor_scalar(xn[:, hf, t, :], x_all[:, k, :].rearrange("p k n -> p (k n)"),
                                                           r[:, k], None, ALU.mult)
                        else:
                            last = nc.vector.tensor_scalar(lat[:, hf, t, :], lat_all[:, k, :].rearrange("p k n -> p (k n)"),
                                                           ns.y[:, k], ns.b[:, k], ALU.mult, ALU.add)
                    last.then_inc(xn_ready, 1)

                def back(w, b, hf):
                    s = STEPS * w + HALVES * b + hf
                    sl = slice(hf * W, (hf + 1) * W)
                    dve.wait_ge(q_done, FREE + s + 1)
                    dve.wait_ge(low_ready, FREE + s - 1)
                    nc.vector.tensor_tensor(rot[:, hf, :], ps[:, 4 + 2 * hf, :], cos[:, sl], ALU.mult)
                    nc.vector.tensor_tensor(rot2[:, hf, :], ps[:, 5 + 2 * hf, :], sin[:, sl], ALU.mult)\
                        .then_inc(rope_ready, 1)
                    if w == 0:
                        dve.wait_ge(small_read, FREE + s + 1)
                        for t in range(G):
                            k = bass.ds(b * TPB + (hf * G + t), 1)
                            last = nc.vector.bn_stats(ns.st[:, k, :].rearrange("p k n -> p (k n)"),
                                                      lat_all[:, k, :].rearrange("p k n -> p (k n)"))
                        last.then_inc(stats_ready, 1)
                    dve.wait_ge(rope_ready, FREE + s + 1)
                    nc.vector.tensor_tensor(rot[:, hf, :], rot[:, hf, :], rot2[:, hf, :], ALU.add).then_inc(rot_ready, 1)

                for w in range(2):
                    if w == 1:
                        dve.wait_ge(stats_ready, STEPS)
                        norm_scales(nc.vector, link, ns, EPS_LN, LAT)
                    front(w, 0, 0)
                    front(w, 0, 1)
                    with dve.Fori(0, BATCH - 1) as b:
                        for hf in range(HALVES):
                            front(w, b + 1, hf)
                            back(w, b, hf)
                    for hf in range(HALVES):
                        back(w, BATCH - 1, hf)
                signals.links = link.start + link.count

                dve.wait_ge(v_padded, 2)

                def maxima(n):
                    for u, (t, part, c0, heads, width) in enumerate(units):
                        dve.wait_ge(max_done, n * NU + u + 1)
                        nc.vector.tensor_reduce(
                            neg[:, part, c0:c0 + heads, t],
                            ps[:, MAX_BANKS[u % len(MAX_BANKS)], 0:heads * width].rearrange("p (c w) -> p c w", c=heads), AX.X, ALU.max,
                            negate=True).then_inc(max_read, 1)
                        yield
                    dve.wait_ge(max_read, (n + 1) * NU)
                    nc.vector.tensor_tensor(nm[:, :], neg[:, 0, :, :].rearrange("p c t -> p (c t)"),
                                            neg[:, 1, :, :].rearrange("p c t -> p (c t)"), ALU.min).then_inc(nm_ready, 1)
                    yield
                    dve.wait_ge(nmT_done, n + 1)
                    dve.wait_ge(shift_placed, 16 * SHIFTS * n)
                    nc.vector.tensor_copy(shift[:, 0, :], ps[0:32, 7, 0:P]).then_inc(shift_hi, 1)
                    dve.wait_ge(shift_hi, n + 1)
                    nc.vector.tensor_tensor(nmr[:, :], ps[0:32, 7, 0:P], shift[:, 0, :], ALU.subtract).then_inc(shift_rest, 1)
                    dve.wait_ge(shift_rest, n + 1)
                    nc.vector.tensor_copy(shift[:, 1, :], nmr[:, :]).then_inc(shift_ready, 1)

                def norm(n, hf):
                    dve.wait_ge(oT_done, FREE + 2 * n + hf + 1)
                    back = ps[:, 7, :].rearrange("p (t c m) -> p t c m", t=4, c=4)
                    nc.vector.reciprocal(rec[:, :, :], back[:, :, :, AD]).then_inc(rec_ready, 1)
                    dve.wait_ge(rec_ready, 2 * n + hf + 1)
                    nc.vector.tensor_tensor(
                        o_all[:, bass.ds(n, 1), 4 * hf:4 * hf + 4, :].rearrange("p n t (c d) -> p (n t) c d", c=4),
                        back[:, :, :, 0:AD], rec[:, :, :].unsqueeze(3).to_broadcast([P, 4, 4, AD]), ALU.mult)\
                        .then_inc(o_read, 1)

                def group(n, first=False):
                    for k, _ in enumerate(maxima(n + 1)):
                        if k == NORM_LAST and not first:
                            norm(n - 1, 1)
                        if k == NORM_AT:
                            norm(n, 0)

                for _ in maxima(0):
                    pass
                group(0, first=True)
                with dve.Fori(1, NG - 1) as n:
                    group(n)
                norm(NG - 2, 1)
                norm(NG - 1, 0)
                norm(NG - 1, 1)


SLOTS = AH // 4
SHIFTS = 2
STACK = SHIFT_ROW + SHIFTS
STACK_DMAS = 16 * 2 * SPLITS * SPLITS
ST_BANKS, MAX_BANKS = 3, (3, 5, 6)
BACK_LAST, BACK_AT, NORM_LAG = 1, 6, 1
NM_GAP, PACE = 0, 0.82
PARTS_DMAS = 16 * SLOTS


class Weights:

    def __init__(self, loads):
        self.loads = loads
        self.count = 16 * len(loads)

    def __getitem__(self, name):
        return self.loads[name][0]

    def load(self, eng, sem):
        for dst, src in self.loads.values():
            eng.dma_start(dst, src).then_inc(sem, 16)


def expert_weights(sb, d, arena):
    n = NE * HID
    return Weights({
        "norm2_w": (sb("norm2_w", [P, 1])[:, :], d["norm2_w"]),
        "wo": (sb("moe_wo", [P, DM])[:, :], d["moe_wo"]),
        "gate_w": (sb("gate_w", [P, NE])[:, :], d["gate_w"]),
        "gate_b": (sb("gate_b", [P, NE])[:, :], d["gate_b"].partition_broadcast(P)),
        "w1": (arena[:, 0:n].rearrange("p (e h) -> p e h", e=NE), d["moe_w1"]),
        "b1": (sb("moe_b1", [P, NE, HID // P])[:, :, :], d["moe_b1"]),
        "w2": (arena[:, n:2 * n].rearrange("p (e k n) -> p e k n", e=NE, k=HID // P), d["moe_w2"]),
        "b2": (sb("moe_b2", [G * NE, G * DM])[:, :], d["moe_b2"]),
        "order": (sb("order", [P, NE])[:, :], d["order"]),
    })


def flow_weights(sb, d):
    loads = {n: (sb("fl_" + n, [P, DM])[:, :], d["fl_" + n]) for n in ("wq", "wk", "wv", "wo")}
    loads |= {n: (sb("fl_" + n, [P, 1])[:, :], d["fl_" + n]) for n in ("bq", "bk")}
    loads |= {n: (sb("fl_" + n, [P, DM])[:, :], d["fl_" + n].partition_broadcast(P)) for n in ("bv", "bo")}
    loads["head"] = (sb("fl_head", [P, AH])[:, :], d["head"])
    loads["same"] = (sb("fl_same", [P, DM])[:, :], d["same"])
    return Weights(loads)


def mlp_weights(sb, d):
    return Weights({
        "wf": (sb("tm_wf", [P, FH])[:, :], d["wf"]),
        "wp": (sb("tm_wp", [P, FH // P, DM])[:, :, :], d["wp"]),
        "ln_w": (sb("tm_ln_w", [P, FH // P])[:, :], d["tm_ln_w"]),
        "ln_b": (sb("tm_ln_b", [P, FH // P])[:, :], d["tm_ln_b"]),
    })


def experts(nc, signals, x_all, ident, o_all, weights, later):
    with ExitStack() as ctx:
        def sb(name, shape, dt=F32):
            return ctx.enter_context(nc.sbuf_tensor(name, shape, dt))

        def sem(name):
            return signals.new(name)

        ps = ctx.enter_context(nc.psum_tensor("moe_psum", [P, 8, 512], F32))

        norm2_w, wo, gate_w, gate_b, w1, b1, w2, b2, order = (
            weights[n] for n in ("norm2_w", "wo", "gate_w", "gate_b", "w1", "b1", "w2", "b2", "order"))

        ost = sb("ost", [P, G, DM])
        oT = sb("moe_oT", [P, W])
        x2 = sb("x2", [P, 2, G, DM])
        acc = sb("moe_acc", [P, 2, G, DM])
        xn = sb("moe_xn", [P, G, DM])
        xnT = sb("moe_xnT", [P, 2, W])
        ss = sb("moe_ss", [P, G])
        rv = sb("moe_rv", [P, G])
        r = sb("moe_r", [P, G])
        rt = sb("moe_rt", [P, G])
        rh = sb("moe_rh", [P, G])
        logits = sb("logits", [P, G, NE])
        best = sb("best", [P, G])
        onehot = sb("onehot", [P, 2, G, NE])
        onehotT = sb("onehotT", [G * NE, P])
        hs = sb("moe_hs", [P, 2, HID // P, W])
        ns = NormScratch(sb, "moenorm")

        loaded, chain = signals.loaded, signals.chain
        folded = sem("moe_folded")
        ost_ready = sem("ost_ready")
        oT_done = sem("moe_oT_done")
        oT_ready = sem("moe_oT_ready")
        ao_done = sem("ao_done")
        xn_ready = sem("moe_xn_ready")
        xnT_done = sem("moe_xnT_done")
        xnT_ready = sem("moe_xnT_ready")
        gate_done = sem("gate_done")
        onehot_ready = sem("onehot_ready")
        onehotT_done = sem("onehotT_done")
        onehotT_ready = sem("onehotT_ready")
        b2_done = sem("b2_done")
        b2_read = sem("b2_read")
        h_done = sem("moe_h_done")
        h_act = sem("moe_h_act")
        h_dve = sem("moe_h_dve")
        y_done = sem("moe_y_done")
        y_read = sem("moe_y_read")

        HALVES = SEQ // W
        STEPS = BATCH * HALVES
        HB = HID // P
        small = ps[:, 0, :]

        signals.loads += weights.count
        with nc.Block() as block:
            @block.sync
            def _(sp):
                start_free(sp, h_act, h_done, h_dve, y_done, y_read)
                sp.wait_ge(loaded, signals.loads)
                for w, sem_loaded in later:
                    w.load(sp, sem_loaded)

            @block.tensor
            def _(pe):
                pe.wait_ge(loaded, signals.loads)
                pe.wait_ge(folded, 1)

                def front(s, hf):
                    pe.wait_ge(ost_ready, s + 1)
                    pe.wait_ge(onehotT_ready, s)
                    for t in range(G):
                        last = nc.tensor.transpose(ps[:, 0, t * P:(t + 1) * P], ost[:, t, :], ident[:, :])
                    last.then_inc(oT_done, 1)
                    yield
                    pe.wait_ge(oT_ready, s + 1)
                    pe.wait_ge(b2_read, s)
                    for t in range(G):
                        last = nc.tensor.matmul(ps[:, 1, t * P:(t + 1) * P], oT[:, t * P:(t + 1) * P], wo[:, :],
                                                start=True, stop=True)
                    last.then_inc(ao_done, 1)
                    yield
                    pe.wait_ge(xn_ready, s + 1)
                    for t in range(G):
                        last = nc.tensor.transpose(ps[:, 0, t * P:(t + 1) * P], xn[:, t, :], ident[:, :])
                    last.then_inc(xnT_done, 1)
                    yield
                    pe.wait_ge(xnT_ready, s + 1)
                    for t in range(G):
                        last = nc.tensor.matmul(small[:, t * NE:(t + 1) * NE], xnT[:, hf, t * P:(t + 1) * P],
                                                gate_w[:, :], start=True, stop=True)
                    last.then_inc(gate_done, 1)
                    yield
                    pe.wait_ge(onehot_ready, s + 1)
                    nc.tensor.transpose(small[0:G * NE, P:2 * P], onehot[:, hf, :, :].rearrange("p t e -> p (t e)"),
                                        ident[:, :]).then_inc(onehotT_done, 1)
                    yield
                    pe.wait_ge(onehotT_ready, s + 1)
                    nc.tensor.matmul(ps[:, 1, :], onehotT[:, :], b2[:, :], start=True, stop=True).then_inc(b2_done, 1)
                    yield

                def expert_steps(s, hf):
                    blocks = [(e, k) for e in range(NE) for k in range(HB)]

                    def hidden(n):
                        e, k = blocks[n]
                        pe.wait_ge(h_act if n % 2 == 0 else h_dve, FREE + 8 * s + (n - 4) // 2 + 1)
                        nc.tensor.matmul(ps[:, 2 + n % 4, :], w1[:, e, k * P:(k + 1) * P], xnT[:, hf, :],
                                         start=True, stop=True).then_inc(h_done, 1)

                    def outputs(e):
                        pe.wait_ge(h_act, FREE + 8 * s + 2 * e + 2)
                        pe.wait_ge(h_dve, FREE + 8 * s + 2 * e + 2)
                        pe.wait_ge(y_read, FREE + 4 * s + max(e - 1, 0))
                        for t in range(G):
                            for k in range(HB):
                                last = nc.tensor.matmul(ps[:, 6 + e % 2, t * P:(t + 1) * P],
                                                        hs[:, e % 2, k, t * P:(t + 1) * P], w2[:, e, k, :],
                                                        start=(k == 0), stop=(k == HB - 1))
                        last.then_inc(y_done, 1)

                    for n in range(NE * HB):
                        hidden(n)
                        yield
                        if n % HB == HB - 1 and n > HB:
                            outputs(n // HB - 1)
                            yield
                    outputs(NE - 1)
                    yield

                for _ in front(0, 0):
                    pass
                with pe.Fori(0, BATCH - 1) as b:
                    for hf in range(HALVES):
                        s = HALVES * b + hf
                        ahead = front(s + 1, 1 - hf)
                        for k, _ in enumerate(expert_steps(s, hf)):
                            if k in PE_FRONT:
                                next(ahead, None)
                        for _ in ahead:
                            pass
                s = STEPS - 2
                ahead = front(s + 1, 1)
                for k, _ in enumerate(expert_steps(s, 0)):
                    if k in PE_FRONT:
                        next(ahead, None)
                for _ in ahead:
                    pass
                for _ in expert_steps(s + 1, 1):
                    pass

            @block.scalar
            def _(act):
                act.wait_ge(loaded, signals.loads)

                def front(s, hf, first=False):
                    act.wait_ge(oT_done, s + 1)
                    nc.scalar.copy(oT[:, :], ps[:, 0, :]).then_inc(oT_ready, 1)
                    yield
                    act.wait_ge(xnT_done, s + 1)
                    if not first:
                        act.wait_ge(h_done, FREE + 16 * (s - 1))
                    nc.scalar.copy(xnT[:, hf, :], ps[:, 0, :]).then_inc(xnT_ready, 1)
                    yield
                    act.wait_ge(onehotT_done, s + 1)
                    nc.scalar.copy(onehotT[:, :], small[0:G * NE, P:2 * P]).then_inc(onehotT_ready, 1)
                    yield

                def relus(s):
                    for n in range(0, NE * HB, 2):
                        e, k = n // HB, n % HB
                        act.wait_ge(h_done, FREE + 16 * s + n + 1)
                        act.wait_ge(y_done, FREE + 4 * s + max(e - 1, 0))
                        nc.scalar.activation(hs[:, e % 2, k, :], ps[:, 2 + n % 4, :], ACT.Relu, bias=b1[:, e, k:k + 1])\
                            .then_inc(h_act, 1)
                        yield

                for _ in front(0, 0, first=True):
                    pass

                def step(s, hf, more=True):
                    ahead = front(s + 1, 1 - hf) if more else iter(())
                    for k, _ in enumerate(relus(s)):
                        if k in ACT_FRONT:
                            next(ahead, None)
                    for _ in ahead:
                        pass

                with act.Fori(0, BATCH - 1) as b:
                    for hf in range(HALVES):
                        step(HALVES * b + hf, hf)
                step(STEPS - 2, 0)
                step(STEPS - 1, 1, more=False)

            @block.vector
            def _(dve):
                dve.wait_ge(loaded, signals.loads)
                nc.vector.tensor_scalar(gate_w[:, :], gate_w[:, :], norm2_w[:, 0:1], None, ALU.mult)
                nc.vector.tensor_scalar(w1[:, :, :], w1[:, :, :], norm2_w[:, 0:1], None, ALU.mult).then_inc(folded, 1)

                def front(b, s, hf, step):
                    x_now = x_all[:, bass.ds(b * TPB + hf * G, G), :]
                    dve.wait_ge(oT_done, s)
                    for g in range(SLOTS):
                        last = nc.vector.tensor_copy(ost[:, :, 32 * g:32 * g + 32],
                                                     o_all[:, bass.ds(b * SLOTS + g, 1), 4 * hf:4 * hf + 4, :]
                                                     .rearrange("p n t m -> p (n t) m"))
                    last.then_inc(ost_ready, 1)
                    yield
                    dve.wait_ge(ao_done, s + 1)
                    dve.wait_ge(xnT_done, s)
                    step(nc.vector.tensor_tensor(x2[:, hf, :, :], ps[:, 1, :].rearrange("p (t n) -> p t n", t=G), x_now,
                                                 ALU.add))
                    for t in range(G):
                        last = nc.vector.tensor_tensor_reduce(xn[:, t, :], x2[:, hf, t, :], x2[:, hf, t, :], 1.0, 0.0,
                                                              ALU.mult, ALU.add, ss[:, t:t + 1])
                    step(last)
                    step(nc.vector.tensor_scalar(rv[:, :], ss[:, :], 1.0 / DM, EPS_RMS2, ALU.mult, ALU.add))
                    inverse_root(nc.vector, step, rv[:, :], r[:, :], rt[:, :], rh[:, :])
                    for t in range(G):
                        last = nc.vector.tensor_scalar(xn[:, t, :], x2[:, hf, t, :], r[:, t:t + 1], None, ALU.mult)
                    last.then_inc(xn_ready, 1)
                    nc.vector.tensor_tensor(acc[:, hf, :, :], x2[:, hf, :, :], x_now, ALU.add)
                    yield
                    dve.wait_ge(gate_done, s + 1)
                    step(nc.vector.tensor_tensor(logits[:, :, :], small[:, 0:G * NE].rearrange("p (t e) -> p t e", t=G),
                                                 gate_b[:, :].unsqueeze(1).to_broadcast([P, G, NE]), ALU.add))
                    step(nc.vector.tensor_reduce(best[:, :], logits[:, :, :], AX.X, ALU.max))
                    step(nc.vector.tensor_tensor(logits[:, :, :], logits[:, :, :],
                                                 best[:, :].unsqueeze(2).to_broadcast([P, G, NE]), ALU.is_equal))
                    step(nc.vector.tensor_tensor(logits[:, :, :], logits[:, :, :],
                                                 order[:, :].unsqueeze(1).to_broadcast([P, G, NE]), ALU.mult))
                    step(nc.vector.tensor_reduce(best[:, :], logits[:, :, :], AX.X, ALU.max))
                    nc.vector.tensor_tensor(onehot[:, hf, :, :], logits[:, :, :],
                                            best[:, :].unsqueeze(2).to_broadcast([P, G, NE]), ALU.is_equal)\
                        .then_inc(onehot_ready, 1)
                    yield
                    dve.wait_ge(b2_done, s + 1)
                    nc.vector.tensor_tensor(acc[:, hf, :, :], acc[:, hf, :, :],
                                            ps[:, 1, :].rearrange("p (t n) -> p t n", t=G), ALU.add).then_inc(b2_read, 1)
                    yield

                def back(b, s, hf, step):
                    def take(e):
                        dve.wait_ge(y_done, FREE + 4 * s + e + 1)
                        if e == 0:
                            dve.wait_ge(b2_read, s + 1)
                        else:
                            dve.wait_ge(y_read, FREE + 4 * s + e)
                        for t in range(G):
                            last = nc.vector.scalar_tensor_tensor(
                                out=acc[:, hf, t, :], in0=ps[:, 6 + e % 2, t * P:(t + 1) * P],
                                scalar=onehot[:, hf, t, e:e + 1], in1=acc[:, hf, t, :], op0=ALU.mult, op1=ALU.add)
                        last.then_inc(y_read, 1)

                    for n in range(1, NE * HB, 2):
                        e, k = n // HB, n % HB
                        dve.wait_ge(h_done, FREE + 16 * s + n + 1)
                        dve.wait_ge(y_done, FREE + 4 * s + max(e - 1, 0))
                        nc.vector.tensor_scalar(hs[:, e % 2, k, :], ps[:, 2 + n % 4, :], b1[:, e, k:k + 1], 0.0,
                                                ALU.add, ALU.max).then_inc(h_dve, 1)
                        yield
                        if n in (9, 13):
                            take(n // HB - 2)
                            yield
                    for e in (2, 3):
                        take(e)

                def finish(b, s, hf, step):
                    dve.wait_ge(y_read, FREE + 4 * s + 4)
                    for t in range(G):
                        last = nc.vector.bn_stats(ns.st[:, t, :], acc[:, hf, t, :])
                    step(last)
                    yield
                    norm_scales(nc.vector, step, ns, EPS_LN, DM)
                    yield
                    x_now = x_all[:, bass.ds(b * TPB + hf * G, G), :]
                    for t in range(G):
                        last = nc.vector.tensor_scalar(x_now[:, t, :], acc[:, hf, t, :], ns.y[:, t:t + 1], ns.b[:, t:t + 1],
                                                       ALU.mult, ALU.add)
                    step(last)
                    yield

                def both(b, s, hf, step, more=True, first=False):
                    ahead = front(b + (1 if hf else 0), s + 1, 1 - hf, step) if more else iter(())
                    behind = iter(()) if first else finish(b - (0 if hf else 1), s - 1, 1 - hf, step)
                    for k, _ in enumerate(back(b, s, hf, step)):
                        for _ in range(DVE_FRONT.count(k)):
                            next(ahead, None)
                        for _ in range(DVE_FINISH.count(k)):
                            next(behind, None)
                    for _ in ahead:
                        pass

                link = Chain(dve, chain, signals.links)
                for _ in front(0, 0, 0, link):
                    pass
                both(0, 0, 0, link, first=True)
                with dve.Fori(0, BATCH - 1) as b:
                    step = Chain(dve, chain, link.start + link.count, b, MOE_LINKS)
                    both(b, HALVES * b + 1, 1, step)
                    both(b + 1, HALVES * b + 2, 0, step)
                    step.end()
                link = Chain(dve, chain, link.start + link.count + (BATCH - 1) * MOE_LINKS)
                both(BATCH - 1, STEPS - 1, 1, link, more=False)
                for _ in finish(BATCH - 1, STEPS - 1, 1, link):
                    pass
                signals.links = link.start + link.count


PE_FRONT = (3, 5, 10, 12, 15, 17)
DVE_FRONT, DVE_FINISH = (0, 2, 6, 9), (0, 1, 1)
ACT_FRONT = (1, 4, 6)
MOE_LINKS = 2 * (1 + 1 + 1 + ROOT_LINKS + 5 + NORM_LINKS)


class Ternary:

    def __init__(self, nc, signals, ctx, weights, weights_loaded):
        def sb(name, shape):
            return ctx.enter_context(nc.sbuf_tensor("tm_" + name, shape, F32))

        self.nc, self.weights, self.weights_loaded = nc, weights, weights_loaded
        self.wf3 = sb("wf3", [P, FH])
        self.wp3 = sb("wp3", [P, FH // P, DM])
        self.low = sb("low", [P, 2, FH])
        self.asum = sb("asum", [P, 2])
        self.bound = sb("bound", [P, 2])
        self.nbound = sb("nbound", [P, 2])
        self.sums_ready, self.sums_done, self.sums_read = (
            signals.new("tm_" + n) for n in ("sums_ready", "sums_done", "sums_read"))

    def tensor(self, pe, ones, bank):
        pe.wait_ge(self.sums_ready, 1)
        self.nc.tensor.matmul(bank[:, 0:2], ones[:, :], self.asum[:, :], start=True, stop=True).then_inc(self.sums_done, 1)
        pe.wait_ge(self.sums_read, 1)

    def vector(self, dve, link, bank):
        nc, wf, wp = self.nc, self.weights["wf"], self.weights["wp"].rearrange("p k n -> p (k n)")
        dve.wait_ge(self.weights_loaded, self.weights.count)
        nc.vector.tensor_reduce(self.asum[:, 0:1], wf, AX.X, ALU.add, apply_absolute_value=True)
        nc.vector.tensor_reduce(self.asum[:, 1:2], wp, AX.X, ALU.add, apply_absolute_value=True)\
            .then_inc(self.sums_ready, 1)
        dve.wait_ge(self.sums_done, 1)
        nc.vector.tensor_scalar(self.bound[:, :], bank[:, 0:2], 1.0 / (FH * DM), GAMMA_EPS, ALU.mult, ALU.add)\
            .then_inc(self.sums_read, 1)
        dve.wait_ge(self.sums_read, 1)
        link(nc.vector.tensor_scalar(self.bound[:, :], self.bound[:, :], 0.5, None, ALU.mult))
        link(nc.vector.tensor_scalar(self.nbound[:, :], self.bound[:, :], -1.0, None, ALU.mult))
        pairs = ((wf, self.wf3[:, :]), (wp, self.wp3[:, :, :].rearrange("p k n -> p (k n)")))
        for n, (w, w3) in enumerate(pairs):
            last = nc.vector.tensor_scalar(self.low[:, n, :], w, self.nbound[:, n:n + 1], None, ALU.is_lt)
        link(last)
        for n, (w, w3) in enumerate(pairs):
            last = nc.vector.scalar_tensor_tensor(out=w3, in0=w, scalar=self.bound[:, n:n + 1], in1=self.low[:, n, :],
                                                  op0=ALU.is_gt, op1=ALU.subtract)
        link(last)


def flow_attention(nc, signals, x_all, ones, ident, weights, weights_loaded, ternary):
    with ExitStack() as ctx:
        def sb(name, shape, dt=F32):
            return ctx.enter_context(nc.sbuf_tensor("fl_" + name, shape, dt))

        def sem(name):
            return signals.new("fl_" + name)

        ps = ctx.enter_context(nc.psum_tensor("flow_psum", [P, 8, 512], F32))
        PAIR = 2
        seqs = range(PAIR)
        A = [ps[:, 4 * s:4 * s + 2, :] for s in seqs]
        B = [ps[:, 4 * s + 2:4 * s + 4, :] for s in seqs]

        def tiles(banks):
            return banks.rearrange("p k (t n) -> p (k t) n", n=P)

        def rows(banks):
            return banks[:, 0, 0:2 * TPB * AH].rearrange("p (w t h) -> p w t h", w=2, t=TPB)

        wq, wk, wv, wo, bq, bk, bv, bo, head, same = (
            weights[n] for n in ("wq", "wk", "wv", "wo", "bq", "bk", "bv", "bo", "head", "same"))

        xin = sb("xin", [P, PAIR, TPB, DM])
        xs = sb("xs", [P, PAIR, TPB, DM])
        xT = sb("xT", [P, PAIR, SEQ])
        qT = sb("qT", [P, PAIR, SEQ])
        kT = sb("kT", [P, PAIR, SEQ])
        qe = sb("qe", [P, PAIR, SEQ])
        ke = sb("ke", [P, PAIR, SEQ])
        sums = sb("sums", [P, PAIR, 2])
        sume = sb("sume", [P, PAIR, 2])
        blk = sb("blk", [P, PAIR, 2, AH])
        vb = sb("vb", [P, PAIR, TPB, DM])
        ktok = sb("ktok", [P, PAIR, TPB, DM])
        qtok = sb("qtok", [P, PAIR, TPB, DM])
        flow = sb("flow", [P, PAIR, 2, TPB, AH])
        gblk = sb("gblk", [P, PAIR, 2, AH])
        alloc = sb("alloc", [P, PAIR, TPB, AH])
        comp = sb("comp", [P, PAIR, TPB, AH])
        total = sb("total", [P, PAIR, AH])
        weight = sb("weight", [P, PAIR, TPB, AH])
        kv = sb("kv", [P, PAIR, DM])
        ot = sb("ot", [P, PAIR, TPB, DM])
        oT = sb("oT", [P, PAIR, SEQ])
        ns = NormScratch(sb, "norm", PAIR * TPB)

        chain = signals.chain
        names = ("xs_ready", "xT_done", "xT_ready", "q_done", "k_done", "q_ready", "k_ready", "v_done", "v_ready",
                 "ktok_done", "ktok_ready", "qtok_done", "qtok_ready", "blk_ready", "flow_done", "flow_ready", "g_done",
                 "gblk_ready", "cons_done", "alloc_ready", "clip_ready", "exp_ready", "total_done", "vs_ready",
                 "kv_done", "kv_ready", "o_done", "o_ready", "oT_done", "oT_ready", "out_done", "out_read")
        done = {n: sem(n) for n in names}

        with nc.Block() as block:
            @block.sync
            def _(sp):
                start_free(sp, done["out_read"])

            @block.tensor
            def _(pe):
                pe.wait_ge(weights_loaded, weights.count)

                def tile(src, s, t):
                    return src[:, s, t * P:(t + 1) * P]

                ternary.tensor(pe, ones, ps[:, 7, :])
                with pe.Fori(0, BATCH // PAIR) as m:
                    def wait(name, s):
                        pe.wait_ge(done[name], PAIR * m + s + 1)

                    for s in seqs:
                        wait("xs_ready", s)
                        for t in range(TPB):
                            last = nc.tensor.transpose(tiles(A[s])[:, t, :], xin[:, s, t, :], ident[:, :])
                        last.then_inc(done["xT_done"], 1)
                    for s in seqs:
                        wait("xT_ready", s)
                        for k in range(2):
                            last = nc.tensor.matmul(A[s][:, k, :], wk[:, :], xT[:, s, k * 512:(k + 1) * 512],
                                                    start=True, stop=True)
                        last.then_inc(done["k_done"], 1)
                        pe.wait_ge(done["out_read"], FREE + PAIR * m + s - 1)
                        for k in range(2):
                            last = nc.tensor.matmul(B[s][:, k, :], wq[:, :], xT[:, s, k * 512:(k + 1) * 512],
                                                    start=True, stop=True)
                        last.then_inc(done["q_done"], 1)
                    for s in seqs:
                        wait("k_ready", s)
                        for t in range(TPB):
                            last = nc.tensor.transpose(tiles(A[s])[:, t, :], tile(kT, s, t), ident[:, :])
                        last.then_inc(done["ktok_done"], 1)
                        wait("q_ready", s)
                        for t in range(TPB):
                            last = nc.tensor.matmul(tiles(B[s])[:, t, :], tile(xT, s, t), wv[:, :], start=True, stop=True)
                        last.then_inc(done["v_done"], 1)
                    for s in seqs:
                        wait("ktok_ready", s)
                        wait("blk_ready", s)
                        for w, src in enumerate((qe, ke)):
                            for t in range(TPB):
                                last = nc.tensor.matmul(rows(A[s])[:, w, t, :], tile(src, s, t), blk[:, s, w, :],
                                                        start=True, stop=True)
                        last.then_inc(done["flow_done"], 1)
                        wait("v_ready", s)
                        for t in range(TPB):
                            last = nc.tensor.transpose(tiles(B[s])[:, t, :], tile(qT, s, t), ident[:, :])
                        last.then_inc(done["qtok_done"], 1)
                    for s in seqs:
                        wait("flow_ready", s)
                        wait("qtok_ready", s)
                        for w, src in enumerate((ktok, qtok)):
                            for t in range(TPB):
                                last = nc.tensor.matmul(B[s][:, 0, w * AH:(w + 1) * AH], src[:, s, t, :],
                                                        flow[:, s, 1 - w, t, :], start=(t == 0), stop=(t == TPB - 1))
                        last.then_inc(done["g_done"], 1)
                    for s in seqs:
                        wait("gblk_ready", s)
                        for w, src in enumerate((qe, ke)):
                            for t in range(TPB):
                                last = nc.tensor.matmul(rows(A[s])[:, w, t, :], tile(src, s, t), gblk[:, s, w, :],
                                                        start=True, stop=True)
                        last.then_inc(done["cons_done"], 1)
                    for s in seqs:
                        wait("exp_ready", s)
                        for t in range(TPB):
                            last = nc.tensor.matmul(B[s][:, 0, 0:AH], ones[:, :], comp[:, s, t, :],
                                                    start=(t == 0), stop=(t == TPB - 1))
                        last.then_inc(done["total_done"], 1)
                    for s in seqs:
                        wait("vs_ready", s)
                        wait("alloc_ready", s)
                        for t in range(TPB):
                            last = nc.tensor.matmul(A[s][:, 0, 0:DM], ktok[:, s, t, :], vb[:, s, t, :],
                                                    start=(t == 0), stop=(t == TPB - 1))
                        last.then_inc(done["kv_done"], 1)
                    for s in seqs:
                        wait("kv_ready", s)
                        for t in range(TPB):
                            last = nc.tensor.matmul(tiles(B[s])[:, t, :], tile(qT, s, t), kv[:, s, :], start=True, stop=True)
                        last.then_inc(done["o_done"], 1)
                    for s in seqs:
                        wait("o_ready", s)
                        for t in range(TPB):
                            last = nc.tensor.transpose(tiles(A[s])[:, t, :], ot[:, s, t, :], ident[:, :])
                        last.then_inc(done["oT_done"], 1)
                    for s in seqs:
                        wait("oT_ready", s)
                        for t in range(TPB):
                            last = nc.tensor.matmul(tiles(B[s])[:, t, :], tile(oT, s, t), wo[:, :], start=True, stop=True)
                        last.then_inc(done["out_done"], 1)

            @block.scalar
            def _(act):
                act.wait_ge(weights_loaded, weights.count)
                with act.Fori(0, BATCH // PAIR) as m:
                    def wait(name, s):
                        act.wait_ge(done[name], PAIR * m + s + 1)

                    for s in seqs:
                        wait("xT_done", s)
                        nc.scalar.copy(xT[:, s, :], A[s].rearrange("p k n -> p (k n)")).then_inc(done["xT_ready"], 1)
                    for s in seqs:
                        wait("k_done", s)
                        nc.scalar.activation(kT[:, s, :], A[s].rearrange("p k n -> p (k n)"), ACT.Sigmoid, bias=bk[:, 0:1],
                                             accum_out=sums[:, s, 0:1]).then_inc(done["k_ready"], 1)
                        wait("q_done", s)
                        nc.scalar.activation(qT[:, s, :], B[s].rearrange("p k n -> p (k n)"), ACT.Sigmoid, bias=bq[:, 0:1],
                                             accum_out=sums[:, s, 1:2]).then_inc(done["q_ready"], 1)
                    for s in seqs:
                        wait("ktok_done", s)
                        nc.scalar.copy(ktok[:, s, :, :], tiles(A[s])).then_inc(done["ktok_ready"], 1)
                    for s in seqs:
                        wait("qtok_done", s)
                        nc.scalar.copy(qtok[:, s, :, :], tiles(B[s])).then_inc(done["qtok_ready"], 1)
                    for s in seqs:
                        wait("cons_done", s)
                        nc.scalar.activation(alloc[:, s, :, :], rows(A[s])[:, 0, :, :], ACT.Sigmoid)\
                            .then_inc(done["alloc_ready"], 1)
                    for s in seqs:
                        wait("clip_ready", s)
                        nc.scalar.activation(comp[:, s, :, :], comp[:, s, :, :], ACT.Exp).then_inc(done["exp_ready"], 1)
                    for s in seqs:
                        wait("oT_done", s)
                        nc.scalar.copy(oT[:, s, :], A[s].rearrange("p k n -> p (k n)")).then_inc(done["oT_ready"], 1)

            @block.vector
            def _(dve):
                dve.wait_ge(weights_loaded, weights.count)

                def x_now(m, s):
                    return x_all[:, bass.ds(m * (PAIR * TPB) + s * TPB, TPB), :]

                def fetch(m):
                    for s in seqs:
                        nc.vector.tensor_copy(xin[:, s, :, :], x_now(m, s)).then_inc(done["xs_ready"], 1)

                def pair(m, step, more=True):
                    def wait(name, s):
                        dve.wait_ge(done[name], PAIR * m + s + 1)

                    for s in seqs:
                        wait("k_ready", s)
                        nc.vector.tensor_scalar(ke[:, s, :], kT[:, s, :], FLOW_EPS, None, ALU.add)
                        wait("q_ready", s)
                        nc.vector.tensor_scalar(qe[:, s, :], qT[:, s, :], FLOW_EPS, None, ALU.add)
                        step(nc.vector.tensor_scalar(sume[:, s, :], sums[:, s, :], FLOW_EPS, None, ALU.add))
                        for w in range(2):
                            last = nc.vector.tensor_scalar(blk[:, s, w, :], head[:, :], sume[:, s, w:w + 1], None, ALU.mult)
                        last.then_inc(done["blk_ready"], 1)
                    for s in seqs:
                        wait("v_done", s)
                        nc.vector.tensor_tensor(vb[:, s, :, :], tiles(B[s]), bv[:, :].unsqueeze(1).to_broadcast([P, TPB, DM]),
                                                ALU.add).then_inc(done["v_ready"], 1)
                    for s in seqs:
                        wait("flow_done", s)
                        nc.vector.reciprocal(flow[:, s, :, :, :], rows(A[s])).then_inc(done["flow_ready"], 1)
                    for s in seqs:
                        wait("g_done", s)
                        nc.vector.scalar_tensor_tensor(
                            out=gblk[:, s, :, :], in0=B[s][:, 0, 0:2 * AH].rearrange("p (w h) -> p w h", w=2), scalar=FLOW_EPS,
                            in1=head[:, :].unsqueeze(1).to_broadcast([P, 2, AH]), op0=ALU.add, op1=ALU.mult)\
                            .then_inc(done["gblk_ready"], 1)
                    for s in seqs:
                        wait("alloc_ready", s)
                        nc.vector.tensor_scalar(comp[:, s, :, :], rows(A[s])[:, 1, :, :], -1.0, 1.0, ALU.max, ALU.min)\
                            .then_inc(done["clip_ready"], 1)
                    for s in seqs:
                        wait("total_done", s)
                        wait("exp_ready", s)
                        step(nc.vector.reciprocal(total[:, s, :], B[s][:, 0, 0:AH]))
                        step(nc.vector.scalar_tensor_tensor(
                            out=comp[:, s, :, :], in0=comp[:, s, :, :], scalar=float(SEQ),
                            in1=total[:, s, :].unsqueeze(1).to_broadcast([P, TPB, AH]), op0=ALU.mult, op1=ALU.mult))
                        split = vb[:, s, :, :].rearrange("p t (h n) -> p (t h) n", h=AH)
                        nc.vector.tensor_tensor(
                            split, split, comp[:, s, :, :].rearrange("p t h -> p (t h)").unsqueeze(2)
                            .to_broadcast([P, TPB * AH, AD]), ALU.mult).then_inc(done["vs_ready"], 1)
                        wait("alloc_ready", s)
                        step(nc.vector.tensor_tensor(weight[:, s, :, :], alloc[:, s, :, :], flow[:, s, 0, :, :], ALU.mult))
                    for s in seqs:
                        wait("kv_done", s)
                        nc.vector.tensor_tensor(kv[:, s, :], A[s][:, 0, 0:DM], same[:, :], ALU.mult)\
                            .then_inc(done["kv_ready"], 1)
                    for s in seqs:
                        wait("o_done", s)
                        nc.vector.tensor_tensor(
                            ot[:, s, :, :].rearrange("p t (h n) -> p (t h) n", h=AH),
                            tiles(B[s]).rearrange("p t (h n) -> p (t h) n", h=AH),
                            weight[:, s, :, :].rearrange("p t h -> p (t h)").unsqueeze(2)
                            .to_broadcast([P, TPB * AH, AD]), ALU.mult).then_inc(done["o_ready"], 1)
                        wait("xT_done", s)
                        step(nc.vector.tensor_tensor(xs[:, s, :, :], x_now(m, s),
                                                     bo[:, :].unsqueeze(1).to_broadcast([P, TPB, DM]), ALU.add))
                    if more:
                        fetch(m + 1)
                    for s in seqs:
                        wait("out_done", s)
                        nc.vector.tensor_tensor(xs[:, s, :, :], xs[:, s, :, :], tiles(B[s]), ALU.add)\
                            .then_inc(done["out_read"], 1)
                        dve.wait_ge(done["out_read"], FREE + PAIR * m + s + 1)
                        for t in range(TPB):
                            last = nc.vector.bn_stats(ns.st[:, s * TPB + t, :], xs[:, s, t, :])
                    step(last)
                    norm_scales(nc.vector, step, ns, EPS_LN, DM)
                    for s in seqs:
                        for t in range(TPB):
                            k = s * TPB + t
                            last = nc.vector.tensor_scalar(x_now(m, s)[:, t, :], xs[:, s, t, :], ns.y[:, k:k + 1],
                                                           ns.b[:, k:k + 1], ALU.mult, ALU.add)
                    step(last)

                fetch(0)
                link = Chain(dve, chain, signals.links)
                ternary.vector(dve, link, ps[:, 7, :])
                with dve.Fori(0, BATCH // PAIR - 1) as m:
                    step = Chain(dve, chain, link.start + link.count, m, FLOW_LINKS)
                    pair(m, step)
                    step.end()
                link = Chain(dve, chain, link.start + link.count + (BATCH // PAIR - 1) * FLOW_LINKS)
                pair(BATCH // PAIR - 1, link, more=False)
                signals.links = link.start + link.count


FLOW_LINKS = 2 * (1 + 2 + 1 + 1) + NORM_LINKS


def ternary_mlp(nc, signals, x_all, ident, ternary, out):
    with ExitStack() as ctx:
        def sb(name, shape, dt=F32):
            return ctx.enter_context(nc.sbuf_tensor("tm_" + name, shape, dt))

        def sem(name):
            return signals.new("tm_" + name)

        ps = ctx.enter_context(nc.psum_tensor("mlp_psum", [P, 8, 512], F32))
        HB = FH // P
        STEPS = TILES // G
        wf3, wp3 = ternary.wf3, ternary.wp3
        ln_w, ln_b = ternary.weights["ln_w"], ternary.weights["ln_b"]

        xs = sb("xs", [P, 2, G, DM])
        xT = sb("xT", [P, 2, W])
        g = sb("g", [P, 2, G, FH])
        nT = sb("nT", [P, HB, W])
        y = sb("y", [P, 2, G, DM])
        ns = NormScratch(sb, "norm", 2 * G)
        ns_first = NormScratch(sb, "norm_first")

        chain = signals.chain
        xs_ready = sem("xs_ready")
        xT_done = sem("xT_done")
        xT_ready = sem("xT_ready")
        h_done = sem("h_done")
        g_ready = sem("g_ready")
        n_ready = sem("n_ready")
        nT_done = sem("nT_done")
        nT_ready = sem("nT_ready")
        y_done = sem("y_done")
        y_read = sem("y_read")
        y_ready = sem("y_ready")
        stored = [sem(f"stored{k}") for k in range(2)]

        with nc.Block() as block:
            @block.sync
            def _(sp):
                start_free(sp, nT_done, nT_ready, y_done, y_read, *stored)
                with sp.Fori(0, STEPS // 2) as m:
                    for hf in range(2):
                        s = 2 * m + hf
                        sp.wait_ge(y_ready, s + 1)
                        sp.dma_start(out[:, bass.ds(s * G, G), :], y[:, hf, :, :]).then_inc(stored[hf], 16)
                for hf in range(2):
                    sp.wait_ge(stored[hf], FREE + 16 * (STEPS // 2))

            @block.tensor
            def _(pe):
                def turn_x(s, hf):
                    pe.wait_ge(xs_ready, s + 1)
                    for t in range(G):
                        last = nc.tensor.transpose(ps[:, 0, t * P:(t + 1) * P], xs[:, hf, t, :], ident[:, :])
                    last.then_inc(xT_done, 1)

                def hidden(s, hf, ts):
                    pe.wait_ge(xT_ready, s + 1)
                    for t in ts:
                        pe.wait_ge(g_ready, 4 * s + max(t - 1, 0))
                        nc.tensor.matmul(ps[:, 1 + t % 2, :], xT[:, hf, t * P:(t + 1) * P], wf3[:, :],
                                         start=True, stop=True).then_inc(h_done, 1)

                def turn_g(s, hf):
                    pe.wait_ge(n_ready, s + 1)
                    pe.wait_ge(nT_ready, FREE + 4 * s)
                    for k in range(HB):
                        for t in range(G):
                            last = nc.tensor.transpose(ps[:, 3 + k, t * P:(t + 1) * P], g[:, hf, t, k * P:(k + 1) * P],
                                                       ident[:, :])
                        last.then_inc(nT_done, 1)

                def outputs(s):
                    pe.wait_ge(nT_ready, FREE + 4 * s + 4)
                    pe.wait_ge(y_read, FREE + s)
                    for t in range(G):
                        for k in range(HB):
                            last = nc.tensor.matmul(ps[:, 7, t * P:(t + 1) * P], nT[:, k, t * P:(t + 1) * P], wp3[:, k, :],
                                                    start=(k == 0), stop=(k == HB - 1))
                    last.then_inc(y_done, 1)

                for s in range(2):
                    turn_x(s, s)
                    hidden(s, s, range(G))
                with pe.Fori(0, STEPS // 2 - 1) as m:
                    for hf in range(2):
                        s = 2 * m + hf
                        turn_x(s + 2, hf)
                        turn_g(s, hf)
                        hidden(s + 2, hf, (0, 1))
                        outputs(s)
                        hidden(s + 2, hf, (2, 3))
                for hf in range(2):
                    turn_g(STEPS - 2 + hf, hf)
                    outputs(STEPS - 2 + hf)

            @block.scalar
            def _(act):
                def copy_x(s, hf):
                    act.wait_ge(xT_done, s + 1)
                    nc.scalar.copy(xT[:, hf, :], ps[:, 0, :]).then_inc(xT_ready, 1)

                def gelu(s, hf):
                    if not isinstance(s, int) or s >= 2:
                        act.wait_ge(nT_done, FREE + 4 * (s - 1))
                    for t in range(G):
                        act.wait_ge(h_done, 4 * s + t + 1)
                        nc.scalar.activation(g[:, hf, t, :], ps[:, 1 + t % 2, :], ACT.Gelu).then_inc(g_ready, 1)

                def copy_g(s):
                    act.wait_ge(y_done, FREE + s)
                    for k in range(HB):
                        act.wait_ge(nT_done, FREE + 4 * s + k + 1)
                        nc.scalar.activation(nT[:, k, :], ps[:, 3 + k, :], ACT.Identity, bias=ln_b[:, k:k + 1],
                                             scale=ln_w[:, k:k + 1]).then_inc(nT_ready, 1)

                for s in range(2):
                    copy_x(s, s)
                    gelu(s, s)
                with act.Fori(0, STEPS // 2 - 1) as m:
                    for hf in range(2):
                        s = 2 * m + hf
                        copy_x(s + 2, hf)
                        copy_g(s)
                        gelu(s + 2, hf)
                for hf in range(2):
                    copy_g(STEPS - 2 + hf)

            @block.vector
            def _(dve):
                link = Chain(dve, chain, signals.links)
                def x_now(s):
                    return x_all[:, bass.ds(s * G, G), :]

                def fetch(s, hf):
                    if not isinstance(s, int) or s >= 2:
                        dve.wait_ge(xT_done, s - 1)
                    nc.vector.tensor_copy(xs[:, hf, :, :], x_now(s)).then_inc(xs_ready, 1)

                def hidden_stats(s, hf, scratch, step):
                    dve.wait_ge(g_ready, 4 * s + 4)
                    for t in range(G):
                        last = nc.vector.bn_stats(scratch.st[:, t, :], g[:, hf, t, :])
                    step(last)

                def output_stats(m, hf, at, step):
                    s = 2 * m + hf
                    dve.wait_ge(y_done, FREE + s + 1)
                    dve.wait_ge(stored[hf], FREE + 16 * m)
                    nc.vector.tensor_tensor(y[:, hf, :, :], ps[:, 7, :].rearrange("p (t n) -> p t n", t=G), x_now(s), ALU.add)\
                        .then_inc(y_read, 1)
                    dve.wait_ge(y_read, FREE + s + 1)
                    for t in range(G):
                        last = nc.vector.bn_stats(ns.st[:, at + t, :], y[:, hf, t, :])
                    step(last)

                def apply(buffer, hf, scratch, at, done):
                    for t in range(G):
                        last = nc.vector.tensor_scalar(buffer[:, hf, t, :], buffer[:, hf, t, :], scratch.y[:, at + t:at + t + 1],
                                                       scratch.b[:, at + t:at + t + 1], ALU.mult, ALU.add)
                    last.then_inc(done, 1)

                def hidden_only(s, hf, step):
                    hidden_stats(s, hf, ns_first, step)
                    norm_scales(nc.vector, step, ns_first, EPS_LN, FH)
                    apply(g, hf, ns_first, 0, n_ready)

                def both(m, hf, step):
                    output_stats(m - 1, hf, G, step)
                    hidden_stats(2 * m + hf, hf, ns, step)
                    norm_scales(nc.vector, step, ns, EPS_LN, FH, DM)
                    apply(g, hf, ns, 0, n_ready)
                    apply(y, hf, ns, G, y_ready)

                fetch(0, 0)
                fetch(1, 1)
                hidden_only(0, 0, link)
                fetch(2, 0)
                hidden_only(1, 1, link)
                with dve.Fori(1, STEPS // 2 - 1) as m:
                    step = Chain(dve, chain, link.start + link.count, m - 1, MLP_LINKS)
                    for hf in range(2):
                        fetch(2 * m + hf + 1, 1 - hf)
                        both(m, hf, step)
                    step.end()
                link = Chain(dve, chain, link.start + link.count + (STEPS // 2 - 2) * MLP_LINKS)
                fetch(STEPS - 1, 1)
                both(STEPS // 2 - 1, 0, link)
                both(STEPS // 2 - 1, 1, link)
                for hf in range(2):
                    output_stats(STEPS // 2 - 1, hf, hf * G, link)
                norm_scales(nc.vector, link, ns, EPS_LN, DM)
                for hf in range(2):
                    apply(y, hf, ns, hf * G, y_ready)


MLP_LINKS = 2 * (2 + 3 + ROOT_LINKS + 1)

def build(nc, d, out):
    with ExitStack() as ctx:
        def sb(name, shape, dt=F32):
            return ctx.enter_context(nc.sbuf_tensor(name, shape, dt))

        x_all = sb("x_all", [P, TILES, DM])
        tri = sb("tri", [P, P])
        past = sb("past", [P, P])
        ones = sb("ones", [P, P])
        ident = sb("ident", [P, P])
        signals = Signals(nc, ctx)
        with nc.Block() as block:
            @block.vector
            def _(dve):
                nc.vector.memset(ones[:, :], 1.0).then_inc(signals.set_up, 1)
                dve.wait_ge(signals.set_up, 1)
        mamba(nc, signals, x_all, tri, past, ones, ident, d)
        arena = sb("arena", [P, 2 * NE * HID])
        moe_w = expert_weights(sb, d, arena)
        fl_w, tm_w = flow_weights(sb, d), mlp_weights(sb, d)
        fl_loaded, tm_loaded = signals.new("fl_loaded"), signals.new("tm_loaded")
        with ExitStack() as layer:
            v_all = layer.enter_context(nc.sbuf_tensor("v_all", [P, BATCH * SLOTS, TPB, 32], F32))
            o_all = layer.enter_context(nc.sbuf_tensor("o_all", [P, BATCH * SLOTS, TPB, 32], F32))
            q_dram = nc.dram_tensor("q_parts", (BATCH * SLOTS, SPLITS, 32, SEQ), BF16).ap()
            k_dram = nc.dram_tensor("k_parts", (BATCH * SLOTS, SPLITS, 32, SEQ), BF16).ap()
            latent_attention(nc, signals, x_all, ident, d, v_all, o_all, q_dram, k_dram, arena, moe_w)
            experts(nc, signals, x_all, ident, o_all, moe_w, ((fl_w, fl_loaded), (tm_w, tm_loaded)))
        ternary = Ternary(nc, signals, ctx, tm_w, tm_loaded)
        flow_attention(nc, signals, x_all, ones, ident, fl_w, fl_loaded, ternary)
        ternary_mlp(nc, signals, x_all, ident, ternary, out)


def layouts(inp):
    f = {}
    x = np.asarray(inp["L0_attn_hidden_states"]).reshape(TOK, DM)
    f["x"] = np.ascontiguousarray(x.reshape(TILES, P, DM).transpose(1, 0, 2))
    f["xT"] = np.ascontiguousarray(x.T)
    w_in = np.asarray(inp["L0_attn_W_in"])
    f["w_in"] = np.ascontiguousarray(w_in[:, :2 * DIN + 2 * NST])
    f["w_dt"] = np.zeros((DM, 32), np.float32)
    f["w_dt"][:, :NH] = w_in[:, 2 * DIN + 2 * NST:]
    f["conv_w"] = np.ascontiguousarray(np.asarray(inp["L0_attn_conv_w"]).reshape(NBLK, P, TAPS).transpose(1, 0, 2))
    f["conv_b"] = np.ascontiguousarray(np.asarray(inp["L0_attn_conv_b"]).reshape(NBLK, P).T)
    f["dcol"] = np.ascontiguousarray(np.repeat(np.asarray(inp["L0_attn_D"]), HD).reshape(ZB, P).T)
    f["rms_w"] = np.ascontiguousarray(np.asarray(inp["L0_attn_rms_w"]).reshape(ZB, P).T)
    f["w_out"] = np.ascontiguousarray(np.asarray(inp["L0_attn_W_out"]).reshape(ZB, P, DM).transpose(1, 0, 2))
    f["dt_bias"] = np.asarray(inp["L0_attn_dt_bias"])
    f["a_log"] = np.asarray(inp["L0_attn_A_log"])
    f["m_ln_g"] = np.asarray(inp["L0_attn_ln_g"])
    f["m_ln_b"] = np.asarray(inp["L0_attn_ln_b"])
    row, col = np.arange(P)[:, None], np.arange(P)[None, :]
    f["tri"] = (row <= col).astype(np.float32)
    f["past"] = (row > col).astype(np.float32)
    f["ident"] = np.eye(P, dtype=np.float32)
    f["norm1_w"] = np.asarray(inp["L0_ffn_norm1_w"])[:, None]
    swap = (np.arange(DM) // AD) * AD + (np.arange(DM) % AD + AD // 2) % AD
    wq = np.asarray(inp["L0_ffn_Wq"]).T
    f["wq"] = np.ascontiguousarray(np.stack([wq, wq[:, swap]], 1))
    f["wdkv"] = np.ascontiguousarray(np.asarray(inp["L0_ffn_Wdkv"]).T)
    wuk = np.asarray(inp["L0_ffn_Wuk"]).T
    f["wuk"] = np.ascontiguousarray(np.stack([wuk, wuk[:, swap]], 1))
    f["wuv"] = np.ascontiguousarray(np.asarray(inp["L0_ffn_Wuv"]).T)
    f["lat_g"] = np.asarray(inp["L0_ffn_ln_g"])[:, None]
    f["lat_b"] = np.asarray(inp["L0_ffn_ln_b"])[:, None]
    half = AD // 2
    inv_freq = (1.0 / 10000.0 ** (np.arange(half, dtype=np.float32) / half)).astype(np.float32)
    angle = (np.arange(SEQ, dtype=np.float32)[:, None] * inv_freq[None, :]).astype(np.float32)
    sign = np.where(np.arange(AD) < half, -1.0, 1.0)[:, None]
    f["cos"] = np.tile(np.cos(angle).T, (2 * AH, 1)).astype(np.float32)
    f["sin"] = np.tile(np.tile(np.sin(angle).T, (2, 1)) * sign, (AH, 1)).astype(np.float32)
    f["norm2_w"] = np.asarray(inp["L0_ffn_norm2_w"])[:, None]
    f["moe_wo"] = np.ascontiguousarray(np.asarray(inp["L0_ffn_Wo"]).T)
    f["gate_w"] = np.ascontiguousarray(np.asarray(inp["L0_ffn_gate_w"]).T)
    f["gate_b"] = np.asarray(inp["L0_ffn_gate_b"])
    f["moe_w1"] = np.ascontiguousarray(np.asarray(inp["L0_ffn_W1"]).transpose(2, 0, 1))
    f["moe_b1"] = np.ascontiguousarray(np.asarray(inp["L0_ffn_b1"]).reshape(NE, HID // P, P).transpose(2, 0, 1))
    f["moe_w2"] = np.ascontiguousarray(
        np.asarray(inp["L0_ffn_W2"]).transpose(0, 2, 1).reshape(NE, HID // P, P, DM).transpose(2, 0, 1, 3))
    b2 = np.zeros((G, NE, G, DM), np.float32)
    for t in range(G):
        b2[t, :, t, :] = np.asarray(inp["L0_ffn_b2"])
    f["moe_b2"] = b2.reshape(G * NE, G * DM)
    f["order"] = np.tile(np.arange(NE, 0, -1, dtype=np.float32), (P, 1))
    for n, key in (("fl_wq", "Wq"), ("fl_wk", "Wk"), ("fl_wv", "Wv"), ("fl_wo", "Wo")):
        f[n] = np.asarray(inp["L1_attn_" + key])
    f["fl_bq"] = np.asarray(inp["L1_attn_bq"])[:, None]
    f["fl_bk"] = np.asarray(inp["L1_attn_bk"])[:, None]
    f["fl_bv"] = np.asarray(inp["L1_attn_bv"])
    f["fl_bo"] = np.asarray(inp["L1_attn_bo"])
    f["head"] = (row // AD == np.arange(AH)[None, :]).astype(np.float32)
    f["same"] = (row // AD == col // AD).astype(np.float32)
    f["wf"] = np.ascontiguousarray(np.asarray(inp["L1_ffn_W_fc"]).T)
    f["wp"] = np.ascontiguousarray(np.asarray(inp["L1_ffn_W_proj"]).T.reshape(FH // P, P, DM).transpose(1, 0, 2))
    f["tm_ln_w"] = np.ascontiguousarray(np.asarray(inp["L1_ffn_ln_w"]).reshape(FH // P, P).T)
    f["tm_ln_b"] = np.ascontiguousarray(np.asarray(inp["L1_ffn_ln_b"]).reshape(FH // P, P).T)
    bf16 = mybir.dt.np(BF16)
    f["identb"] = np.eye(P).astype(bf16)
    f["mask_q"] = np.where(col > row, MASKED, 0.0).astype(bf16)
    f["mask_k"] = np.where(row > col, MASKED, 0.0).astype(bf16)
    f["pad"] = np.repeat((np.arange(STACK - SROWS) >= SHIFT_ROW - SROWS), 4 * SEQ).reshape(-1, 4, SEQ).astype(bf16)
    return f


def kernel(**inputs):
    import concourse.bacc as bacc
    from concourse.bass_utils import run_bass_kernel_spmd

    nc = bacc.Bacc("TRN2", target_bir_lowering=False, num_devices=1)
    arrays = layouts(inputs)
    d = {n: nc.dram_tensor("in_" + n, a.shape, mybir.dt.from_np(a.dtype), kind="ExternalInput").ap() for n, a in arrays.items()}
    out = nc.dram_tensor("out", (P, TILES, DM), F32, kind="ExternalOutput").ap()
    build(nc, d, out)
    res = run_bass_kernel_spmd(nc, [{"in_" + n: a for n, a in arrays.items()}], core_ids=[0]).results[0]["out"]
    return res.transpose(1, 0, 2).reshape(BATCH, SEQ, DM)
```
